# Optimizing a Trainium2 kernel written in Bass

```python
import numpy as np
import jax
import jax.numpy as jnp

def _softmax(x, axis=-1):
    return jax.nn.softmax(x, axis=axis)

def _gelu(x):
    return jax.nn.gelu(x, approximate=True)

def _silu(x):
    return jax.nn.silu(x)

def _sigmoid(x):
    return jax.nn.sigmoid(x)

def _layernorm(x, axis=-1, eps=1e-05):
    m = jnp.mean(x, axis=axis, keepdims=True)
    v = jnp.var(x, axis=axis, keepdims=True)
    return (x - m) / jnp.sqrt(v + eps)

def _scatter_add(tgt, idx, src, axis=0):
    return tgt.at[idx].add(src)

def _segment_sum(src, seg, n):
    return jax.ops.segment_sum(src, seg, n)
kernel_name = 'mk_decoder_postln_d1_seqx_r8_83a17e'

def setup_inputs(seed: int=0):
    np.random.seed(seed)
    _w = jnp.asarray

    def _rec_inputs():
        import jax
        import jax.numpy as jnp
        _rk = jax.random.key(seed)
        x = 7.22e-05 + 1 * jax.random.normal(jax.random.fold_in(_rk, 1), (16, 128, 128), jnp.float32)
        _lenS = 128 - jax.random.randint(jax.random.fold_in(_rk, 7), (16,), 0, max(1, 128 // 4) + 1, jnp.int32)
        _lenS2 = 128 - jax.random.randint(jax.random.fold_in(_rk, 8), (16,), 0, max(1, 128 // 4) + 1, jnp.int32)
        _ctx_1024P = jax.random.normal(jax.random.fold_in(_rk, 11), (16, 16, 128), jnp.float32)
        _ctx_1024c = jax.random.dirichlet(jax.random.fold_in(_rk, 511), 0.3 * jnp.ones((16,), jnp.float32), (16, 128))
        _ctx_1024t = jnp.einsum('bsk,bkd->bsd', _ctx_1024c, _ctx_1024P)
        _ctx_1024t = _ctx_1024t * jax.lax.rsqrt(jnp.mean(jnp.square(_ctx_1024t)) + 1e-12) * 0.953939
        ctx_1024 = 4.13588e-05 + 0.999923 * (_ctx_1024t + 0.3 * jax.random.normal(jax.random.fold_in(_rk, 611), (16, 128, 128), jnp.float32))
        return (x, ctx_1024)
    x, ctx_1024 = _rec_inputs()

    def _L0_attn_setup():
        import math
        import jax, jax.numpy as jnp
        import numpy as np
        CHUNK = 32
        PROB_FLOOR = 0.02
        EPS = 1e-05

        def l2norm(x):
            return x * jax.lax.rsqrt(jnp.sum(x * x, -1, keepdims=True) + 1e-06)

        def causal_dwconv(x, w):
            B, L, C = x.shape
            K = w.shape[-1]
            y = jax.lax.conv_general_dilated(jnp.transpose(x, (0, 2, 1)), w[:, None, :], (1,), [(K - 1, 0)], feature_group_count=C)
            return jnp.transpose(y, (0, 2, 1))

        def delta_rule_chunkwise(q, k, v, beta, chunk=CHUNK):
            b, h, L, dk = q.shape
            dv = v.shape[-1]
            pad = -L % chunk
            if pad:
                q = jnp.pad(q, ((0, 0), (0, 0), (0, pad), (0, 0)))
                k = jnp.pad(k, ((0, 0), (0, 0), (0, pad), (0, 0)))
                v = jnp.pad(v, ((0, 0), (0, 0), (0, pad), (0, 0)))
                beta = jnp.pad(beta, ((0, 0), (0, 0), (0, pad)))
            Lp = L + pad
            n = Lp // chunk
            q = l2norm(q)
            k = l2norm(k)
            v = v * beta[..., None]
            kb = k * beta[..., None]
            r = lambda t: t.reshape(b, h, n, chunk, t.shape[-1])
            q, k, v, kb = (r(q), r(k), r(v), r(kb))
            i_ = jnp.arange(chunk)
            strict_lower = (i_[:, None] > i_[None, :]).astype(q.dtype)
            lower_incl = (i_[:, None] >= i_[None, :]).astype(q.dtype)
            inv = -(kb @ jnp.swapaxes(k, -1, -2)) * strict_lower
            for i in range(1, chunk):
                inv = inv.at[..., i, :].add(jnp.einsum('...j,...jk->...k', inv[..., i, :], inv))
            inv = inv + jnp.eye(chunk, dtype=q.dtype)
            u = inv @ v
            w = inv @ kb
            mv = lambda t: jnp.moveaxis(t, 2, 0)

            def step(S, xs):
                qi, ki, ui, wi = xs
                attn = qi @ jnp.swapaxes(ki, -1, -2) * lower_incl
                ui2 = ui - wi @ S
                oi = qi @ S + attn @ ui2
                return (S + jnp.swapaxes(ki, -1, -2) @ ui2, oi)
            S0 = jnp.zeros((b, h, dk, dv), q.dtype)
            S, outs = jax.lax.scan(step, S0, (mv(q), mv(k), mv(u), mv(w)))
            out = jnp.moveaxis(outs, 0, 2).reshape(b, h, Lp, dv)[:, :, :L]
            return (out, S)

        def head_stats(x):
            mean = x.mean(-1)
            var = ((x - mean[..., None]) ** 2).mean(-1)
            am = jnp.abs(x).mean(-1)
            l2 = jnp.sqrt((x * x).sum(-1))
            return jnp.stack([mean, var, am, l2], -1).mean(2)

        def rmsnorm(x, w):
            return x * jax.lax.rsqrt((x * x).mean(-1, keepdims=True) + EPS) * w
        key = jax.random.key(seed)
        ks = jax.random.split(key, 20)
        B, L, D, H = (2, 512, 128, 4)
        dv = D // H
        f32 = jnp.float32
        rn = lambda k, shape, s: (jax.random.normal(k, shape) * s).astype(f32)
        fir = lambda k, shape: rn(k, shape, 0.02).at[..., -1].add(1.0)
        return {'hidden_states': jax.random.normal(ks[0], (B, L, D), f32), 'Wq': rn(ks[1], (D, D), 0.02), 'Wk': rn(ks[2], (D, D), 0.02), 'Wv': rn(ks[3], (D, D), 0.02), 'Wb': rn(ks[4], (D, H), 0.02), 'wq_conv': fir(ks[5], (D, 4)), 'wk_conv': fir(ks[6], (D, 4)), 'wv_conv': fir(ks[7], (D, 4)), 'fir_long': fir(ks[8], (H, dv, 64)), 'fir_short': fir(ks[9], (H, dv, 5)), 'Wg1': rn(ks[10], (D + 16, D), 0.02), 'bg1': jnp.zeros((D,), f32), 'Wg2': rn(ks[11], (D, 4), 0.02), 'bg2': jnp.array([-0.5, -0.5, 1.0, 3.0], f32), 'logit_temp': jnp.array([math.log(math.expm1(0.7))], f32), 'conv_res_logit': jnp.full((H,), -1.0, f32), 'Wres': rn(ks[12], (D, H), 0.02), 'bres': jnp.full((H,), -1.0, f32), 'Wog1': rn(ks[13], (D + 8, D // 2), 0.02), 'bog1': jnp.zeros((D // 2,), f32), 'Wog2': rn(ks[14], (D // 2, 1), 0.02), 'bog2': jnp.full((1,), -1.0986122886681098, f32), 'norm_w': jnp.ones((dv,), f32), 'Wo': rn(ks[15], (D, D), 0.02)}
    _L0_attn_all = _L0_attn_setup()
    _L0_attn_in = {k: v for k, v in _L0_attn_all.items() if k in ('Wq', 'Wk', 'Wv', 'Wb', 'wq_conv', 'wk_conv', 'wv_conv', 'fir_long', 'fir_short', 'Wg1', 'bg1', 'Wg2', 'bg2', 'logit_temp', 'conv_res_logit', 'Wres', 'bres', 'Wog1', 'bog1', 'Wog2', 'bog2', 'norm_w', 'Wo')}
    del _L0_attn_all

    def _L0_xattn_setup():
        import jax, jax.numpy as jnp
        import numpy as np
        EMBED_DIM = 128
        HEAD_DIM = 128
        GAMMA = 0.96875
        THETA = 10000.0
        SCALE_BASE = 512.0

        def _dup_interleave(x):
            return jnp.repeat(x, 2, axis=-1)

        def _rotate_half(x):
            x_even = x[..., ::2]
            x_odd = x[..., 1::2]
            return jnp.stack((-x_odd, x_even), axis=-1).reshape(x.shape)

        def _xpos(x, offset=0, inverse_scale=False):
            l = x.shape[-2]
            half = HEAD_DIM // 2
            scale_vec = (jnp.arange(0, HEAD_DIM, 2, dtype=jnp.float32) + 0.4 * HEAD_DIM) / (1.4 * HEAD_DIM)
            pos = jnp.arange(offset, offset + l, dtype=jnp.float32)
            scale = scale_vec[None, :] ** (pos / SCALE_BASE)[:, None]
            freqs = 1.0 / THETA ** (jnp.arange(half, dtype=jnp.float32) / half)
            sin_in = pos[:, None] * freqs[None, :]
            sin, cos = (jnp.sin(sin_in), jnp.cos(sin_in))
            if inverse_scale:
                scale = 1.0 / scale
            return x * _dup_interleave(cos * scale) + _rotate_half(x) * _dup_interleave(sin * scale)

        def _decay_mask(l, gamma):
            idx = jnp.arange(l, dtype=jnp.float32)
            diff = idx[:, None] - idx[None, :]
            return jnp.where(diff >= 0, gamma ** diff, 0.0)
        key = jax.random.key(seed)
        k1, k2, k3, k4, k5, k6 = jax.random.split(key, 6)
        B, L = (4, 256)
        s = 1.0 / np.sqrt(EMBED_DIM)
        return {'q': jax.random.normal(k1, (B, L, EMBED_DIM), dtype=jnp.float32), 'k': jax.random.normal(k2, (B, L, EMBED_DIM), dtype=jnp.float32), 'v': jax.random.normal(k3, (B, L, EMBED_DIM), dtype=jnp.float32), 'Wq': jax.random.normal(k4, (EMBED_DIM, HEAD_DIM), dtype=jnp.float32) * s, 'Wk': jax.random.normal(k5, (EMBED_DIM, HEAD_DIM), dtype=jnp.float32) * s, 'Wv': jax.random.normal(k6, (EMBED_DIM, HEAD_DIM), dtype=jnp.float32) * s}
    _L0_xattn_all = _L0_xattn_setup()
    _L0_xattn_in = {k: v for k, v in _L0_xattn_all.items() if k in ('Wq', 'Wk', 'Wv')}
    del _L0_xattn_all

    def _L0_ffn_setup():
        import jax, jax.numpy as jnp
        import numpy as np
        E = 8
        D = 128
        H = 256
        TOP_K = 2
        key = jax.random.key(seed)
        k_x, k_g, k_w1, k_w2 = jax.random.split(key, 4)
        B, S = (4, 256)
        inp = {'input': jax.random.normal(k_x, (B, S, D), dtype=jnp.float32), 'Wg': jax.random.normal(k_g, (D, E), dtype=jnp.float32) * 0.02, 'W1': jax.random.normal(k_w1, (E, D, H), dtype=jnp.float32) * 0.02, 'b1': jnp.zeros((E, H), dtype=jnp.float32), 'W2': jax.random.normal(k_w2, (E, H, D), dtype=jnp.float32) * 0.02, 'b2': jnp.zeros((E, D), dtype=jnp.float32)}
        return inp
    _L0_ffn_all = _L0_ffn_setup()
    _L0_ffn_in = {k: v for k, v in _L0_ffn_all.items() if k in ('Wg', 'W1', 'b1', 'W2', 'b2')}
    del _L0_ffn_all
    return {'x': x, 'ctx_1024': ctx_1024, 'L0_attn_Wq': _L0_attn_in['Wq'], 'L0_attn_Wk': _L0_attn_in['Wk'], 'L0_attn_Wv': _L0_attn_in['Wv'], 'L0_attn_Wb': _L0_attn_in['Wb'], 'L0_attn_wq_conv': _L0_attn_in['wq_conv'], 'L0_attn_wk_conv': _L0_attn_in['wk_conv'], 'L0_attn_wv_conv': _L0_attn_in['wv_conv'], 'L0_attn_fir_long': _L0_attn_in['fir_long'], 'L0_attn_fir_short': _L0_attn_in['fir_short'], 'L0_attn_Wg1': _L0_attn_in['Wg1'], 'L0_attn_bg1': _L0_attn_in['bg1'], 'L0_attn_Wg2': _L0_attn_in['Wg2'], 'L0_attn_bg2': _L0_attn_in['bg2'], 'L0_attn_logit_temp': _L0_attn_in['logit_temp'], 'L0_attn_conv_res_logit': _L0_attn_in['conv_res_logit'], 'L0_attn_Wres': _L0_attn_in['Wres'], 'L0_attn_bres': _L0_attn_in['bres'], 'L0_attn_Wog1': _L0_attn_in['Wog1'], 'L0_attn_bog1': _L0_attn_in['bog1'], 'L0_attn_Wog2': _L0_attn_in['Wog2'], 'L0_attn_bog2': _L0_attn_in['bog2'], 'L0_attn_norm_w': _L0_attn_in['norm_w'], 'L0_attn_Wo': _L0_attn_in['Wo'], 'L0_xattn_Wq': _L0_xattn_in['Wq'], 'L0_xattn_Wk': _L0_xattn_in['Wk'], 'L0_xattn_Wv': _L0_xattn_in['Wv'], 'L0_ffn_Wg': _L0_ffn_in['Wg'], 'L0_ffn_W1': _L0_ffn_in['W1'], 'L0_ffn_b1': _L0_ffn_in['b1'], 'L0_ffn_W2': _L0_ffn_in['W2'], 'L0_ffn_b2': _L0_ffn_in['b2']}

def reference(x, ctx_1024, L0_attn_Wq, L0_attn_Wk, L0_attn_Wv, L0_attn_Wb, L0_attn_wq_conv, L0_attn_wk_conv, L0_attn_wv_conv, L0_attn_fir_long, L0_attn_fir_short, L0_attn_Wg1, L0_attn_bg1, L0_attn_Wg2, L0_attn_bg2, L0_attn_logit_temp, L0_attn_conv_res_logit, L0_attn_Wres, L0_attn_bres, L0_attn_Wog1, L0_attn_bog1, L0_attn_Wog2, L0_attn_bog2, L0_attn_norm_w, L0_attn_Wo, L0_xattn_Wq, L0_xattn_Wk, L0_xattn_Wv, L0_ffn_Wg, L0_ffn_W1, L0_ffn_b1, L0_ffn_W2, L0_ffn_b2):
    import jax
    import jax.numpy as jnp

    def _L0_attn_ref(hidden_states, Wq, Wk, Wv, Wb, wq_conv, wk_conv, wv_conv, fir_long, fir_short, Wg1, bg1, Wg2, bg2, logit_temp, conv_res_logit, Wres, bres, Wog1, bog1, Wog2, bog2, norm_w, Wo):
        import math
        import jax, jax.numpy as jnp
        import numpy as np
        CHUNK = 32
        PROB_FLOOR = 0.02
        EPS = 1e-05

        def l2norm(x):
            return x * jax.lax.rsqrt(jnp.sum(x * x, -1, keepdims=True) + 1e-06)

        def causal_dwconv(x, w):
            B, L, C = x.shape
            K = w.shape[-1]
            y = jax.lax.conv_general_dilated(jnp.transpose(x, (0, 2, 1)), w[:, None, :], (1,), [(K - 1, 0)], feature_group_count=C)
            return jnp.transpose(y, (0, 2, 1))

        def delta_rule_chunkwise(q, k, v, beta, chunk=CHUNK):
            b, h, L, dk = q.shape
            dv = v.shape[-1]
            pad = -L % chunk
            if pad:
                q = jnp.pad(q, ((0, 0), (0, 0), (0, pad), (0, 0)))
                k = jnp.pad(k, ((0, 0), (0, 0), (0, pad), (0, 0)))
                v = jnp.pad(v, ((0, 0), (0, 0), (0, pad), (0, 0)))
                beta = jnp.pad(beta, ((0, 0), (0, 0), (0, pad)))
            Lp = L + pad
            n = Lp // chunk
            q = l2norm(q)
            k = l2norm(k)
            v = v * beta[..., None]
            kb = k * beta[..., None]
            r = lambda t: t.reshape(b, h, n, chunk, t.shape[-1])
            q, k, v, kb = (r(q), r(k), r(v), r(kb))
            i_ = jnp.arange(chunk)
            strict_lower = (i_[:, None] > i_[None, :]).astype(q.dtype)
            lower_incl = (i_[:, None] >= i_[None, :]).astype(q.dtype)
            inv = -(kb @ jnp.swapaxes(k, -1, -2)) * strict_lower
            for i in range(1, chunk):
                inv = inv.at[..., i, :].add(jnp.einsum('...j,...jk->...k', inv[..., i, :], inv))
            inv = inv + jnp.eye(chunk, dtype=q.dtype)
            u = inv @ v
            w = inv @ kb
            mv = lambda t: jnp.moveaxis(t, 2, 0)

            def step(S, xs):
                qi, ki, ui, wi = xs
                attn = qi @ jnp.swapaxes(ki, -1, -2) * lower_incl
                ui2 = ui - wi @ S
                oi = qi @ S + attn @ ui2
                return (S + jnp.swapaxes(ki, -1, -2) @ ui2, oi)
            S0 = jnp.zeros((b, h, dk, dv), q.dtype)
            S, outs = jax.lax.scan(step, S0, (mv(q), mv(k), mv(u), mv(w)))
            out = jnp.moveaxis(outs, 0, 2).reshape(b, h, Lp, dv)[:, :, :L]
            return (out, S)

        def head_stats(x):
            mean = x.mean(-1)
            var = ((x - mean[..., None]) ** 2).mean(-1)
            am = jnp.abs(x).mean(-1)
            l2 = jnp.sqrt((x * x).sum(-1))
            return jnp.stack([mean, var, am, l2], -1).mean(2)

        def rmsnorm(x, w):
            return x * jax.lax.rsqrt((x * x).mean(-1, keepdims=True) + EPS) * w
        B, L, D = hidden_states.shape
        H = Wb.shape[-1]
        silu = jax.nn.silu
        q_in = silu(causal_dwconv(hidden_states @ Wq, wq_conv))
        k_in = silu(causal_dwconv(hidden_states @ Wk, wk_conv))
        v_in = silu(causal_dwconv(hidden_states @ Wv, wv_conv))
        dk = q_in.shape[-1] // H
        dv = v_in.shape[-1] // H
        q = q_in.reshape(B, L, H, dk)
        k = k_in.reshape(B, L, H, dk)
        v_direct = v_in.reshape(B, L, H, dv)
        beta = jax.nn.sigmoid(hidden_states @ Wb)
        do, S = delta_rule_chunkwise(jnp.transpose(q, (0, 2, 1, 3)), jnp.transpose(k, (0, 2, 1, 3)), jnp.transpose(v_direct, (0, 2, 1, 3)), jnp.transpose(beta, (0, 2, 1)))
        delta_out = jnp.transpose(do, (0, 2, 1, 3))
        local_long = causal_dwconv(v_in, fir_long.reshape(-1, fir_long.shape[-1])).reshape(B, L, H, dv)
        local_short = causal_dwconv(v_in, fir_short.reshape(-1, fir_short.shape[-1])).reshape(B, L, H, dv)
        stats = jnp.concatenate([head_stats(t) for t in (local_short, local_long, delta_out, v_direct)], -1)
        gate_in = jnp.concatenate([hidden_states, stats], -1)
        logits = (jax.nn.gelu(gate_in @ Wg1 + bg1, approximate=False) @ Wg2 + bg2) / jax.nn.softplus(logit_temp)
        p = jax.nn.softmax(logits, -1)
        p = jnp.clip(p, PROB_FLOOR, None)
        p = p / p.sum(-1, keepdims=True)
        pw = p[:, :, None, :]
        o = pw[..., 0:1] * local_short + pw[..., 1:2] * local_long + pw[..., 2:3] * delta_out + pw[..., 3:4] * v_direct
        res_gate = jax.nn.sigmoid(hidden_states @ Wres + bres)
        static = jax.nn.sigmoid(conv_res_logit)
        o = o + (static[None, None, :] * res_gate)[..., None] * local_short
        og_stats = jnp.concatenate([head_stats(o), head_stats(v_direct)], -1)
        og_in = jnp.concatenate([hidden_states, og_stats], -1)
        og = jax.nn.sigmoid(jax.nn.gelu(og_in @ Wog1 + bog1, approximate=False) @ Wog2 + bog2)
        o = o * og[:, :, :, None]
        o = rmsnorm(o, norm_w)
        return o.reshape(B, L, -1) @ Wo

    def _L0_xattn_ref(q, k, v, Wq, Wk, Wv):
        import jax, jax.numpy as jnp
        import numpy as np
        EMBED_DIM = 128
        HEAD_DIM = 128
        GAMMA = 0.96875
        THETA = 10000.0
        SCALE_BASE = 512.0

        def _dup_interleave(x):
            return jnp.repeat(x, 2, axis=-1)

        def _rotate_half(x):
            x_even = x[..., ::2]
            x_odd = x[..., 1::2]
            return jnp.stack((-x_odd, x_even), axis=-1).reshape(x.shape)

        def _xpos(x, offset=0, inverse_scale=False):
            l = x.shape[-2]
            half = HEAD_DIM // 2
            scale_vec = (jnp.arange(0, HEAD_DIM, 2, dtype=jnp.float32) + 0.4 * HEAD_DIM) / (1.4 * HEAD_DIM)
            pos = jnp.arange(offset, offset + l, dtype=jnp.float32)
            scale = scale_vec[None, :] ** (pos / SCALE_BASE)[:, None]
            freqs = 1.0 / THETA ** (jnp.arange(half, dtype=jnp.float32) / half)
            sin_in = pos[:, None] * freqs[None, :]
            sin, cos = (jnp.sin(sin_in), jnp.cos(sin_in))
            if inverse_scale:
                scale = 1.0 / scale
            return x * _dup_interleave(cos * scale) + _rotate_half(x) * _dup_interleave(sin * scale)

        def _decay_mask(l, gamma):
            idx = jnp.arange(l, dtype=jnp.float32)
            diff = idx[:, None] - idx[None, :]
            return jnp.where(diff >= 0, gamma ** diff, 0.0)
        qh = _xpos(q @ Wq, offset=0, inverse_scale=False)
        kh = _xpos(k @ Wk, offset=0, inverse_scale=True)
        vh = v @ Wv
        L = qh.shape[-2]
        mask = _decay_mask(L, GAMMA)
        scores = jnp.einsum('bld,bmd->blm', qh, kh) * mask[None, :, :]
        return scores @ vh

    def _L0_ffn_ref(input, Wg, W1, b1, W2, b2):
        import jax, jax.numpy as jnp
        import numpy as np
        E = 8
        D = 128
        H = 256
        TOP_K = 2
        logits = jnp.einsum('bsd,de->bse', input, Wg)
        probs = jax.nn.softmax(logits, axis=-1)
        top_vals, top_idx = jax.lax.top_k(probs, TOP_K)
        top_vals = top_vals / jnp.sum(top_vals, axis=-1, keepdims=True)
        onehot = jax.nn.one_hot(top_idx, E, dtype=input.dtype)
        mask = jnp.sum(onehot, axis=2)
        scores = jnp.sum(onehot * top_vals[..., None], axis=2)
        xm = input[None] * jnp.moveaxis(mask, -1, 0)[..., None]
        h = jnp.einsum('ebsd,edh->ebsh', xm, W1) + b1[:, None, None, :]
        h = jax.nn.relu(h)
        y = jnp.einsum('ebsh,ehd->ebsd', h, W2) + b2[:, None, None, :]
        out = jnp.sum(y * jnp.moveaxis(scores, -1, 0)[..., None], axis=0)
        return out
    x = _layernorm(x + _L0_attn_ref(x, L0_attn_Wq, L0_attn_Wk, L0_attn_Wv, L0_attn_Wb, L0_attn_wq_conv, L0_attn_wk_conv, L0_attn_wv_conv, L0_attn_fir_long, L0_attn_fir_short, L0_attn_Wg1, L0_attn_bg1, L0_attn_Wg2, L0_attn_bg2, L0_attn_logit_temp, L0_attn_conv_res_logit, L0_attn_Wres, L0_attn_bres, L0_attn_Wog1, L0_attn_bog1, L0_attn_Wog2, L0_attn_bog2, L0_attn_norm_w, L0_attn_Wo), axis=-1)
    x = _layernorm(x + _L0_xattn_ref(x, ctx_1024, ctx_1024, L0_xattn_Wq, L0_xattn_Wk, L0_xattn_Wv), axis=-1)
    x = _layernorm(x + _L0_ffn_ref(x, L0_ffn_Wg, L0_ffn_W1, L0_ffn_b1, L0_ffn_W2, L0_ffn_b2), axis=-1)
    return x

_drawn_inputs = setup_inputs


def setup_inputs(seed=0):
    import zlib

    import numpy as np

    out = dict(_drawn_inputs(seed))
    spreads = {'L0_attn_bg1': (0.0, 2.0),
     'L0_attn_conv_res_logit': (-1.0, 0.6),
     'L0_attn_bres': (-1.0, 0.6),
     'L0_attn_bog1': (0.0, 2.0),
     'L0_attn_norm_w': (1.0, 0.2),
     'L0_ffn_b1': (0.0, 0.534),
     'L0_ffn_b2': (0.0, 0.1)}
    factors = {'L0_attn_Wq': 6.203,
     'L0_attn_Wk': 6.561,
     'L0_attn_Wb': 25.049,
     'L0_attn_wq_conv': 6.422,
     'L0_attn_wk_conv': 6.875,
     'L0_attn_fir_long': 8.0,
     'L0_attn_fir_short': 2.678,
     'L0_attn_Wg1': 8.0,
     'L0_attn_Wg2': 8.0,
     'L0_attn_Wres': 146.919,
     'L0_attn_Wog1': 31.328,
     'L0_attn_Wog2': 34.492}
    for name, (base, spread) in spreads.items():
        noise = np.random.default_rng([zlib.crc32(name.encode()), seed]).standard_normal(out[name].shape)
        drawn = base * np.exp(spread * noise) if base else spread * noise
        out[name] = jnp.asarray(drawn.astype(out[name].dtype))
    for name, factor in factors.items():
        out[name] = (out[name] * factor).astype(out[name].dtype)
    return out
```

```python
from contextlib import ExitStack

import concourse.bass as bass
from concourse import mybir

F32 = mybir.dt.float32
I32 = mybir.dt.int32
ALU = mybir.AluOpType
ACT = mybir.ActivationFunctionType
AX = mybir.AxisListType

B, L, D = 16, 128, 128
H, DH = 4, 32
G = 4
NG = B // G
N = G * L
NP = B * H
GP = G * H
CH = 32
NC = L // CH
E, HID = 8, 256
NQKV = 3 * D
TAPS = 4
LONG, SHORT = 64, 5
EPS = 1e-5
FLOOR = 0.02
RSQRT_GUESS = float(0x5F3759DF)

WB = {}
_at = 0
for _name, _n in (("qkv", NQKV), ("gates", 2 * H), ("g1", D), ("og1", D // 2), ("g2", 4), ("o", D),
                  ("xq", D), ("xqr", D), ("xk", D), ("xkr", D), ("xv", D), ("route", E)):
    WB[_name] = (_at, _at + _n)
    _at += _n
WB_N = _at
RB = {}
_at = 0
for _name, _n in (("gate_bias", 2 * H), ("bg2", 4), ("temp", 1), ("static", H), ("bog2", 1)):
    RB[_name] = (_at, _at + _n)
    _at += _n
RB_N = _at
CB = {}
_at = 0
for _name, _n in (("bg1", 1), ("bog1", 1), ("norm", 1), ("short", SHORT), ("b1", 2 * E)):
    CB[_name] = (_at, _at + _n)
    _at += _n
CB_N = _at


def decoder_kernel(nc, x, ctx_in, wbundle, rbundle, cbundle, ws, wog2, taps_long, w1, w2, b2, tables, decay,
                   blocks_dram, inverse_dram, out):
    stack = ExitStack()
    with stack:
        def sb(name, shape, dt=F32):
            return stack.enter_context(nc.sbuf_tensor(name, shape, dt))

        def sem(name):
            return stack.enter_context(nc.semaphore(name))

        wb = sb("wb", [128, WB_N])
        rb = sb("rb", [128, RB_N])
        cb = sb("cb", [128, CB_N])
        ws_sb = sb("ws_sb", [32, D + D // 2])
        wog2_sb = sb("wog2_sb", [D // 2, 1])
        w1_sb = sb("w1_sb", [128, E, HID])
        w2_sb = sb("w2_sb", [128, E, 2, D])
        b2_sb = sb("b2_sb", [E, D])
        tab = sb("tab", [128, 4, L])
        decay_sb = sb("decay_sb", [128, L])
        ident = sb("ident", [128, 128])
        flip = sb("flip", [128, 128])
        masks = sb("masks", [128, 2, L])
        tie = sb("tie", [128, 2, E, E])
        stat_scale = sb("stat_scale", [128, 16])
        wtap = sb("wtap", [128, TAPS, NQKV])
        diag_short = sb("diag_short", [128, SHORT, 128])
        wo_n = sb("wo_n", [128, D])
        temp = sb("temp", [128, 8])
        bg2_t = sb("bg2_t", [128, G, 4])
        static_g = sb("static_g", [128, H])
        half_bog2 = sb("half_bog2", [128, 1])

        def w_of(name):
            a, b = WB[name]
            return wb[:, a:b]

        def r_of(name):
            a, b = RB[name]
            return rb[:, a:b]

        def c_of(name, i=0):
            a, _ = CB[name]
            return cb[:, a + i:a + i + 1]

        src = sb("src", [128, B, 4, D])
        vb = sb("vb", [128, NP, DH])
        as_t = sb("as_t", [128, NP, 2, L])
        early = sb("early", [128, 3 * NP * CH])
        inv_t = early[:, 0:NP * CH].rearrange("p (r i) -> p r i", r=NP)
        u = early[:, NP * CH:2 * NP * CH].rearrange("p (r i) -> p r i", r=NP)
        blk = early[:, 2 * NP * CH:3 * NP * CH].rearrange("p (a j i) -> p a j i", a=2, j=CH)
        rq = sb("rq", [128, B, H])
        gates = sb("gates", [128, B, 2 * H])
        inv = sb("inv", [128, 2, CH, CH])
        prod = sb("prod", [128, 2 * 272])
        toep = sb("toep", [128, 2, 16, L])

        qkv_g = early[:, 0:G * NQKV].rearrange("p (b c) -> p b c", b=G)
        kh_g = early[:, G * NQKV:G * NQKV + N].rearrange("p (b c) -> p b c", b=G)
        kh_c = early[:, 4 * N:8 * N].rearrange("p (h b t) -> p h b t", h=H, b=G)
        x_g = early[:, 8 * N:9 * N].rearrange("p (b c) -> p b c", b=G)
        kb_g = early[:, 9 * N:10 * N].rearrange("p (b c) -> p b c", b=G)
        kq_c = early[:, 10 * N:12 * N].rearrange("p (b k t) -> p b k t", b=G, k=2)
        xc_pad = sb("xc_pad", [128, G, TAPS - 1 + L])
        graw = sb("graw", [128, G, 2 * H])
        gtmp = sb("gtmp", [128, G, 2 * H])
        sq_g = sb("sq_g", [128, G * 4, D])
        ss_g = sb("ss_g", [128, G, 2 * H])
        rn_g = sb("rn_g", [128, G, 2 * H])
        nt1 = sb("nt1", [128, 64])
        nt2 = sb("nt2", [128, 64])

        old = [[as_t[:, :, :, :].rearrange("p a b c -> p (a b c)"), 0, NP * 2 * L],
               [early[:, :], 0, 3 * NP * CH]]

        def over(n, parts=128):
            for region in old:
                memory, a, size = region
                if a + n <= size:
                    region[1] += n
                    return memory[0:parts, a:a + n]
            raise AssertionError("no room")

        def over3(b, c, parts=128):
            return over(b * c, parts).rearrange("p (b c) -> p b c", b=b)

        xa = over3(G, D)
        xa_c = over3(G, L)
        v_g = over3(G, D)
        vc_pad = over3(G, SHORT - 1 + L)
        st = over3(G, 32)
        st2 = over3(G, 32)
        st_c = over(N, 32)
        st2_c = over(N, 32)
        h1 = over(N)
        h2 = over(N, 64)
        sumx = over(64)
        sumq = over(64)
        sm1 = over(64)
        sm2 = over(64)
        lg = over3(G, 4)
        pe4 = over3(G, 4)
        pw = over3(G, 4)
        red = over(G)
        w0 = over3(G, H)
        og = over(G)
        ogr = over3(G, H)
        o_g = over3(G, D)
        on_g = over3(G, D)
        on_c = over3(G, L)
        y_g = over3(G, D)
        bn6 = over3(G, 6)
        mv = over3(G, 2)
        x1 = over3(G, D)
        x1_c = over3(G, L)
        c_g = over3(G, D)
        c_c = over3(G, L)
        vh = over3(G, D)
        qr = over3(G, L)
        qt = over3(G, L)
        kr = over3(G, L)
        kt = over3(G, L)
        sc_t = over3(G, L)
        x2 = over3(G, D)
        x2_c = over3(G, L)
        ex = over3(G, E)
        cmp_ = over(G * E * 2 * E).rearrange("p (b i k j) -> p b i k j", b=G, i=E, k=2)
        rank = over3(G, E)
        score = over3(G, E)
        sct = over(N, E)
        hid = over(2 * 2 * N).rearrange("p (s k n) -> p s k n", s=2, k=2)
        acc = over3(G, D)
        fin = over3(G, D)

        ps = [stack.enter_context(nc.psum_tensor(f"bank{i}", [128, 512], F32)) for i in range(8)]

        def bank(i, b=G):
            return ps[i][:, :].rearrange("p (b c) -> p b c", b=b)

        w_in = sem("w_in")
        w_late = sem("w_late")
        x_in = sem("x_in")
        toep_in = [sem("toep_in0"), sem("toep_in1")]
        blocks_out = sem("blocks_out")
        blocks_in = sem("blocks_in")
        inverse_out = sem("inverse_out")
        inverse_in = sem("inverse_in")
        xa_in = sem("xa_in")
        ctx_loaded = sem("ctx_loaded")
        stored = sem("stored")
        dve_step = sem("dve_step")
        pool_step = sem("pool_step")
        act_step = sem("act_step")

        names = ("ident_ready pool_const act_const dve_const "
                 "vrev_ps vrev_kept xt_ps xc_ready proj_ready proj_free silu_ready zsum_ready tanh_ready sq_ready k_ready kb_ready "
                 "vb_ready v_kept q_ps q_c kh_ps kh_cready kb_ps kb_c gram_ps gram_kept "
                 "solved fir_ps fir_kept a_ps r_ready d_ps u_ready o_ps delta_ready "
                 "xat_ps xac_ready vg_ready vt_ps vc_ready short_ps short_ready ssq_ready stats_ready st_ps "
                 "stc_ready h1_ps h1_ready logit_ps lmax_ready exp_ready o_ready osq_ready ostats_ready st2_ps "
                 "st2c_ready h2_ps h2_ready z_ps og_tanh on_ready ont_ps onc_ready wo_ps x1_ready "
                 "ct_ps cc_ready vh_ps vh_ready k_rot_ps kr_ready x1t_ps x1c_ready qx_ps qr_ready sc_ps sct_ready "
                 "att_ps x2_ready "
                 "x2t_ps x2c_ready route_ps rmax_ready rexp_ready score_ready scoret_ps scoret_ready "
                 "binit_ps hid_ps hid_ready y_ps y_added fin_ready").split()
        s = {n: sem(n) for n in names}

        CREDITS = {
            "pe": {"proj_ready": 1, "q_ps": 1, "kh_ps": 1, "kb_ps": 1, "gram_ps": 1, "vt_ps": 1, "short_ps": 1,
                   "z_ps": 1, "st_ps": 1, "st2_ps": 1, "y_ps": 2},
            "act": {"kb_c": 1, "proj_free": 2, "onc_ready": 1, "hid_ready": 2},
            "dve": {"vb_ready": 1, "gram_kept": H, "x1_ready": 1, "x2_ready": 1, "ostats_ready": 1, "y_added": 2},
            "pool": {"v_kept": 1},
        }
        credit = {n: k for of in CREDITS.values() for n, k in of.items()}

        def give_credits(eng, who):
            for n, k in CREDITS[who].items():
                eng.sem_inc(s[n], k)

        def after(eng, name, count):
            eng.wait_ge(s[name], count + credit.get(name, 0))

        settled = {who: sem("settled_" + who) for who in ("act", "dve")}

        def settle(eng, who):
            eng.sem_inc(settled[who], 1)

        block = stack.enter_context(nc.Block())

        EARLY_LOADS, LATE_LOADS = 4, 8

        @block.sync
        def _(sp):
            sp.sem_inc(stored, 16)
            def every_partition(source, a, n):
                return bass.AP(tensor=source.tensor, offset=a, ap=[[0, 128], [1, n]])

            sp.dma_start(x_g[:, :, :], x[0:G].rearrange("b t c -> t b c")).then_inc(x_in, 16)
            for dst, source in ((wb[:, :], wbundle),
                                (rb[:, :], every_partition(rbundle, 0, RB_N)),
                                (wtap[:, :, :].rearrange("p t n -> p (t n)"),
                                 every_partition(rbundle, RB_N, TAPS * NQKV)),
                                (cb[:, :], cbundle)):
                sp.dma_start(dst, source).then_inc(w_in, 16)
            for dst, source in ((ws_sb[:, :], ws), (wog2_sb[:, :], wog2),
                                (tab[:, :, :], tables), (decay_sb[:, :], decay), (b2_sb[:, :], b2),
                                (w1_sb[:, :, :], w1.rearrange("e d h -> d e h")),
                                (w2_sb[:, :, 0, :], w2[:, 0:128, :].rearrange("e h d -> h e d")),
                                (w2_sb[:, :, 1, :], w2[:, 128:256, :].rearrange("e h d -> h e d"))):
                sp.dma_start(dst, source).then_inc(w_late, 16)
            with sp.Fori(1, NG) as g:
                after(sp, "xt_ps", g)
                sp.dma_start(x_g[:, :, :], x[bass.ds(g * G, G)].rearrange("b t c -> t b c")).then_inc(x_in, 16)
            for g in range(NG):
                after(sp, "gram_kept", 2 * H * (g + 1))
                for n in range(NC):
                    rows = slice(CH * n, CH * n + CH)
                    sp.dma_start(blocks_dram[GP * g:GP * g + GP, n].rearrange("r j i -> j r i"),
                                 as_t[rows, GP * g:GP * g + GP, 0, rows]).then_inc(blocks_out, 16)
            sp.wait_ge(blocks_out, 16 * NG * NC)
            after(sp, "v_kept", NG)
            after(sp, "vb_ready", NG)
            sp.dma_start(blk[:, :, :, :].rearrange("p a j i -> p (a j i)"),
                         blocks_dram.rearrange("r n j i -> (r n j i)").rearrange("(p m) -> p m", p=128)
                         ).then_inc(blocks_in, 16)
            after(sp, "solved", 1)
            sp.dma_start(inverse_dram.rearrange("r n j i -> (r n j i)").rearrange("(p m) -> p m", p=128),
                         inv[:, :, :, :].rearrange("p a j i -> p (a j i)")).then_inc(inverse_out, 16)
            sp.wait_ge(inverse_out, 16)
            for n in range(NC):
                rows = slice(CH * n, CH * n + CH)
                sp.dma_start(inv_t[rows, :, :], inverse_dram[:, n].rearrange("r j i -> j r i")).then_inc(inverse_in, 16)
            after(sp, "delta_ready", NG)
            sp.dma_start(xa, x[0:G].rearrange("b t c -> t b c")).then_inc(xa_in, 16)
            sp.dma_start(c_g, ctx_in[0:G].rearrange("b t c -> t b c")).then_inc(ctx_loaded, 16)
            with sp.Fori(1, NG) as g:
                after(sp, "ct_ps", g)
                sp.dma_start(c_g, ctx_in[bass.ds(g * G, G)].rearrange("b t c -> t b c")).then_inc(ctx_loaded, 16)
                after(sp, "x1_ready", g)
                sp.dma_start(xa, x[bass.ds(g * G, G)].rearrange("b t c -> t b c")).then_inc(xa_in, 16)
                after(sp, "fin_ready", g)
                sp.dma_start(out[bass.ds(g * G - G, G)].rearrange("b t c -> t b c"), fin).then_inc(stored, 16)
            after(sp, "fin_ready", NG)
            sp.dma_start(out[B - G:B].rearrange("b t c -> t b c"), fin).then_inc(stored, 16)
            sp.wait_ge(stored, 16 * (NG + 1))

        @block.gpsimd
        def _(pool):
            give_credits(pool, "pool")
            pool.memset(ident[:, :], 0.0).then_inc(pool_step, 1)
            pool.memset(masks[:, :, :], 1.0).then_inc(pool_step, 1)
            pool.memset(tie[:, :, :, :], 1.0).then_inc(pool_step, 1)
            pool.memset(xc_pad[:, :, :], 0.0).then_inc(pool_step, 1)
            pool.memset(kh_c[:, :, :, :], 0.0).then_inc(pool_step, 1)
            pool.memset(inv[:, :, :, :], 0.0).then_inc(pool_step, 1)
            for k, scale in enumerate((1 / D, 1 / (H * DH * DH), 1 / D, 1 / H)):
                pool.memset(stat_scale[:, :].rearrange("p (a k) -> p a k", k=4)[:, :, k], scale).then_inc(pool_step, 1)
            pool.memset(flip[:, :], 0.0).then_inc(pool_step, 1)
            pool.wait_ge(pool_step, 11)
            pool.affine_select(out=flip[:, :], in_=flip[:, :], compare_op=ALU.not_equal, fill=1.0, base=1 - L,
                               pattern=[[1, 128]], channel_multiplier=1).then_inc(pool_step, 1)
            pool.affine_select(out=ident[:, :], in_=ident[:, :], compare_op=ALU.not_equal, fill=1.0, base=0,
                               pattern=[[-1, 128]], channel_multiplier=1).then_inc(s["ident_ready"], 1)
            pool.affine_select(out=masks[:, 0, :], in_=masks[:, 0, :], compare_op=ALU.is_gt, fill=0.0, base=0,
                               pattern=[[1, L]], channel_multiplier=-1).then_inc(s["pool_const"], 1)
            pool.affine_select(out=masks[:, 1, :], in_=masks[:, 1, :], compare_op=ALU.is_ge, fill=0.0, base=0,
                               pattern=[[1, L]], channel_multiplier=-1).then_inc(s["pool_const"], 1)
            pool.affine_select(out=tie[:, 0, :, :], in_=tie[:, 0, :, :], compare_op=ALU.is_gt, fill=0.0, base=0,
                               pattern=[[1, E], [-1, E]], channel_multiplier=0).then_inc(s["pool_const"], 1)
            pool.affine_select(out=tie[:, 1, :, :], in_=tie[:, 1, :, :], compare_op=ALU.is_gt, fill=0.0, base=0,
                               pattern=[[-1, E], [1, E]], channel_multiplier=0).then_inc(s["pool_const"], 1)
            pool.affine_select(out=inv[:, :, :, :], in_=inv[:, :, :, :], compare_op=ALU.not_equal, fill=1.0, base=0,
                               pattern=[[0, 2], [1, CH], [-1, CH]], channel_multiplier=0).then_inc(s["pool_const"], 1)
            with pool.Fori(0, NG) as g:
                after(pool, "silu_ready", (g + 1) * G)
                pool.tensor_copy(src[:, bass.ds(g * G, G), 3, :], qkv_g[:, :, 2 * D:3 * D]).then_inc(s["v_kept"], 1)
            after(pool, "delta_ready", NG)
            pool.memset(vc_pad, 0.0).then_inc(pool_step, 1)
            pool.memset(st, 0.0).then_inc(pool_step, 1)
            pool.memset(st2, 0.0).then_inc(pool_step, 1)
            with pool.Fori(0, NG) as g:
                after(pool, "vt_ps", g)
                pool.tensor_copy(v_g, src[:, bass.ds(g * G, G), 3, :]).then_inc(s["vg_ready"], 1)

        @block.tensor
        def _(pe):
            give_credits(pe, "pe")
            def transposes(dst, source, rows=128):
                for b in range(G):
                    last = pe.transpose(ps[dst][0:rows, b * L:(b + 1) * L], source[:, b, :], ident[:, :])
                return last

            after(pe, "ident_ready", 1)
            pe.wait_ge(pool_step, 12)
            with pe.Fori(0, NG) as g:
                pe.wait_ge(x_in, 16 * (g + 1))
                after(pe, "kb_c", g)
                transposes(0, x_g).then_inc(s["xt_ps"], 1)
                after(pe, "xc_ready", g + 1)
                after(pe, "dve_const", 1)
                pe.wait_ge(w_in, 16 * EARLY_LOADS)
                for b in range(G):
                    after(pe, "proj_free", g * G + b - 1)
                    pr = ps[1 + b % 2]
                    for t in range(TAPS):
                        pe.matmul(pr[:, 0:NQKV], xc_pad[:, b, t:t + L], wtap[:, t, :],
                                  start=(t == 0), stop=(t == TAPS - 1))
                    pe.matmul(pr[:, NQKV:NQKV + 2 * H], xc_pad[:, b, TAPS - 1:TAPS - 1 + L], w_of("gates"),
                              start=True, stop=True).then_inc(s["proj_ready"], 1)
                after(pe, "silu_ready", (g + 1) * G)
                transposes(0, qkv_g[:, :, 0:D]).then_inc(s["q_ps"], 1)
                pe.matmul(bank(3), flip[:, :], qkv_g[:, :, 2 * D:3 * D], start=True, stop=True
                          ).then_inc(s["vrev_ps"], 1)
                after(pe, "k_ready", g + 1)
                after(pe, "vrev_kept", g + 1)
                transposes(3, kh_g).then_inc(s["kh_ps"], 1)
                after(pe, "kb_ready", g + 1)
                after(pe, "q_c", g + 1)
                transposes(0, kb_g).then_inc(s["kb_ps"], 1)
                after(pe, "kb_c", g + 1)
                after(pe, "kh_cready", g + 1)
                for r in range(2):
                    for h in range(H):
                        after(pe, "gram_kept", g * 2 * H + r * H + h + 1 - H)
                        for b in (2 * r, 2 * r + 1):
                            last = pe.matmul(ps[4 + h][:, (b % 2) * 2 * L:(b % 2 + 1) * 2 * L], kh_c[:, h, b, :],
                                             kq_c[:, b, :, :].rearrange("p k t -> p (k t)"), start=True, stop=True)
                        last.then_inc(s["gram_ps"], 1)
            after(pe, "v_kept", NG)
            after(pe, "kb_c", NG)
            after(pe, "proj_free", B)
            after(pe, "kh_cready", NG)
            for k in range(D // 16):
                pe.wait_ge(toep_in[k % 2], 16 * (k // 2 + 1))
                for c in range(16):
                    last = pe.matmul(ps[k // 2][:, (k % 2 * 16 + c) * B:(k % 2 * 16 + c + 1) * B],
                                     toep[:, k % 2, c, :], src[:, :, 2, k * 16 + c], start=True, stop=True)
                last.then_inc(s["fir_ps"], 1)
            pe.wait_ge(inverse_in, 16 * NC)
            after(pe, "gram_kept", 2 * H * NG)
            for n in range(NC):
                rows = slice(CH * n, CH * n + CH)
                for g in range(NG):
                    at = n * NG + g
                    if n:
                        after(pe, "u_ready", (n - 1) * NG + g + 1)
                        m = (n - 1) * NG + g
                        if m >= 2:
                            after(pe, "r_ready", m - 1)
                        for r in range(GP):
                            last = pe.matmul(ps[4 + m % 2][rows, r * DH:(r + 1) * DH],
                                             as_t[0:CH * n, GP * g + r, 0, rows], u[0:CH * n, GP * g + r, :],
                                             start=True, stop=True)
                        last.then_inc(s["a_ps"], 1)
                        after(pe, "r_ready", m + 1)
                    if at >= 2:
                        after(pe, "u_ready", at - 1)
                    for r in range(GP):
                        last = pe.matmul(ps[6 + at % 2][rows, r * DH:(r + 1) * DH], inv_t[rows, GP * g + r, :],
                                         vb[rows, GP * g + r, :], start=True, stop=True)
                    last.then_inc(s["d_ps"], 1)
            for g in range(NG):
                after(pe, "u_ready", (NC - 1) * NG + g + 1)
                if g < 2:
                    after(pe, "r_ready", (NC - 1) * NG)
                else:
                    after(pe, "delta_ready", g - 1)
                for r in range(GP):
                    last = pe.matmul(ps[4 + g % 2][:, r * DH:(r + 1) * DH], as_t[:, GP * g + r, 1, :],
                                     u[:, GP * g + r, :], start=True, stop=True)
                last.then_inc(s["o_ps"], 1)
            after(pe, "fir_kept", 4)
            after(pe, "delta_ready", NG)
            pe.wait_ge(w_late, 16 * LATE_LOADS)

            with pe.Fori(0, NG) as g:
                v = g + 1
                pe.wait_ge(xa_in, 16 * v)
                after(pe, "onc_ready", g)
                transposes(0, xa).then_inc(s["xat_ps"], 1)
                after(pe, "vg_ready", v)
                after(pe, "x1_ready", g)
                transposes(1, v_g).then_inc(s["vt_ps"], 1)
                after(pe, "vc_ready", v)
                for b in range(G):
                    for t in range(SHORT):
                        last = pe.matmul(bank(1)[:, b, :], vc_pad[:, b, t:t + L], diag_short[:, t, :],
                                         start=(t == 0), stop=(t == SHORT - 1))
                last.then_inc(s["short_ps"], 1)
                after(pe, "stats_ready", v)
                after(pe, "xac_ready", v)
                transposes(0, st, 32).then_inc(s["st_ps"], 1)
                after(pe, "short_ready", v)
                pe.matmul(ps[1][:, :], w_of("g1"), xa_c.rearrange("p b t -> p (b t)"), start=True, stop=False)
                after(pe, "stc_ready", v)
                pe.matmul(ps[1][:, :], ws_sb[:, 0:D], st_c, start=False, stop=True).then_inc(s["h1_ps"], 1)
                after(pe, "h1_ready", v)
                for b in range(G):
                    last = pe.matmul(ps[0][:, b * 4:b * 4 + 4], h1[:, b * L:(b + 1) * L], w_of("g2"),
                                     start=True, stop=True)
                last.then_inc(s["logit_ps"], 1)
                pe.matmul(ps[1][0:64, :], w_of("og1"), xa_c.rearrange("p b t -> p (b t)"), start=True, stop=False)
                after(pe, "ostats_ready", v)
                transposes(0, st2, 32).then_inc(s["st2_ps"], 1)
                after(pe, "st2c_ready", v)
                pe.matmul(ps[1][0:64, :], ws_sb[:, D:D + 64], st2_c, start=False, stop=True).then_inc(s["h2_ps"], 1)
                after(pe, "h2_ready", v)
                for b in range(G):
                    last = pe.matmul(ps[0][:, b:b + 1], h2[:, b * L:(b + 1) * L], wog2_sb[:, :], start=True, stop=True)
                last.then_inc(s["z_ps"], 1)
                after(pe, "on_ready", v)
                transposes(0, on_g).then_inc(s["ont_ps"], 1)
                after(pe, "onc_ready", v)
                for b in range(G):
                    last = pe.matmul(bank(1)[:, b, :], on_c[:, b, :], wo_n[:, :], start=True, stop=True)
                last.then_inc(s["wo_ps"], 1)
                pe.wait_ge(ctx_loaded, 16 * v)
                after(pe, "x2_ready", g)
                transposes(2, c_g).then_inc(s["ct_ps"], 1)
                after(pe, "cc_ready", v)
                for b in range(G):
                    last = pe.matmul(bank(2)[:, b, :], c_c[:, b, :], w_of("xv"), start=True, stop=True)
                last.then_inc(s["vh_ps"], 1)
                after(pe, "vh_ready", v)
                pe.matmul(ps[2][:, :], w_of("xk"), c_c.rearrange("p b t -> p (b t)"), start=True, stop=True)
                pe.matmul(ps[3][:, :], w_of("xkr"), c_c.rearrange("p b t -> p (b t)"),
                          start=True, stop=True).then_inc(s["k_rot_ps"], 1)
                after(pe, "x1_ready", v)
                after(pe, "kr_ready", v)
                transposes(2, x1).then_inc(s["x1t_ps"], 1)
                after(pe, "x1c_ready", v)
                pe.matmul(ps[2][:, :], w_of("xq"), x1_c.rearrange("p b t -> p (b t)"), start=True, stop=True)
                pe.matmul(ps[3][:, :], w_of("xqr"), x1_c.rearrange("p b t -> p (b t)"),
                          start=True, stop=True).then_inc(s["qx_ps"], 1)
                after(pe, "qr_ready", v)
                for b in range(G):
                    last = pe.matmul(bank(3)[:, b, :], kr[:, b, :], qr[:, b, :], start=True, stop=True)
                last.then_inc(s["sc_ps"], 1)
                after(pe, "sct_ready", v)
                for b in range(G):
                    last = pe.matmul(bank(2)[:, b, :], sc_t[:, b, :], vh[:, b, :], start=True, stop=True)
                last.then_inc(s["att_ps"], 1)
                after(pe, "x2_ready", v)
                transposes(3, x2).then_inc(s["x2t_ps"], 1)
                after(pe, "x2c_ready", v)
                for b in range(G):
                    last = pe.matmul(ps[3][:, b * E:(b + 1) * E], x2_c[:, b, :], w_of("route"), start=True, stop=True)
                last.then_inc(s["route_ps"], 1)
                for k in range(E + 1):
                    if k < E:
                        for half in range(2):
                            after(pe, "hid_ready", g * 2 * E + 2 * k + half - 1)
                            pe.matmul(ps[4 + half][:, :], w1_sb[:, k, half * 128:half * 128 + 128],
                                      x2_c.rearrange("p b t -> p (b t)"), start=True, stop=True
                                      ).then_inc(s["hid_ps"], 1)
                    if k == 0:
                        after(pe, "score_ready", v)
                        for b in range(G):
                            last = pe.transpose(ps[3][0:E, b * L:(b + 1) * L], score[:, b, :], ident[:, :])
                        last.then_inc(s["scoret_ps"], 1)
                        after(pe, "scoret_ready", v)
                        for b in range(G):
                            last = pe.matmul(bank(3)[:, b, :], sct[:, b * L:(b + 1) * L], b2_sb[:, :],
                                             start=True, stop=True)
                        last.then_inc(s["binit_ps"], 1)
                    else:
                        e = k - 1
                        after(pe, "hid_ready", g * 2 * E + 2 * e + 2)
                        after(pe, "y_added", g * E + e - 1)
                        for b in range(G):
                            for half in range(2):
                                last = pe.matmul(bank(6 + e % 2)[:, b, :], hid[:, e % 2, half, b * L:(b + 1) * L],
                                                 w2_sb[:, e, half, :], start=(half == 0), stop=(half == 1))
                        last.then_inc(s["y_ps"], 1)

        @block.scalar
        def _(act):
            give_credits(act, "act")
            def toeplitz(k):
                source = bass.AP(tensor=taps_long.tensor, offset=k * 16 * (2 * L - 1),
                                 ap=[[1, 128], [2 * L - 1, 16], [1, L]])
                act.dma_start(toep[:, k % 2, :, :], source).then_inc(toep_in[k % 2], 16)

            toeplitz(0)
            toeplitz(1)
            act.wait_ge(w_in, 16 * EARLY_LOADS)
            a0 = RB["temp"][0]
            act.activation(temp[:, 0:1], rb[:, a0:a0 + 1], ACT.Abs).then_inc(act_step, 1)
            act.wait_ge(act_step, 1)
            act.activation(temp[:, 1:2], temp[:, 0:1], ACT.Exp, scale=-1.0).then_inc(act_step, 1)
            act.wait_ge(act_step, 2)
            act.activation(temp[:, 2:3], temp[:, 1:2], ACT.Ln, bias=1.0).then_inc(act_step, 1)
            act.activation(static_g[:, :], r_of("static"), ACT.Tanh, scale=0.5).then_inc(act_step, 1)
            act.activation(half_bog2[:, :], r_of("bog2"), ACT.Copy, scale=0.5).then_inc(act_step, 1)
            act.wait_ge(act_step, 5)
            act.sem_inc(s["act_const"], 1)
            act.wait_ge(pool_step, 12)
            with act.Fori(0, NG) as g:
                v = g + 1
                after(act, "xt_ps", v)
                after(act, "proj_ready", G * g)
                act.activation(xc_pad[:, :, TAPS - 1:], bank(0), ACT.Copy).then_inc(s["xc_ready"], 1)
                after(act, "vb_ready", g)
                after(act, "v_kept", g)
                after(act, "q_ps", g)
                for b in range(G):
                    after(act, "proj_ready", g * G + b + 1)
                    pr = ps[1 + b % 2]
                    act.activation(qkv_g[:, b, :], pr[:, 0:NQKV], ACT.Silu).then_inc(s["silu_ready"], 1)
                    act.activation(graw[:, b, :], pr[:, NQKV:NQKV + 2 * H], ACT.Copy).then_inc(s["proj_free"], 1)
                after(act, "silu_ready", v * G)
                act.activation(sq_g[:, 0:2 * G, :].rearrange("p (b k) c -> p b (k c)", b=G), qkv_g[:, :, 0:2 * D],
                               ACT.Square).then_inc(s["sq_ready"], 1)
                after(act, "zsum_ready", v)
                act.activation(gtmp[:, :, :], graw[:, :, :], ACT.Tanh, scale=0.5).then_inc(s["tanh_ready"], 1)
                after(act, "q_ps", v)
                after(act, "gram_ps", g * 2 * H)
                act.activation(kq_c[:, :, 1, :], bank(0), ACT.Copy).then_inc(s["q_c"], 1)
                after(act, "vrev_ps", v)
                settle(act, "act")
                act.activation(src[:, bass.ds(g * G, G), 2, :], bank(3), ACT.Copy).then_inc(s["vrev_kept"], 1)
                after(act, "kh_ps", v)
                for h in range(H):
                    rows = slice(DH * h, DH * h + DH)
                    last = act.activation(kh_c[rows, h, :, :], ps[3][rows, :].rearrange("p (b t) -> p b t", b=G),
                                          ACT.Copy)
                last.then_inc(s["kh_cready"], 1)
                after(act, "kb_ps", v)
                act.activation(kq_c[:, :, 0, :], bank(0), ACT.Copy).then_inc(s["kb_c"], 1)
            for k in range(D // 16):
                after(act, "fir_ps", k + 1)
                if k + 2 < D // 16:
                    toeplitz(k + 2)
                if k % 2:
                    c = k // 2 * 32
                    act.activation(src[:, :, 1, c:c + 32].rearrange("p b c -> p c b"), bank(k // 2, 32), ACT.Copy
                                   ).then_inc(s["fir_kept"], 1)
            for n in range(NC):
                rows = slice(CH * n, CH * n + CH)
                for g in range(NG):
                    at = n * NG + g
                    after(act, "d_ps", at + 1)
                    act.activation(u[rows, GP * g:GP * g + GP, :],
                                   ps[6 + at % 2][rows, :].rearrange("p (r d) -> p r d", r=GP), ACT.Copy
                                   ).then_inc(s["u_ready"], 1)
            after(act, "delta_ready", NG)
            act.wait_ge(pool_step, 15)
            with act.Fori(0, NG) as g:
                v = g + 1
                after(act, "xat_ps", v)
                after(act, "z_ps", g)
                act.activation(xa_c, bank(0), ACT.Copy).then_inc(s["xac_ready"], 1)
                after(act, "vt_ps", v)
                after(act, "short_ps", g)
                act.activation(vc_pad[:, :, SHORT - 1:], bank(1), ACT.Copy).then_inc(s["vc_ready"], 1)
                after(act, "short_ps", v)
                settle(act, "act")
                act.activation(src[:, bass.ds(g * G, G), 0, :], bank(1), ACT.Copy).then_inc(s["short_ready"], 1)
                after(act, "short_ready", v)
                after(act, "ostats_ready", g)
                settle(act, "act")
                act.activation(sq_g[:, :, :], src[:, bass.ds(g * G, G), :, :].rearrange("p b s c -> p (b s) c"),
                               ACT.Square).then_inc(s["ssq_ready"], 1)
                after(act, "st_ps", v)
                act.activation(st_c, ps[0][0:32, :], ACT.Copy).then_inc(s["stc_ready"], 1)
                after(act, "h1_ps", v)
                act.activation(h1, ps[1][:, :], ACT.Gelu, bias=c_of("bg1")).then_inc(s["h1_ready"], 1)
                after(act, "lmax_ready", v)
                act.activation(pe4, lg, ACT.Exp).then_inc(s["exp_ready"], 1)
                after(act, "o_ready", v)
                act.activation(sq_g[:, 0:G, :], o_g, ACT.Square).then_inc(s["osq_ready"], 1)
                after(act, "st2_ps", v)
                act.activation(st2_c, ps[0][0:32, :], ACT.Copy).then_inc(s["st2c_ready"], 1)
                after(act, "h2_ps", v)
                act.activation(h2, ps[1][0:64, :], ACT.Gelu, bias=cb[0:64, CB["bog1"][0]:CB["bog1"][1]]
                               ).then_inc(s["h2_ready"], 1)
                after(act, "z_ps", v)
                act.activation(og, ps[0][:, 0:G], ACT.Tanh, scale=0.5, bias=half_bog2[:, :]).then_inc(s["og_tanh"], 1)
                after(act, "ont_ps", v)
                act.activation(on_c, bank(0), ACT.Copy).then_inc(s["onc_ready"], 1)
                after(act, "ct_ps", v)
                act.activation(c_c, bank(2), ACT.Copy).then_inc(s["cc_ready"], 1)
                after(act, "vh_ps", v)
                act.activation(vh, bank(2), ACT.Copy).then_inc(s["vh_ready"], 1)
                after(act, "x1t_ps", v)
                act.activation(x1_c, bank(2), ACT.Copy).then_inc(s["x1c_ready"], 1)
                after(act, "x2t_ps", v)
                act.activation(x2_c, bank(3), ACT.Copy).then_inc(s["x2c_ready"], 1)
                after(act, "rmax_ready", v)
                act.activation(score, ex, ACT.Exp).then_inc(s["rexp_ready"], 1)
                for e in range(E):
                    for half in range(2):
                        after(act, "hid_ps", g * 2 * E + 2 * e + half + 1)
                        if half == 0:
                            after(act, "y_ps", g * E + e - 1)
                        act.activation(hid[:, e % 2, half, :], ps[4 + half][:, :], ACT.Relu,
                                       bias=c_of("b1", 2 * e + half)).then_inc(s["hid_ready"], 1)
                    if e == 0:
                        after(act, "scoret_ps", v)
                        act.activation(sct, ps[3][0:E, :], ACT.Copy).then_inc(s["scoret_ready"], 1)

        @block.vector
        def _(dve):
            give_credits(dve, "dve")
            base = [0, 0]

            def own(ins):
                base[1] += 1
                ins.then_inc(dve_step, 1)
                dve.wait_ge(dve_step, base[0] + base[1])

            def rsqrt(y, a, n):
                t = nt1[:, 0:n]
                own(dve.tensor_scalar(y.bitcast(I32), a.bitcast(I32), -0.5, RSQRT_GUESS, ALU.mult, ALU.add))
                for i in range(3):
                    own(dve.tensor_tensor(out=t, in0=y, in1=y, op=ALU.mult))
                    own(dve.scalar_tensor_tensor(out=t, in0=t, scalar=-0.5, in1=a, op0=ALU.mult, op1=ALU.mult))
                    own(dve.scalar_tensor_tensor(out=y, in0=t, scalar=1.5, in1=y, op0=ALU.add, op1=ALU.mult))

            def wide(a, m):
                return a.unsqueeze(len(a.shape)).broadcast_to(list(a.shape) + [m])

            def mid(a, m):
                return a.unsqueeze(1).broadcast_to([a.shape[0], m, a.shape[1]])

            dve.wait_ge(w_in, 16 * EARLY_LOADS)
            after(dve, "ident_ready", 1)
            dve.tensor_tensor(out=wtap[:, :, :], in0=mid(w_of("qkv"), TAPS),
                              in1=wtap[:, :, :], op=ALU.mult)
            for t in range(SHORT):
                dve.tensor_scalar(diag_short[:, t, :], ident[:, :], c_of("short", t), None, ALU.mult)
            dve.tensor_scalar(wo_n[:, :], w_of("o"), c_of("norm"), None, ALU.mult)
            after(dve, "act_const", 1)
            own(dve.tensor_scalar(static_g[:, :], static_g[:, :], 0.5, 0.5, ALU.mult, ALU.add))
            a0 = RB["temp"][0]
            own(dve.scalar_tensor_tensor(out=temp[:, 3:4], in0=rb[:, a0:a0 + 1], scalar=0.0, in1=temp[:, 2:3],
                                         op0=ALU.max, op1=ALU.add))
            own(dve.reciprocal(temp[:, 4:5], temp[:, 3:4]))
            own(dve.tensor_scalar(bg2_t[:, :, :], mid(r_of("bg2"), G), temp[:, 4:5], None, ALU.mult))
            dve.sem_inc(s["dve_const"], 1)
            after(dve, "pool_const", 5)

            PROJ_STEPS = 13
            start = base[1]
            with dve.Fori(0, NG) as g:
                base[0], base[1] = start + g * PROJ_STEPS, 0
                seqs = bass.ds(g * G, G)
                after(dve, "proj_free", G * (g + 1))
                dve.tensor_tensor(out=gtmp[:, :, :], in0=graw[:, :, :], in1=mid(r_of("gate_bias"), G),
                                  op=ALU.add).then_inc(s["zsum_ready"], 1)
                after(dve, "sq_ready", g + 1)
                own(dve.tensor_reduce(out=ss_g[:, :, :].rearrange("p b h -> p (b h)"),
                                      in_=sq_g[:, 0:2 * G, :].rearrange("p k (h d) -> p (k h) d", h=H),
                                      axis=AX.X, op=ALU.add))
                own(dve.tensor_scalar(ss_g[:, :, :], ss_g[:, :, :], 1e-6, None, ALU.add))
                rsqrt(rn_g[:, :, :].rearrange("p b h -> p (b h)"), ss_g[:, :, :].rearrange("p b h -> p (b h)"),
                      G * 2 * H)
                after(dve, "kh_ps", g)
                dve.tensor_tensor(out=kh_g[:, :, :].rearrange("p b (h d) -> p b h d", h=H),
                                  in0=qkv_g[:, :, D:2 * D].rearrange("p b (h d) -> p b h d", h=H),
                                  in1=wide(rn_g[:, :, H:2 * H], DH), op=ALU.mult).then_inc(s["k_ready"], 1)
                after(dve, "tanh_ready", g + 1)
                own(dve.tensor_scalar(gates[:, seqs, :], gtmp[:, :, :], 0.5, 0.5, ALU.mult, ALU.add))
                after(dve, "k_ready", g + 1)
                after(dve, "kb_ps", g)
                dve.tensor_tensor(out=kb_g[:, :, :].rearrange("p b (h d) -> p b h d", h=H),
                                  in0=kh_g[:, :, :].rearrange("p b (h d) -> p b h d", h=H),
                                  in1=wide(gates[:, seqs, 0:H], DH), op=ALU.mult).then_inc(s["kb_ready"], 1)
                dve.tensor_copy(rq[:, seqs, :], rn_g[:, :, 0:H])
                dve.tensor_tensor(out=vb[:, :, :].rearrange("p (b h) d -> p b h d", h=H)[:, seqs, :, :],
                                  in0=qkv_g[:, :, 2 * D:3 * D].rearrange("p b (h d) -> p b h d", h=H),
                                  in1=wide(gates[:, seqs, 0:H], DH), op=ALU.mult).then_inc(s["vb_ready"], 1)
                rows_of = as_t[:, :, :, :].rearrange("p (b h) k t -> p b h (k t)", h=H)
                for r in range(2):
                    for h in range(H):
                        after(dve, "gram_ps", g * 2 * H + r * H + h + 1)
                        dve.tensor_tensor(out=rows_of[:, bass.ds(g * G + 2 * r, 2), h, :], in0=bank(4 + h, 2),
                                          in1=mid(masks[:, :, :].rearrange("p k t -> p (k t)"), 2),
                                          op=ALU.mult).then_inc(s["gram_kept"], 1)
            assert base[1] == PROJ_STEPS, base[1]
            base[0], base[1] = 0, start + NG * PROJ_STEPS

            dve.wait_ge(blocks_in, 16)
            for j in range(CH - 1):
                n = CH - 1 - j
                p = prod[:, 0:2 * (j + 1) * n].rearrange("p (a c i) -> p a c i", a=2, c=j + 1)
                own(dve.tensor_tensor(out=p, in0=blk[:, :, j, j + 1:].unsqueeze(2).broadcast_to([128, 2, j + 1, n]),
                                      in1=wide(inv[:, :, 0:j + 1, j], n), op=ALU.mult))
                own(dve.tensor_tensor(out=inv[:, :, 0:j + 1, j + 1:], in0=inv[:, :, 0:j + 1, j + 1:], in1=p,
                                      op=ALU.subtract))
            dve.sem_inc(s["solved"], 1)

            for n in range(1, NC):
                rows = slice(CH * n, CH * n + CH)
                for g in range(NG):
                    after(dve, "a_ps", (n - 1) * NG + g + 1)
                    pairs = vb[rows, GP * g:GP * g + GP, :]
                    dve.tensor_tensor(out=pairs, in0=pairs,
                                      in1=ps[4 + ((n - 1) * NG + g) % 2][rows, :].rearrange("p (r d) -> p r d", r=GP),
                                      op=ALU.subtract).then_inc(s["r_ready"], 1)
            after(dve, "fir_ps", D // 16)
            for g in range(NG):
                after(dve, "o_ps", g + 1)
                dve.tensor_tensor(out=src[:, g * G:g * G + G, 2, :].rearrange("p b (h d) -> p b h d", h=H),
                                  in0=ps[4 + g % 2][:, :].rearrange("p (b h d) -> p b h d", b=G, h=H),
                                  in1=wide(rq[:, g * G:g * G + G, :], DH), op=ALU.mult
                                  ).then_inc(s["delta_ready"], 1)

            def layernorm(y, dst, done):
                for b in range(G):
                    last = dve.bn_stats(out=bn6[:, b, :], in_=y[:, b, :])
                own(last)
                settle(dve, "dve")
                for b in range(G):
                    last = dve.bn_aggr(out=mv[:, b, :], in_=bn6[:, b, :])
                own(last)
                own(dve.tensor_scalar(sm1[:, 0:G], mv[:, :, 1], EPS, None, ALU.add))
                rsqrt(sm2[:, 0:G], sm1[:, 0:G], G)
                for b in range(G):
                    last = dve.tensor_scalar(dst[:, b, :], y[:, b, :], mv[:, b, 0:1], sm2[:, b:b + 1],
                                             ALU.subtract, ALU.mult)
                last.then_inc(s[done], 1)

            def head_stats(xs, squares, to, n):
                settle(dve, "dve")
                own(dve.tensor_reduce(out=sumx[:, 0:n * H], in_=xs.rearrange("p n (h d) -> p (n h) d", h=H),
                                      axis=AX.X, op=ALU.add))
                own(dve.tensor_reduce(out=sumq[:, 0:n * H], in_=squares.rearrange("p n (h d) -> p (n h) d", h=H),
                                      axis=AX.X, op=ALU.add))
                settle(dve, "dve")
                dve.tensor_reduce(out=to(2), in_=xs, axis=AX.X, op=ALU.add, apply_absolute_value=True)
                dve.tensor_reduce(out=to(0), in_=sumx[:, 0:n * H].rearrange("p (n h) -> p n h", h=H),
                                  axis=AX.X, op=ALU.add)
                own(dve.tensor_tensor(out=sm1[:, 0:n * H], in0=sumx[:, 0:n * H], in1=sumx[:, 0:n * H], op=ALU.mult))
                own(dve.scalar_tensor_tensor(out=sm1[:, 0:n * H], in0=sumq[:, 0:n * H], scalar=float(DH),
                                             in1=sm1[:, 0:n * H], op0=ALU.mult, op1=ALU.subtract))
                dve.tensor_reduce(out=to(1), in_=sm1[:, 0:n * H].rearrange("p (n h) -> p n h", h=H),
                                  axis=AX.X, op=ALU.add)
                own(dve.tensor_scalar(sm2[:, 0:n * H], sumq[:, 0:n * H], 1e-30, None, ALU.max))
                rsqrt(nt2[:, 0:n * H], sm2[:, 0:n * H], n * H)
                own(dve.tensor_tensor(out=sm2[:, 0:n * H], in0=sumq[:, 0:n * H], in1=nt2[:, 0:n * H], op=ALU.mult))
                own(dve.tensor_reduce(out=to(3), in_=sm2[:, 0:n * H].rearrange("p (n h) -> p n h", h=H),
                                      axis=AX.X, op=ALU.add))

            def by_head(a):
                return a.rearrange("p b (h d) -> p b h d", h=H)

            dve.wait_ge(pool_step, 15)
            dve.wait_ge(w_late, 16 * LATE_LOADS)
            MIX_STEPS = 119
            start = base[1]
            with dve.Fori(0, NG) as g:
                base[0], base[1] = start + g * MIX_STEPS, 0
                seqs = bass.ds(g * G, G)
                after(dve, "ssq_ready", g + 1)
                after(dve, "st_ps", g)

                def st_to(k):
                    return st[:, :, 0:16].rearrange("p b (s k) -> p b s k", k=4)[:, :, :, k]

                head_stats(src[:, seqs, :, :].rearrange("p b s c -> p (b s) c"), sq_g[:, :, :], st_to, 4 * G)
                dve.tensor_tensor(out=st[:, :, 0:16], in0=st[:, :, 0:16], in1=mid(stat_scale[:, :], G), op=ALU.mult
                                  ).then_inc(s["stats_ready"], 1)
                after(dve, "logit_ps", g + 1)
                own(dve.scalar_tensor_tensor(out=lg, in0=ps[0][:, 0:16].rearrange("p (b k) -> p b k", b=G),
                                             scalar=temp[:, 4:5], in1=bg2_t[:, :, :], op0=ALU.mult, op1=ALU.add))
                own(dve.tensor_reduce(out=red, in_=lg, axis=AX.X, op=ALU.max))
                dve.tensor_tensor(out=lg, in0=lg, in1=wide(red, 4), op=ALU.subtract).then_inc(s["lmax_ready"], 1)
                after(dve, "exp_ready", g + 1)
                own(dve.tensor_reduce(out=red, in_=pe4, axis=AX.X, op=ALU.add))
                own(dve.reciprocal(red, red))
                own(dve.tensor_tensor(out=pw, in0=pe4, in1=wide(red, 4), op=ALU.mult))
                own(dve.tensor_scalar(pw, pw, FLOOR, None, ALU.max))
                own(dve.tensor_reduce(out=red, in_=pw, axis=AX.X, op=ALU.add))
                own(dve.reciprocal(red, red))
                own(dve.tensor_tensor(out=pw, in0=pw, in1=wide(red, 4), op=ALU.mult))
                own(dve.tensor_tensor(out=w0, in0=gates[:, seqs, H:2 * H], in1=mid(static_g[:, :], G), op=ALU.mult))
                own(dve.tensor_tensor(out=w0, in0=w0, in1=wide(pw[:, :, 0], H), op=ALU.add))
                own(dve.tensor_tensor(out=by_head(o_g), in0=by_head(src[:, seqs, 0, :]), in1=wide(w0, DH),
                                      op=ALU.mult))
                for k in range(1, 4):
                    for b in range(G):
                        last = dve.scalar_tensor_tensor(
                            out=o_g[:, b, :], in0=src[:, bass.ds(g * G + b, 1), k, :].rearrange("p a c -> p (a c)"),
                            scalar=pw[:, b, k:k + 1], in1=o_g[:, b, :], op0=ALU.mult, op1=ALU.add)
                    if k < 3:
                        own(last)
                    else:
                        last.then_inc(s["o_ready"], 1)
                after(dve, "osq_ready", g + 1)
                after(dve, "o_ready", g + 1)
                after(dve, "st2_ps", g)
                after(dve, "stats_ready", g + 1)
                head_stats(o_g, sq_g[:, 0:G, :], lambda k: st2[:, :, k], G)
                own(dve.tensor_tensor(out=st2[:, :, 0:4], in0=st2[:, :, 0:4], in1=mid(stat_scale[:, 0:4], G),
                                      op=ALU.mult))
                dve.tensor_copy(st2[:, :, 4:8], st[:, :, 12:16]).then_inc(s["ostats_ready"], 1)
                after(dve, "og_tanh", g + 1)
                own(dve.tensor_scalar(og, og, 0.5, 0.5, ALU.mult, ALU.add))
                own(dve.tensor_tensor(out=sm1[:, 0:G], in0=og, in1=og, op=ALU.mult))
                own(dve.tensor_tensor(out=ogr, in0=sumq[:, 0:G * H].rearrange("p (b h) -> p b h", b=G),
                                      in1=wide(sm1[:, 0:G], H), op=ALU.mult))
                own(dve.tensor_scalar(ogr, ogr, 1.0 / DH, EPS, ALU.mult, ALU.add))
                rsqrt(sm2[:, 0:G * H], ogr.rearrange("p b h -> p (b h)"), G * H)
                own(dve.tensor_tensor(out=ogr, in0=sm2[:, 0:G * H].rearrange("p (b h) -> p b h", b=G),
                                      in1=wide(og, H), op=ALU.mult))
                dve.tensor_tensor(out=by_head(on_g), in0=by_head(o_g), in1=wide(ogr, DH), op=ALU.mult
                                  ).then_inc(s["on_ready"], 1)
                after(dve, "wo_ps", g + 1)
                own(dve.tensor_tensor(out=y_g, in0=bank(1), in1=xa, op=ALU.add))
                layernorm(y_g, x1, "x1_ready")
                after(dve, "k_rot_ps", g + 1)
                own(dve.tensor_tensor(out=kt, in0=bank(3), in1=mid(tab[:, 3, :], G), op=ALU.mult))
                own(dve.tensor_tensor(out=kr, in0=bank(2), in1=mid(tab[:, 2, :], G), op=ALU.mult))
                dve.tensor_tensor(out=kr, in0=kr, in1=kt, op=ALU.add).then_inc(s["kr_ready"], 1)
                after(dve, "qx_ps", g + 1)
                own(dve.tensor_tensor(out=qt, in0=bank(3), in1=mid(tab[:, 1, :], G), op=ALU.mult))
                own(dve.tensor_tensor(out=qr, in0=bank(2), in1=mid(tab[:, 0, :], G), op=ALU.mult))
                dve.tensor_tensor(out=qr, in0=qr, in1=qt, op=ALU.add).then_inc(s["qr_ready"], 1)
                after(dve, "sc_ps", g + 1)
                dve.tensor_tensor(out=sc_t, in0=bank(3), in1=mid(decay_sb[:, :], G), op=ALU.mult
                                  ).then_inc(s["sct_ready"], 1)
                after(dve, "att_ps", g + 1)
                after(dve, "x1_ready", g + 1)
                own(dve.tensor_tensor(out=y_g, in0=bank(2), in1=x1, op=ALU.add))
                layernorm(y_g, x2, "x2_ready")
                after(dve, "route_ps", g + 1)
                logits = ps[3][:, 0:G * E].rearrange("p (b e) -> p b e", b=G)
                own(dve.tensor_reduce(out=red, in_=logits, axis=AX.X, op=ALU.max))
                dve.tensor_tensor(out=ex, in0=logits, in1=wide(red, E), op=ALU.subtract
                                  ).then_inc(s["rmax_ready"], 1)
                after(dve, "rexp_ready", g + 1)
                for k, op in enumerate((ALU.is_ge, ALU.is_gt)):
                    own(dve.tensor_tensor(out=cmp_[:, :, :, k, :], in0=score.unsqueeze(2).broadcast_to([128, G, E, E]),
                                          in1=wide(score, E), op=op))
                for k in range(2):
                    own(dve.tensor_tensor(out=cmp_[:, :, :, k, :], in0=cmp_[:, :, :, k, :],
                                          in1=tie[:, k, :, :].unsqueeze(1).broadcast_to([128, G, E, E]), op=ALU.mult))
                own(dve.tensor_reduce(out=rank, in_=cmp_.rearrange("p b i k j -> p (b i) (k j)"), axis=AX.X,
                                      op=ALU.add))
                own(dve.scalar_tensor_tensor(out=ex, in0=rank, scalar=2.0, in1=score, op0=ALU.is_lt, op1=ALU.mult))
                own(dve.tensor_reduce(out=red, in_=ex, axis=AX.X, op=ALU.add))
                own(dve.reciprocal(red, red))
                dve.tensor_tensor(out=score, in0=ex, in1=wide(red, E), op=ALU.mult).then_inc(s["score_ready"], 1)
                after(dve, "x2_ready", g + 1)
                after(dve, "binit_ps", g + 1)
                own(dve.tensor_tensor(out=acc, in0=bank(3), in1=x2, op=ALU.add))
                after(dve, "score_ready", g + 1)
                for e in range(E):
                    after(dve, "y_ps", g * E + e + 1)
                    for b in range(G):
                        last = dve.scalar_tensor_tensor(out=acc[:, b, :], in0=bank(6 + e % 2)[:, b, :],
                                                        scalar=score[:, b, e:e + 1], in1=acc[:, b, :],
                                                        op0=ALU.mult, op1=ALU.add)
                    last.then_inc(s["y_added"], 1)
                    after(dve, "y_added", g * E + e + 1)
                dve.wait_ge(stored, 16 * (g + 1))
                layernorm(acc, fin, "fin_ready")
            assert base[1] == MIX_STEPS, base[1]


def xpos_tables():
    import numpy as np

    half = D // 2
    scale_vec = (np.arange(0, D, 2, dtype=np.float32) + np.float32(0.4 * D)) / np.float32(1.4 * D)
    pos = np.arange(L, dtype=np.float32)
    scale = scale_vec[None, :] ** (pos / np.float32(512.0))[:, None]
    freqs = np.float32(1.0) / np.float32(10000.0) ** (np.arange(half, dtype=np.float32) / np.float32(half))
    angle = (pos[:, None] * freqs[None, :]).astype(np.float64)
    sign = np.tile(np.array([-1.0, 1.0]), half)
    out = []
    for sc in (scale.astype(np.float64), 1.0 / scale.astype(np.float64)):
        out += [np.repeat(np.cos(angle) * sc, 2, axis=1), np.repeat(np.sin(angle) * sc, 2, axis=1) * sign]
    return np.ascontiguousarray(np.stack(out).transpose(2, 0, 1).astype(np.float32))


def decay_table():
    import numpy as np

    diff = np.arange(L)[None, :] - np.arange(L)[:, None]
    return np.where(diff >= 0, 0.96875 ** np.maximum(diff, 0), 0.0).astype(np.float32)


def kernel(**inputs):
    import numpy as np
    import concourse.bacc as bacc
    from concourse.bass_utils import run_bass_kernel_spmd

    a = {k: np.asarray(v) for k, v in inputs.items()}
    w = {k[8:]: v for k, v in a.items() if k.startswith("L0_attn_")}

    swap = np.arange(D) ^ 1
    wbundle = np.concatenate(
        [w["Wq"], w["Wk"], w["Wv"], w["Wb"], w["Wres"], w["Wg1"][:D], w["Wog1"][:D], w["Wg2"], w["Wo"],
         a["L0_xattn_Wq"], a["L0_xattn_Wq"][:, swap], a["L0_xattn_Wk"], a["L0_xattn_Wk"][:, swap],
         a["L0_xattn_Wv"], a["L0_ffn_Wg"]], axis=1)
    taps = np.concatenate([w["wq_conv"], w["wk_conv"], w["wv_conv"]], axis=0).T
    rbundle = np.concatenate([np.zeros(H, np.float32), w["bres"], w["bg2"], w["logit_temp"],
                              w["conv_res_logit"], w["bog2"], taps.reshape(-1)])
    col = [w["bg1"][:, None], np.concatenate([w["bog1"], np.zeros(D - D // 2, np.float32)])[:, None],
           np.tile(w["norm_w"], H)[:, None], w["fir_short"].reshape(D, SHORT),
           a["L0_ffn_b1"].reshape(2 * E, 128).T]
    cbundle = np.concatenate(col, axis=1)
    ws = np.zeros((32, D + D // 2), np.float32)
    ws[:16, :D] = w["Wg1"][D:]
    ws[:8, D:] = w["Wog1"][D:]
    taps_long = np.zeros((D, 2 * L - 1), np.float32)
    taps_long[:, L - 1:L - 1 + LONG] = w["fir_long"].reshape(D, LONG)[:, ::-1]
    arrays = {
        "x": a["x"], "ctx_in": a["ctx_1024"], "wbundle": wbundle, "rbundle": rbundle, "cbundle": cbundle, "ws": ws,
        "wog2": w["Wog2"], "taps_long": taps_long, "w1": a["L0_ffn_W1"], "w2": a["L0_ffn_W2"], "b2": a["L0_ffn_b2"],
        "tables": xpos_tables(), "decay": decay_table(),
    }
    arrays = {k: np.ascontiguousarray(v) for k, v in arrays.items()}
    nc = bacc.Bacc("TRN2", target_bir_lowering=False, num_devices=1)
    args = [nc.dram_tensor(k, v.shape, mybir.dt.from_np(v.dtype), kind="ExternalInput").ap()
            for k, v in arrays.items()]
    args += [nc.dram_tensor(k, (NP, NC, CH, CH), F32, kind="Internal").ap() for k in ("blocks", "inverses")]
    out = nc.dram_tensor("result", (B, L, D), F32, kind="ExternalOutput").ap()
    decoder_kernel(nc, *args, out)
    r = run_bass_kernel_spmd(nc, [arrays], core_ids=[0])
    return r.results[0]["result"]
```

```python
from contextlib import ExitStack

import concourse.bass as bass
from concourse import mybir

F32 = mybir.dt.float32
I32 = mybir.dt.int32
ALU = mybir.AluOpType
ACT = mybir.ActivationFunctionType
AX = mybir.AxisListType

B, L, D = 16, 128, 128
H, DH = 4, 32
G = 4
NG = B // G
N = G * L
NP = B * H
GP = G * H
CH = 32
NC = L // CH
E, HID = 8, 256
NQKV = 3 * D
TAPS = 4
LONG, SHORT = 64, 5
PAD = SHORT - 1
EPS = 1e-5
FLOOR = 0.02
RSQRT_GUESS = float(0x5F3759DF)

WB = {}
_at = 0
for _name, _n in (("qkv", NQKV), ("gates", 2 * H), ("g1", D), ("og1", D // 2), ("g2", 4), ("o", D),
                  ("xq", D), ("xqr", D), ("xk", D), ("xkr", D), ("xv", D), ("route", E)):
    WB[_name] = (_at, _at + _n)
    _at += _n
WB_N = _at
RB = {}
_at = 0
for _name, _n in (("gate_bias", 2 * H), ("bg2", 4), ("temp", 1), ("static", H), ("bog2", 1)):
    RB[_name] = (_at, _at + _n)
    _at += _n
RB_N = _at
CB = {}
_at = 0
for _name, _n in (("bg1", 1), ("bog1", 1), ("norm", 1), ("short", SHORT), ("b1", 2 * E)):
    CB[_name] = (_at, _at + _n)
    _at += _n
CB_N = _at


def decoder_kernel(nc, x, ctx_in, wbundle, rbundle, cbundle, ws, wog2, taps_long, w1, w2, b2, tables, decay,
                   blocks_dram, inverse_dram, out):
    stack = ExitStack()
    with stack:
        def sb(name, shape, dt=F32):
            return stack.enter_context(nc.sbuf_tensor(name, shape, dt))

        def sem(name):
            return stack.enter_context(nc.semaphore(name))

        wb = sb("wb", [128, WB_N])
        rb = sb("rb", [128, RB_N])
        cb = sb("cb", [128, CB_N])
        ws_sb = sb("ws_sb", [32, D + D // 2])
        wog2_sb = sb("wog2_sb", [D // 2, 1])
        w1_sb = sb("w1_sb", [128, E, HID])
        w2_sb = sb("w2_sb", [128, E, 2, D])
        b2_sb = sb("b2_sb", [E, D])
        tab = sb("tab", [128, 4, L])
        decay_sb = sb("decay_sb", [128, L])
        ident = sb("ident", [128, 128])
        flip = sb("flip", [128, 128])
        masks = sb("masks", [128, 2, L])
        tie = sb("tie", [128, 2, E, E])
        stat_scale = sb("stat_scale", [128, 16])
        wtap = sb("wtap", [128, TAPS, NQKV])
        diag_short = sb("diag_short", [128, SHORT, 128])
        wo_n = sb("wo_n", [128, D])
        temp = sb("temp", [128, 8])
        bg2_t = sb("bg2_t", [128, G, 4])
        static_g = sb("static_g", [128, H])
        half_bog2 = sb("half_bog2", [128, 1])

        def w_of(name):
            a, b = WB[name]
            return wb[:, a:b]

        def r_of(name):
            a, b = RB[name]
            return rb[:, a:b]

        def c_of(name, i=0):
            a, _ = CB[name]
            return cb[:, a + i:a + i + 1]

        src = sb("src", [128, B, 4, D])
        vb = sb("vb", [128, NP, DH])
        as_t = sb("as_t", [128, NP, 2, L])
        early = sb("early", [128, 3 * NP * CH])
        inv_t = early[:, 0:NP * CH].rearrange("p (r i) -> p r i", r=NP)
        u = early[:, NP * CH:2 * NP * CH].rearrange("p (r i) -> p r i", r=NP)
        fir_c = early[:, NP * CH:NP * CH + 2 * N].rearrange("p (k b t) -> p k b t", k=2, b=4)
        blk = early[:, 2 * NP * CH:3 * NP * CH].rearrange("p (a j i) -> p a j i", a=2, j=CH)
        rq = sb("rq", [128, B, H])
        gates = sb("gates", [128, B, 2 * H])
        inv = sb("inv", [128, 2, CH, CH])
        o_c = inv[:, :, :, :].rearrange("p a j i -> p (a j i)").rearrange("p (g b t) -> p g b t", g=NG, b=G)
        prod = sb("prod", [128, 2 * 272])
        toep = sb("toep", [128, 2, 16, L])

        qkv_g = early[:, 0:G * NQKV].rearrange("p (b c) -> p b c", b=G)
        kh_g = early[:, G * NQKV:G * NQKV + N].rearrange("p (b c) -> p b c", b=G)
        kh_c = early[:, 4 * N:8 * N].rearrange("p (h b t) -> p h b t", h=H, b=G)
        x_g = early[:, 8 * N:9 * N].rearrange("p (b c) -> p b c", b=G)
        kb_g = early[:, 9 * N:10 * N].rearrange("p (b c) -> p b c", b=G)
        kq_c = early[:, 10 * N:12 * N].rearrange("p (b k t) -> p b k t", b=G, k=2)
        xc_pad = sb("xc_pad", [128, G, PAD + L])
        vc_pad = sb("vc_pad", [128, G, PAD + L])
        v_columns = (xc_pad, vc_pad)
        graw = sb("graw", [128, G, 2 * H])
        gtmp = sb("gtmp", [128, G, 2 * H])
        sq_g = sb("sq_g", [128, G * 4, D])
        ss_g = sb("ss_g", [128, G, 2 * H])
        rn_g = sb("rn_g", [128, G, 2 * H])
        nt1 = sb("nt1", [128, 64])
        nt2 = sb("nt2", [128, 64])
        sumx = sb("sumx", [128, NP])
        sumq = sb("sumq", [128, NP])
        sm1 = sb("sm1", [128, NP])
        sm2 = sb("sm2", [128, NP])
        st_all = sb("st_all", [128, B, 16])

        old = [[toep[:, :, :, :].rearrange("p a b c -> p (a b c)"), 0, 2 * 16 * L],
               [as_t[:, :, :, :].rearrange("p a b c -> p (a b c)"), 0, NP * 2 * L],
               [early[:, :], 0, 3 * NP * CH]]

        def over(n, parts=128):
            for region in old:
                memory, a, size = region
                if a + n <= size:
                    region[1] += n
                    return memory[0:parts, a:a + n]
            raise AssertionError("no room")

        def over3(b, c, parts=128):
            return over(b * c, parts).rearrange("p (b c) -> p b c", b=b)

        xa = over3(G, D)
        xt = over3(G, D)
        xa_c = over3(G, L)
        c_g = over3(G, D)
        c_c = over3(G, L)
        vh = over3(G, D)
        kr = over3(G, L)
        kt = over3(G, L)
        assert [region[1] > 0 for region in old] == [True, False, False]
        old[0][1] = 2 * 16 * L
        st = over3(G, 32)
        st2 = over3(G, 32)
        st_c = over(N, 32)
        st2_c = over(N, 32)
        h1 = over(N)
        h2 = over(N, 64)
        lg = over3(G, 4)
        pe4 = over3(G, 4)
        pw = over3(G, 4)
        red = over(G)
        w0 = over3(G, H)
        og = over(G)
        ogr = over3(G, H)
        o_g = over3(G, D)
        on_g = over3(G, D)
        on_c = over3(G, L)
        y_g = over3(G, D)
        bn6 = over3(G, 6)
        mv = over3(G, 2)
        x1 = over3(G, D)
        x1_c = over3(G, L)
        qr = over3(G, L)
        qt = over3(G, L)
        sc_t = over3(G, L)
        x2 = over3(G, D)
        x2_c = over3(G, L)
        ex = over3(G, E)
        cmp_ = over(G * E * 2 * E).rearrange("p (b i k j) -> p b i k j", b=G, i=E, k=2)
        rank = over3(G, E)
        score = over3(G, E)
        sct = over(N, E)
        hid = over(2 * 2 * N).rearrange("p (s k n) -> p s k n", s=2, k=2)
        acc = over3(G, D)
        fin = over3(G, D)

        ps = [stack.enter_context(nc.psum_tensor(f"bank{i}", [128, 512], F32)) for i in range(8)]

        def bank(i, b=G):
            return ps[i][:, :].rearrange("p (b c) -> p b c", b=b)

        w_in = sem("w_in")
        w_late = sem("w_late")
        x_in = sem("x_in")
        toep_in = [sem("toep_in0"), sem("toep_in1")]
        blocks_out = sem("blocks_out")
        blocks_in = sem("blocks_in")
        inverse_out = sem("inverse_out")
        inverse_in = sem("inverse_in")
        xa_in = sem("xa_in")
        xt_in = sem("xt_in")
        ctx_loaded = sem("ctx_loaded")
        stored = sem("stored")
        dve_step = sem("dve_step")
        pool_step = sem("pool_step")
        act_step = sem("act_step")

        names = ("ident_ready pool_const act_const dve_const "
                 "vrev_ps vrev_kept xt_ps xc_ready proj_ready proj_free silu_ready zsum_ready tanh_ready sq_ready k_ready kb_ready "
                 "vb_ready v_kept q_ps q_c kh_ps kh_cready kb_ps kb_c gram_ps gram_kept "
                 "solved fir_ps fir_c firt_ps fir_kept a_ps r_ready d_ps u_ready o_ps oc_ready ot_ps delta_ready "
                 "xat_ps xac_ready vt_ps vc_ready short_ps short_ready ssq_ready sums_ready stats_ready st_ready st2v_ready st_ps "
                 "stc_ready h1_ps h1_ready logit_ps lmax_ready exp_ready o_ready osq_ready ostats_ready st2_ps "
                 "st2c_ready h2_ps h2_ready z_ps og_tanh on_ready ont_ps onc_ready wo_ps x1_ready "
                 "ct_ps cc_ready vh_ps vh_ready k_rot_ps kr_ready x1t_ps x1c_ready qx_ps qr_ready sc_ps sct_ready "
                 "att_ps x2_ready "
                 "x2t_ps x2c_ready route_ps rmax_ready rexp_ready score_ready scoret_ps scoret_ready "
                 "binit_ps hid_ps hid_ready y_ps sum_started y_added fin_ready").split()
        s = {n: sem(n) for n in names}

        CREDITS = {
            "pe": {"proj_ready": 1, "q_ps": 1, "kh_ps": 1, "kb_ps": 1, "gram_ps": 1,
                   "z_ps": 1, "st_ps": 1, "st2_ps": 1, "y_ps": 2},
            "act": {"kb_c": 1, "proj_free": 2, "onc_ready": 1, "hid_ready": 2},
            "dve": {"vb_ready": 1, "gram_kept": H, "x1_ready": 1, "x2_ready": 1, "ostats_ready": 1, "y_added": 2,
                    "fin_ready": 1, "sum_started": 1},
            "pool": {"v_kept": 1},
        }
        credit = {n: k for of in CREDITS.values() for n, k in of.items()}

        def give_credits(eng, who):
            for n, k in CREDITS[who].items():
                eng.sem_inc(s[n], k)

        settled = {who: sem("settled_" + who) for who in ("act", "dve")}

        def settle(eng, who):
            eng.sem_inc(settled[who], 1)

        block = stack.enter_context(nc.Block())

        EARLY_LOADS, LATE_LOADS = 4, 8
        CW = 16
        CHUNKS = D // CW

        @block.sync
        def _(sp):
            sp.sem_inc(stored, 16)
            def every_partition(source, a, n):
                return bass.AP(tensor=source.tensor, offset=a, ap=[[0, 128], [1, n]])

            sp.dma_start(x_g[:, :, :], x[0:G].rearrange("b t c -> t b c")).then_inc(x_in, 16)
            for dst, source in ((wb[:, :], wbundle),
                                (rb[:, :], every_partition(rbundle, 0, RB_N)),
                                (wtap[:, :, :].rearrange("p t n -> p (t n)"),
                                 every_partition(rbundle, RB_N, TAPS * NQKV)),
                                (cb[:, :], cbundle)):
                sp.dma_start(dst, source).then_inc(w_in, 16)
            for dst, source in ((ws_sb[:, :], ws), (wog2_sb[:, :], wog2),
                                (tab[:, :, :], tables), (decay_sb[:, :], decay), (b2_sb[:, :], b2),
                                (w1_sb[:, :, :], w1.rearrange("e d h -> d e h")),
                                (w2_sb[:, :, 0, :], w2[:, 0:128, :].rearrange("e h d -> h e d")),
                                (w2_sb[:, :, 1, :], w2[:, 128:256, :].rearrange("e h d -> h e d"))):
                sp.dma_start(dst, source).then_inc(w_late, 16)
            with sp.Fori(1, NG) as g:
                sp.wait_ge(s["xt_ps"], g)
                sp.dma_start(x_g[:, :, :], x[bass.ds(g * G, G)].rearrange("b t c -> t b c")).then_inc(x_in, 16)
            for g in range(NG):
                sp.wait_ge(s["gram_kept"], 2 * H * (g + 1) + credit["gram_kept"])
                for n in range(NC):
                    rows = slice(CH * n, CH * n + CH)
                    sp.dma_start(blocks_dram[GP * g:GP * g + GP, n].rearrange("r j i -> j r i"),
                                 as_t[rows, GP * g:GP * g + GP, 0, rows]).then_inc(blocks_out, 16)
            sp.wait_ge(blocks_out, 16 * NG * NC)
            sp.wait_ge(s["v_kept"], NG + credit["v_kept"])
            sp.wait_ge(s["vb_ready"], NG + credit["vb_ready"])
            sp.dma_start(blk[:, :, :, :].rearrange("p a j i -> p (a j i)"),
                         blocks_dram.rearrange("r n j i -> (r n j i)").rearrange("(p m) -> p m", p=128)
                         ).then_inc(blocks_in, 16)
            sp.wait_ge(s["solved"], 1)
            sp.dma_start(inverse_dram.rearrange("r n j i -> (r n j i)").rearrange("(p m) -> p m", p=128),
                         inv[:, :, :, :].rearrange("p a j i -> p (a j i)")).then_inc(inverse_out, 16)
            sp.wait_ge(inverse_out, 16)
            for n in range(NC):
                rows = slice(CH * n, CH * n + CH)
                sp.dma_start(inv_t[rows, :, :], inverse_dram[:, n].rearrange("r j i -> j r i")).then_inc(inverse_in, 16)
            sp.wait_ge(s["fir_ps"], CHUNKS)
            sp.dma_start(xt, x[0:G].rearrange("b t c -> t b c")).then_inc(xt_in, 16)
            sp.dma_start(xa, x[0:G].rearrange("b t c -> t b c")).then_inc(xa_in, 16)
            sp.dma_start(c_g, ctx_in[0:G].rearrange("b t c -> t b c")).then_inc(ctx_loaded, 16)

            def load_xt(g):
                sp.wait_ge(s["xat_ps"], g)
                sp.dma_start(xt, x[bass.ds(g * G, G)].rearrange("b t c -> t b c")).then_inc(xt_in, 16)

            def load_x(g):
                sp.wait_ge(s["x1_ready"], g + credit["x1_ready"])
                sp.dma_start(xa, x[bass.ds(g * G, G)].rearrange("b t c -> t b c")).then_inc(xa_in, 16)

            def load_ctx(g):
                sp.wait_ge(s["ct_ps"], g)
                sp.dma_start(c_g, ctx_in[bass.ds(g * G, G)].rearrange("b t c -> t b c")).then_inc(ctx_loaded, 16)

            def store(g):
                sp.wait_ge(s["fin_ready"], g + 1 + credit["fin_ready"])
                sp.dma_start(out[bass.ds(g * G, G)].rearrange("b t c -> t b c"), fin).then_inc(stored, 16)

            load_ctx(1)
            load_xt(1)
            load_x(1)
            with sp.Fori(2, NG) as g:
                load_xt(g)
                load_ctx(g)
                load_x(g)
                store(g - 2)
            store(NG - 2)
            store(NG - 1)
            sp.wait_ge(stored, 16 * (NG + 1))

        @block.gpsimd
        def _(pool):
            give_credits(pool, "pool")
            pool.memset(ident[:, :], 0.0).then_inc(pool_step, 1)
            pool.memset(masks[:, :, :], 1.0).then_inc(pool_step, 1)
            pool.memset(tie[:, :, :, :], 1.0).then_inc(pool_step, 1)
            pool.memset(xc_pad[:, :, :], 0.0).then_inc(pool_step, 1)
            pool.memset(vc_pad[:, :, :], 0.0).then_inc(pool_step, 1)
            pool.memset(kh_c[:, :, :, :], 0.0).then_inc(pool_step, 1)
            pool.memset(inv[:, :, :, :], 0.0).then_inc(pool_step, 1)
            for k, scale in enumerate((1 / D, 1 / (H * DH * DH), 1 / D, 1 / H)):
                pool.memset(stat_scale[:, :].rearrange("p (a k) -> p a k", k=4)[:, :, k], scale).then_inc(pool_step, 1)
            pool.memset(flip[:, :], 0.0).then_inc(pool_step, 1)
            pool.wait_ge(pool_step, 12)
            pool.affine_select(out=flip[:, :], in_=flip[:, :], compare_op=ALU.not_equal, fill=1.0, base=1 - L,
                               pattern=[[1, 128]], channel_multiplier=1).then_inc(pool_step, 1)
            pool.affine_select(out=ident[:, :], in_=ident[:, :], compare_op=ALU.not_equal, fill=1.0, base=0,
                               pattern=[[-1, 128]], channel_multiplier=1).then_inc(s["ident_ready"], 1)
            pool.affine_select(out=masks[:, 0, :], in_=masks[:, 0, :], compare_op=ALU.is_gt, fill=0.0, base=0,
                               pattern=[[1, L]], channel_multiplier=-1).then_inc(s["pool_const"], 1)
            pool.affine_select(out=masks[:, 1, :], in_=masks[:, 1, :], compare_op=ALU.is_ge, fill=0.0, base=0,
                               pattern=[[1, L]], channel_multiplier=-1).then_inc(s["pool_const"], 1)
            pool.affine_select(out=tie[:, 0, :, :], in_=tie[:, 0, :, :], compare_op=ALU.is_gt, fill=0.0, base=0,
                               pattern=[[1, E], [-1, E]], channel_multiplier=0).then_inc(s["pool_const"], 1)
            pool.affine_select(out=tie[:, 1, :, :], in_=tie[:, 1, :, :], compare_op=ALU.is_gt, fill=0.0, base=0,
                               pattern=[[-1, E], [1, E]], channel_multiplier=0).then_inc(s["pool_const"], 1)
            pool.affine_select(out=inv[:, :, :, :], in_=inv[:, :, :, :], compare_op=ALU.not_equal, fill=1.0, base=0,
                               pattern=[[0, 2], [1, CH], [-1, CH]], channel_multiplier=0).then_inc(s["pool_const"], 1)
            with pool.Fori(0, NG) as g:
                pool.wait_ge(s["silu_ready"], (g + 1) * G)
                pool.tensor_copy(src[:, bass.ds(g * G, G), 3, :], qkv_g[:, :, 2 * D:3 * D]).then_inc(s["v_kept"], 1)
            pool.wait_ge(s["delta_ready"], NG)
            pool.memset(st, 0.0).then_inc(pool_step, 1)
            pool.memset(st2, 0.0).then_inc(pool_step, 1)
            pool.wait_ge(pool_step, 15)
            pool.wait_ge(s["stats_ready"], 4)
            with pool.Fori(0, NG) as g:
                pool.wait_ge(s["st_ps"], g + credit["st_ps"])
                pool.tensor_copy(st[:, :, 0:16], st_all[:, bass.ds(g * G, G), :]).then_inc(s["st_ready"], 1)
                pool.wait_ge(s["st2_ps"], g + credit["st2_ps"])
                pool.tensor_copy(st2[:, :, 4:8], st_all[:, bass.ds(g * G, G), 12:16]).then_inc(s["st2v_ready"], 1)

        @block.tensor
        def _(pe):
            give_credits(pe, "pe")
            def transposes(dst, source, rows=128):
                for b in range(G):
                    last = pe.transpose(ps[dst][0:rows, b * L:(b + 1) * L], source[:, b, :], ident[:, :])
                return last

            pe.wait_ge(s["ident_ready"], 1)
            pe.wait_ge(pool_step, 13)
            with pe.Fori(0, NG) as g:
                pe.wait_ge(x_in, 16 * (g + 1))
                pe.wait_ge(s["kb_c"], g + credit["kb_c"])
                transposes(0, x_g).then_inc(s["xt_ps"], 1)
                pe.wait_ge(s["xc_ready"], g + 1)
                pe.wait_ge(s["dve_const"], 1)
                pe.wait_ge(w_in, 16 * EARLY_LOADS)
                for b in range(G):
                    pe.wait_ge(s["proj_free"], g * G + b - 1 + credit["proj_free"])
                    pr = ps[1 + b % 2]
                    for t in range(TAPS):
                        pe.matmul(pr[:, 0:NQKV], xc_pad[:, b, PAD - TAPS + 1 + t:PAD - TAPS + 1 + t + L], wtap[:, t, :],
                                  start=(t == 0), stop=(t == TAPS - 1))
                    pe.matmul(pr[:, NQKV:NQKV + 2 * H], xc_pad[:, b, PAD:PAD + L], w_of("gates"),
                              start=True, stop=True).then_inc(s["proj_ready"], 1)
                pe.wait_ge(s["silu_ready"], (g + 1) * G)
                transposes(0, qkv_g[:, :, 0:D]).then_inc(s["q_ps"], 1)
                pe.matmul(bank(3), flip[:, :], qkv_g[:, :, 2 * D:3 * D], start=True, stop=True
                          ).then_inc(s["vrev_ps"], 1)
                pe.wait_ge(s["k_ready"], g + 1)
                pe.wait_ge(s["vrev_kept"], g + 1)
                transposes(3, kh_g).then_inc(s["kh_ps"], 1)
                pe.wait_ge(s["kb_ready"], g + 1)
                pe.wait_ge(s["q_c"], g + 1)
                transposes(0, kb_g).then_inc(s["kb_ps"], 1)
                pe.wait_ge(s["kb_c"], g + 1 + credit["kb_c"])
                pe.wait_ge(s["kh_cready"], g + 1)
                for r in range(2):
                    for h in range(H):
                        pe.wait_ge(s["gram_kept"], g * 2 * H + r * H + h + 1 - H + credit["gram_kept"])
                        for b in (2 * r, 2 * r + 1):
                            last = pe.matmul(ps[4 + h][:, (b % 2) * 2 * L:(b % 2 + 1) * 2 * L], kh_c[:, h, b, :],
                                             kq_c[:, b, :, :].rearrange("p k t -> p (k t)"), start=True, stop=True)
                        last.then_inc(s["gram_ps"], 1)
            pe.wait_ge(s["v_kept"], NG + credit["v_kept"])
            pe.wait_ge(s["kb_c"], NG + credit["kb_c"])
            pe.wait_ge(s["proj_free"], B + credit["proj_free"])
            pe.wait_ge(s["kh_cready"], NG)
            for g in range(NG + 1):
                if g < NG:
                    if g >= 2:
                        pe.wait_ge(s["vc_ready"], g - 1)
                    transposes(g % 2, src[:, g * G:g * G + G, 3, :]).then_inc(s["vt_ps"], 1)
                if g:
                    pe.wait_ge(s["vc_ready"], g)
                    if g >= 3:
                        pe.wait_ge(s["short_ready"], g - 2)
                    for b in range(G):
                        for k in range(SHORT):
                            last = pe.matmul(bank(2 + (g - 1) % 2)[:, b, :], v_columns[(g - 1) % 2][:, b, k:k + L],
                                             diag_short[:, k, :], start=(k == 0), stop=(k == SHORT - 1))
                    last.then_inc(s["short_ps"], 1)
            for k in range(CHUNKS + 1):
                if k < CHUNKS:
                    pe.wait_ge(toep_in[k % 2], 16 * (k // 2 + 1))
                    if k < 2:
                        pe.wait_ge(s["vc_ready"], NG)
                    else:
                        pe.wait_ge(s["fir_c"], k - 1)
                    for c in range(CW):
                        last = pe.matmul(ps[k % 2][c % 4 * 32:c % 4 * 32 + B, c // 4 * L:(c // 4 + 1) * L],
                                         src[:, :, 2, k * CW + c],
                                         toep[:, k % 2, c, :], start=True, stop=True)
                    last.then_inc(s["fir_ps"], 1)
                if k:
                    pe.wait_ge(s["fir_c"], k)
                    if k < 3:
                        pe.wait_ge(s["short_ready"], NG)
                    else:
                        pe.wait_ge(s["fir_kept"], k - 2)
                    transposes(2 + (k - 1) % 2, fir_c[:, (k - 1) % 2, :, :]).then_inc(s["firt_ps"], 1)
            def xat(g):
                pe.wait_ge(xt_in, 16 * (g + 1))
                pe.wait_ge(s["onc_ready"], g + credit["onc_ready"])
                transposes(0, xt).then_inc(s["xat_ps"], 1)

            def source_gate(g):
                pe.wait_ge(s["xac_ready"], g + 1)
                pe.wait_ge(s["x1_ready"], g + credit["x1_ready"])
                pe.matmul(ps[1][:, :], w_of("g1"), xa_c.rearrange("p b t -> p (b t)"), start=True, stop=False)
                pe.wait_ge(s["st_ready"], g + 1)
                transposes(0, st, 32).then_inc(s["st_ps"], 1)
                pe.wait_ge(s["stc_ready"], g + 1)
                pe.matmul(ps[1][:, :], ws_sb[:, 0:D], st_c, start=False, stop=True).then_inc(s["h1_ps"], 1)

            def source_logits(g):
                pe.wait_ge(s["h1_ready"], g + 1)
                for b in range(G):
                    last = pe.matmul(ps[0][:, b * 4:b * 4 + 4], h1[:, b * L:(b + 1) * L], w_of("g2"),
                                     start=True, stop=True)
                last.then_inc(s["logit_ps"], 1)
                pe.matmul(ps[1][0:64, :], w_of("og1"), xa_c.rearrange("p b t -> p (b t)"), start=True, stop=False)

            def output_gate(g):
                pe.wait_ge(s["ostats_ready"], g + 1 + credit["ostats_ready"])
                pe.wait_ge(s["st2v_ready"], g + 1)
                transposes(0, st2, 32).then_inc(s["st2_ps"], 1)
                pe.wait_ge(s["st2c_ready"], g + 1)
                pe.matmul(ps[1][0:64, :], ws_sb[:, D:D + 64], st2_c, start=False, stop=True).then_inc(s["h2_ps"], 1)

            def output_z(g):
                pe.wait_ge(s["h2_ready"], g + 1)
                for b in range(G):
                    last = pe.matmul(ps[0][:, b:b + 1], h2[:, b * L:(b + 1) * L], wog2_sb[:, :], start=True, stop=True)
                last.then_inc(s["z_ps"], 1)

            def ont(g):
                pe.wait_ge(s["on_ready"], g + 1)
                transposes(0, on_g).then_inc(s["ont_ps"], 1)

            def wo(g):
                pe.wait_ge(s["onc_ready"], g + 1 + credit["onc_ready"])
                for b in range(G):
                    last = pe.matmul(bank(1)[:, b, :], on_c[:, b, :], wo_n[:, :], start=True, stop=True)
                last.then_inc(s["wo_ps"], 1)

            def ct(g):
                pe.wait_ge(ctx_loaded, 16 * (g + 1))
                pe.wait_ge(s["x2_ready"], g + credit["x2_ready"])
                transposes(2, c_g).then_inc(s["ct_ps"], 1)

            def values(g):
                pe.wait_ge(s["cc_ready"], g + 1)
                for b in range(G):
                    last = pe.matmul(bank(2)[:, b, :], c_c[:, b, :], w_of("xv"), start=True, stop=True)
                last.then_inc(s["vh_ps"], 1)

            def keys(g):
                pe.wait_ge(s["vh_ready"], g + 1)
                pe.wait_ge(s["sum_started"], g + credit["sum_started"])
                pe.matmul(ps[2][:, :], w_of("xk"), c_c.rearrange("p b t -> p (b t)"), start=True, stop=True)
                pe.matmul(ps[3][:, :], w_of("xkr"), c_c.rearrange("p b t -> p (b t)"),
                          start=True, stop=True).then_inc(s["k_rot_ps"], 1)

            def x1t(g):
                pe.wait_ge(s["x1_ready"], g + 1 + credit["x1_ready"])
                pe.wait_ge(s["kr_ready"], g + 1)
                transposes(2, x1).then_inc(s["x1t_ps"], 1)

            def queries(g):
                pe.wait_ge(s["x1c_ready"], g + 1)
                pe.matmul(ps[2][:, :], w_of("xq"), x1_c.rearrange("p b t -> p (b t)"), start=True, stop=True)
                pe.matmul(ps[3][:, :], w_of("xqr"), x1_c.rearrange("p b t -> p (b t)"),
                          start=True, stop=True).then_inc(s["qx_ps"], 1)

            def scores(g):
                pe.wait_ge(s["qr_ready"], g + 1)
                for b in range(G):
                    last = pe.matmul(bank(3)[:, b, :], kr[:, b, :], qr[:, b, :], start=True, stop=True)
                last.then_inc(s["sc_ps"], 1)

            def attend(g):
                pe.wait_ge(s["sct_ready"], g + 1)
                for b in range(G):
                    last = pe.matmul(bank(2)[:, b, :], sc_t[:, b, :], vh[:, b, :], start=True, stop=True)
                last.then_inc(s["att_ps"], 1)

            def x2t(g):
                pe.wait_ge(s["x2_ready"], g + 1 + credit["x2_ready"])
                transposes(3, x2).then_inc(s["x2t_ps"], 1)

            def route(g):
                pe.wait_ge(s["x2c_ready"], g + 1)
                for b in range(G):
                    last = pe.matmul(ps[3][:, b * E:(b + 1) * E], x2_c[:, b, :], w_of("route"), start=True, stop=True)
                last.then_inc(s["route_ps"], 1)

            def second_biases(g):
                pe.wait_ge(s["score_ready"], g + 1)
                for b in range(G):
                    last = pe.transpose(ps[3][0:E, b * L:(b + 1) * L], score[:, b, :], ident[:, :])
                last.then_inc(s["scoret_ps"], 1)
                pe.wait_ge(s["scoret_ready"], g + 1)
                for b in range(G):
                    last = pe.matmul(bank(3)[:, b, :], sct[:, b * L:(b + 1) * L], b2_sb[:, :], start=True, stop=True)
                last.then_inc(s["binit_ps"], 1)

            def hidden(g, e):
                for half in range(2):
                    pe.wait_ge(s["hid_ready"], g * 2 * E + 2 * e + half - 1 + credit["hid_ready"])
                    pe.matmul(ps[4 + half][:, :], w1_sb[:, e, half * 128:half * 128 + 128],
                              x2_c.rearrange("p b t -> p (b t)"), start=True, stop=True).then_inc(s["hid_ps"], 1)

            def result(g, e):
                pe.wait_ge(s["hid_ready"], g * 2 * E + 2 * e + 2 + credit["hid_ready"])
                pe.wait_ge(s["y_added"], g * E + e - 1 + credit["y_added"])
                for b in range(G):
                    for half in range(2):
                        last = pe.matmul(bank(6 + e % 2)[:, b, :], hid[:, e % 2, half, b * L:(b + 1) * L],
                                         w2_sb[:, e, half, :], start=(half == 0), stop=(half == 1))
                last.then_inc(s["y_ps"], 1)

            pe.wait_ge(inverse_in, 16 * NC)
            pe.wait_ge(s["fir_kept"], CHUNKS)
            pe.wait_ge(s["gram_kept"], 2 * H * NG + credit["gram_kept"])

            def solve_block(n, g):
                at = n * NG + g
                rows = slice(CH * n, CH * n + CH)
                if at >= 2:
                    pe.wait_ge(s["u_ready"], at - 1)
                for r in range(GP):
                    last = pe.matmul(ps[6 + at % 2][rows, r * DH:(r + 1) * DH], inv_t[rows, GP * g + r, :],
                                     vb[rows, GP * g + r, :], start=True, stop=True)
                last.then_inc(s["d_ps"], 1)

            def apply_solved(n, g):
                m = (n - 1) * NG + g
                rows = slice(CH * n, CH * n + CH)
                pe.wait_ge(s["u_ready"], m + 1)
                if m >= 2:
                    pe.wait_ge(s["r_ready"], m - 1)
                for r in range(GP):
                    last = pe.matmul(ps[4 + m % 2][rows, r * DH:(r + 1) * DH],
                                     as_t[0:CH * n, GP * g + r, 0, rows], u[0:CH * n, GP * g + r, :],
                                     start=True, stop=True)
                last.then_inc(s["a_ps"], 1)

            for g in range(NG):
                solve_block(0, g)
            for m in range((NC - 1) * NG + 1):
                if m < (NC - 1) * NG:
                    apply_solved(m // NG + 1, m % NG)
                if m:
                    pe.wait_ge(s["r_ready"], m)
                    solve_block((m - 1) // NG + 1, (m - 1) % NG)
            pe.wait_ge(w_late, 16 * LATE_LOADS)
            ct(0)
            xat(0)
            values(0)
            keys(0)
            for g in range(NG + 1):
                if g < NG:
                    pe.wait_ge(s["u_ready"], (NC - 1) * NG + g + 1)
                    if g < 2:
                        pe.wait_ge(s["r_ready"], (NC - 1) * NG)
                    else:
                        pe.wait_ge(s["oc_ready"], g - 1)
                    for r in range(GP):
                        last = pe.matmul(ps[4 + g % 2][r % H * DH:r % H * DH + DH, r // H * L:(r // H + 1) * L],
                                         u[:, GP * g + r, :], as_t[:, GP * g + r, 1, :], start=True, stop=True)
                    last.then_inc(s["o_ps"], 1)
                if g:
                    pe.wait_ge(s["oc_ready"], g)
                    if g < 3:
                        pe.wait_ge(s["u_ready"], NC * NG)
                    else:
                        pe.wait_ge(s["delta_ready"], g - 2)
                    transposes(6 + (g - 1) % 2, o_c[:, g - 1, :, :]).then_inc(s["ot_ps"], 1)
            pe.wait_ge(s["delta_ready"], NG)


            source_gate(0)
            source_logits(0)
            output_gate(0)
            output_z(0)
            ont(0)
            wo(0)
            def step(g, experts_left):
                p, q = g - 1, g - 2
                x1t(p)
                xat(g)
                queries(p)
                source_gate(g)
                if experts_left:
                    result(q, 5)
                source_logits(g)
                if experts_left:
                    hidden(q, 7)
                scores(p)
                if experts_left:
                    result(q, 6)
                attend(p)
                if experts_left:
                    result(q, 7)
                x2t(p)
                route(p)
                hidden(p, 0)
                hidden(p, 1)
                result(p, 0)
                second_biases(p)
                ct(g)
                hidden(p, 2)
                values(g)
                result(p, 1)
                output_gate(g)
                hidden(p, 3)
                keys(g)
                output_z(g)
                result(p, 2)
                hidden(p, 4)
                result(p, 3)
                ont(g)
                hidden(p, 5)
                wo(g)
                result(p, 4)
                hidden(p, 6)

            step(1, False)
            with pe.Fori(2, NG) as g:
                step(g, True)
            p, q = NG - 1, NG - 2
            x1t(p)
            queries(p)
            result(q, 5)
            hidden(q, 7)
            scores(p)
            result(q, 6)
            attend(p)
            result(q, 7)
            x2t(p)
            route(p)
            hidden(p, 0)
            hidden(p, 1)
            result(p, 0)
            second_biases(p)
            for e in range(2, E):
                hidden(p, e)
                result(p, e - 1)
            result(p, E - 1)

        @block.scalar
        def _(act):
            give_credits(act, "act")
            def toeplitz(k):
                source = bass.AP(tensor=taps_long.tensor, offset=k * CW * (2 * L - 1),
                                 ap=[[1, 128], [2 * L - 1, CW], [1, L]])
                act.dma_start(toep[:, k % 2, :, :], source).then_inc(toep_in[k % 2], 16)

            toeplitz(0)
            toeplitz(1)
            act.wait_ge(w_in, 16 * EARLY_LOADS)
            a0 = RB["temp"][0]
            act.activation(temp[:, 0:1], rb[:, a0:a0 + 1], ACT.Abs).then_inc(act_step, 1)
            act.wait_ge(act_step, 1)
            act.activation(temp[:, 1:2], temp[:, 0:1], ACT.Exp, scale=-1.0).then_inc(act_step, 1)
            act.wait_ge(act_step, 2)
            act.activation(temp[:, 2:3], temp[:, 1:2], ACT.Ln, bias=1.0).then_inc(act_step, 1)
            act.activation(static_g[:, :], r_of("static"), ACT.Tanh, scale=0.5).then_inc(act_step, 1)
            act.activation(half_bog2[:, :], r_of("bog2"), ACT.Copy, scale=0.5).then_inc(act_step, 1)
            act.wait_ge(act_step, 5)
            act.sem_inc(s["act_const"], 1)
            act.wait_ge(pool_step, 13)
            with act.Fori(0, NG) as g:
                v = g + 1
                act.wait_ge(s["xt_ps"], v)
                act.wait_ge(s["proj_ready"], G * g + credit["proj_ready"])
                act.activation(xc_pad[:, :, PAD:], bank(0), ACT.Copy).then_inc(s["xc_ready"], 1)
                act.wait_ge(s["vb_ready"], g + credit["vb_ready"])
                act.wait_ge(s["v_kept"], g + credit["v_kept"])
                act.wait_ge(s["q_ps"], g + credit["q_ps"])
                for b in range(G):
                    act.wait_ge(s["proj_ready"], g * G + b + 1 + credit["proj_ready"])
                    pr = ps[1 + b % 2]
                    act.activation(qkv_g[:, b, :], pr[:, 0:NQKV], ACT.Silu).then_inc(s["silu_ready"], 1)
                    act.activation(graw[:, b, :], pr[:, NQKV:NQKV + 2 * H], ACT.Copy).then_inc(s["proj_free"], 1)
                act.wait_ge(s["silu_ready"], v * G)
                act.activation(sq_g[:, 0:2 * G, :].rearrange("p (b k) c -> p b (k c)", b=G), qkv_g[:, :, 0:2 * D],
                               ACT.Square).then_inc(s["sq_ready"], 1)
                act.wait_ge(s["zsum_ready"], v)
                act.activation(gtmp[:, :, :], graw[:, :, :], ACT.Tanh, scale=0.5).then_inc(s["tanh_ready"], 1)
                act.wait_ge(s["q_ps"], v + credit["q_ps"])
                act.wait_ge(s["gram_ps"], g * 2 * H + credit["gram_ps"])
                act.activation(kq_c[:, :, 1, :], bank(0), ACT.Copy).then_inc(s["q_c"], 1)
                act.wait_ge(s["vrev_ps"], v)
                settle(act, "act")
                act.activation(src[:, bass.ds(g * G, G), 2, :], bank(3), ACT.Copy).then_inc(s["vrev_kept"], 1)
                act.wait_ge(s["kh_ps"], v + credit["kh_ps"])
                for h in range(H):
                    rows = slice(DH * h, DH * h + DH)
                    last = act.activation(kh_c[rows, h, :, :], ps[3][rows, :].rearrange("p (b t) -> p b t", b=G),
                                          ACT.Copy)
                last.then_inc(s["kh_cready"], 1)
                act.wait_ge(s["kb_ps"], v + credit["kb_ps"])
                act.activation(kq_c[:, :, 0, :], bank(0), ACT.Copy).then_inc(s["kb_c"], 1)
            def x_columns(g):
                act.wait_ge(s["xat_ps"], g + 1)
                act.wait_ge(s["z_ps"], g + credit["z_ps"])
                act.activation(xa_c, bank(0), ACT.Copy).then_inc(s["xac_ready"], 1)

            def source_gate(g):
                act.wait_ge(s["st_ps"], g + 1 + credit["st_ps"])
                act.activation(st_c, ps[0][0:32, :], ACT.Copy).then_inc(s["stc_ready"], 1)
                act.wait_ge(s["h1_ps"], g + 1)
                act.activation(h1, ps[1][:, :], ACT.Gelu, bias=c_of("bg1")).then_inc(s["h1_ready"], 1)

            def source_exp(g):
                act.wait_ge(s["lmax_ready"], g + 1)
                act.activation(pe4, lg, ACT.Exp).then_inc(s["exp_ready"], 1)

            def square_mixture(g):
                act.wait_ge(s["o_ready"], g + 1)
                act.activation(sq_g[:, 0:G, :], o_g, ACT.Square).then_inc(s["osq_ready"], 1)

            def output_gate(g):
                act.wait_ge(s["st2_ps"], g + 1 + credit["st2_ps"])
                act.activation(st2_c, ps[0][0:32, :], ACT.Copy).then_inc(s["st2c_ready"], 1)
                act.wait_ge(s["h2_ps"], g + 1)
                act.activation(h2, ps[1][0:64, :], ACT.Gelu, bias=cb[0:64, CB["bog1"][0]:CB["bog1"][1]]
                               ).then_inc(s["h2_ready"], 1)

            def output_tanh(g):
                act.wait_ge(s["z_ps"], g + 1 + credit["z_ps"])
                act.activation(og, ps[0][:, 0:G], ACT.Tanh, scale=0.5, bias=half_bog2[:, :]).then_inc(s["og_tanh"], 1)

            def on_columns(g):
                act.wait_ge(s["ont_ps"], g + 1)
                act.activation(on_c, bank(0), ACT.Copy).then_inc(s["onc_ready"], 1)

            def ctx_columns(g):
                act.wait_ge(s["ct_ps"], g + 1)
                act.activation(c_c, bank(2), ACT.Copy).then_inc(s["cc_ready"], 1)

            def keep_values(g):
                act.wait_ge(s["vh_ps"], g + 1)
                act.activation(vh, bank(2), ACT.Copy).then_inc(s["vh_ready"], 1)

            def x1_columns(g):
                act.wait_ge(s["x1t_ps"], g + 1)
                act.activation(x1_c, bank(2), ACT.Copy).then_inc(s["x1c_ready"], 1)

            def x2_columns(g):
                act.wait_ge(s["x2t_ps"], g + 1)
                act.activation(x2_c, bank(3), ACT.Copy).then_inc(s["x2c_ready"], 1)

            def route_exp(g):
                act.wait_ge(s["rmax_ready"], g + 1)
                act.activation(score, ex, ACT.Exp).then_inc(s["rexp_ready"], 1)

            def score_columns(g):
                act.wait_ge(s["scoret_ps"], g + 1)
                act.activation(sct, ps[3][0:E, :], ACT.Copy).then_inc(s["scoret_ready"], 1)

            def hidden(g, e):
                for half in range(2):
                    act.wait_ge(s["hid_ps"], g * 2 * E + 2 * e + half + 1)
                    if half == 0:
                        act.wait_ge(s["y_ps"], g * E + e - 1 + credit["y_ps"])
                    act.activation(hid[:, e % 2, half, :], ps[4 + half][:, :], ACT.Relu,
                                   bias=c_of("b1", 2 * e + half)).then_inc(s["hid_ready"], 1)

            act.wait_ge(s["v_kept"], NG + credit["v_kept"])
            act.wait_ge(s["k_ready"], NG)
            act.activation(sq_g[:, :, :], src[:, :, 3, :], ACT.Square).then_inc(s["ssq_ready"], 1)
            for g in range(NG + 1):
                if g < NG:
                    act.wait_ge(s["vt_ps"], g + 1)
                    if g >= 2:
                        act.wait_ge(s["short_ps"], g - 1)
                    act.activation(v_columns[g % 2][:, :, PAD:], bank(g % 2), ACT.Copy).then_inc(s["vc_ready"], 1)
                if g:
                    act.wait_ge(s["short_ps"], g)
                    act.activation(src[:, g * G - G:g * G, 0, :], bank(2 + (g - 1) % 2), ACT.Copy
                                   ).then_inc(s["short_ready"], 1)
            act.wait_ge(s["short_ready"], NG)
            act.wait_ge(s["sums_ready"], 1)
            act.activation(sq_g[:, :, :], src[:, :, 0, :], ACT.Square).then_inc(s["ssq_ready"], 1)
            for k in range(CHUNKS + 1):
                if k < CHUNKS:
                    act.wait_ge(s["fir_ps"], k + 1)
                    if k + 2 < CHUNKS:
                        toeplitz(k + 2)
                    if k >= 2:
                        act.wait_ge(s["firt_ps"], k - 1)
                    act.activation(fir_c[:, k % 2, :, :], bank(k % 2), ACT.Copy).then_inc(s["fir_c"], 1)
                if k:
                    act.wait_ge(s["firt_ps"], k)
                    act.activation(src[:, :, 1, (k - 1) * CW:k * CW].rearrange("p b c -> p c b"),
                                   bank(2 + (k - 1) % 2, CW)[:, :, 0:B], ACT.Copy).then_inc(s["fir_kept"], 1)
            for n in range(NC):
                rows = slice(CH * n, CH * n + CH)
                for g in range(NG):
                    at = n * NG + g
                    act.wait_ge(s["d_ps"], at + 1)
                    act.activation(u[rows, GP * g:GP * g + GP, :],
                                   ps[6 + at % 2][rows, :].rearrange("p (r d) -> p r d", r=GP), ACT.Copy
                                   ).then_inc(s["u_ready"], 1)
            act.wait_ge(s["fir_kept"], CHUNKS)
            act.wait_ge(s["sums_ready"], 2)
            act.activation(sq_g[:, :, :], src[:, :, 1, :], ACT.Square).then_inc(s["ssq_ready"], 1)
            ctx_columns(0)
            x_columns(0)
            keep_values(0)
            act.wait_ge(s["sums_ready"], 3)
            for g in range(NG + 1):
                if g < NG:
                    act.wait_ge(s["o_ps"], g + 1)
                    act.activation(o_c[:, g, :, :], bank(4 + g % 2), ACT.Copy).then_inc(s["oc_ready"], 1)
                if not g:
                    continue
                act.wait_ge(s["delta_ready"], g)
                rows = slice(g * G - G, g * G)
                act.activation(sq_g[:, rows, :], src[:, rows, 2, :], ACT.Square).then_inc(s["ssq_ready"], 1)
            source_gate(0)
            source_exp(0)
            square_mixture(0)
            output_gate(0)
            output_tanh(0)
            on_columns(0)
            def step(g, experts_left):
                p, q = g - 1, g - 2
                x1_columns(p)
                x_columns(g)
                source_gate(g)
                if experts_left:
                    hidden(q, 7)
                source_exp(g)
                x2_columns(p)
                route_exp(p)
                square_mixture(g)
                hidden(p, 0)
                hidden(p, 1)
                score_columns(p)
                ctx_columns(g)
                hidden(p, 2)
                keep_values(g)
                output_gate(g)
                hidden(p, 3)
                output_tanh(g)
                hidden(p, 4)
                on_columns(g)
                hidden(p, 5)
                hidden(p, 6)

            step(1, False)
            with act.Fori(2, NG) as g:
                step(g, True)
            p, q = NG - 1, NG - 2
            x1_columns(p)
            hidden(q, 7)
            x2_columns(p)
            route_exp(p)
            hidden(p, 0)
            hidden(p, 1)
            score_columns(p)
            for e in range(2, E):
                hidden(p, e)

        @block.vector
        def _(dve):
            give_credits(dve, "dve")
            base = [0, 0]

            def own(ins):
                base[1] += 1
                ins.then_inc(dve_step, 1)
                dve.wait_ge(dve_step, base[0] + base[1])

            def rsqrt(y, a, n):
                t = nt1[:, 0:n]
                own(dve.tensor_scalar(y.bitcast(I32), a.bitcast(I32), -0.5, RSQRT_GUESS, ALU.mult, ALU.add))
                for i in range(3):
                    own(dve.tensor_tensor(out=t, in0=y, in1=y, op=ALU.mult))
                    own(dve.scalar_tensor_tensor(out=t, in0=t, scalar=-0.5, in1=a, op0=ALU.mult, op1=ALU.mult))
                    own(dve.scalar_tensor_tensor(out=y, in0=t, scalar=1.5, in1=y, op0=ALU.add, op1=ALU.mult))

            def wide(a, m):
                return a.unsqueeze(len(a.shape)).broadcast_to(list(a.shape) + [m])

            def mid(a, m):
                return a.unsqueeze(1).broadcast_to([a.shape[0], m, a.shape[1]])

            dve.wait_ge(w_in, 16 * EARLY_LOADS)
            dve.wait_ge(s["ident_ready"], 1)
            dve.tensor_tensor(out=wtap[:, :, :], in0=mid(w_of("qkv"), TAPS),
                              in1=wtap[:, :, :], op=ALU.mult)
            for t in range(SHORT):
                dve.tensor_scalar(diag_short[:, t, :], ident[:, :], c_of("short", t), None, ALU.mult)
            dve.tensor_scalar(wo_n[:, :], w_of("o"), c_of("norm"), None, ALU.mult)
            dve.wait_ge(s["act_const"], 1)
            own(dve.tensor_scalar(static_g[:, :], static_g[:, :], 0.5, 0.5, ALU.mult, ALU.add))
            a0 = RB["temp"][0]
            own(dve.scalar_tensor_tensor(out=temp[:, 3:4], in0=rb[:, a0:a0 + 1], scalar=0.0, in1=temp[:, 2:3],
                                         op0=ALU.max, op1=ALU.add))
            own(dve.reciprocal(temp[:, 4:5], temp[:, 3:4]))
            own(dve.tensor_scalar(bg2_t[:, :, :], mid(r_of("bg2"), G), temp[:, 4:5], None, ALU.mult))
            dve.sem_inc(s["dve_const"], 1)
            dve.wait_ge(s["pool_const"], 5)

            PROJ_STEPS = 13
            start = base[1]
            with dve.Fori(0, NG) as g:
                base[0], base[1] = start + g * PROJ_STEPS, 0
                seqs = bass.ds(g * G, G)
                dve.wait_ge(s["proj_free"], G * (g + 1) + credit["proj_free"])
                dve.tensor_tensor(out=gtmp[:, :, :], in0=graw[:, :, :], in1=mid(r_of("gate_bias"), G),
                                  op=ALU.add).then_inc(s["zsum_ready"], 1)
                dve.wait_ge(s["sq_ready"], g + 1)
                own(dve.tensor_reduce(out=ss_g[:, :, :].rearrange("p b h -> p (b h)"),
                                      in_=sq_g[:, 0:2 * G, :].rearrange("p k (h d) -> p (k h) d", h=H),
                                      axis=AX.X, op=ALU.add))
                own(dve.tensor_scalar(ss_g[:, :, :], ss_g[:, :, :], 1e-6, None, ALU.add))
                rsqrt(rn_g[:, :, :].rearrange("p b h -> p (b h)"), ss_g[:, :, :].rearrange("p b h -> p (b h)"),
                      G * 2 * H)
                dve.wait_ge(s["kh_ps"], g + credit["kh_ps"])
                dve.tensor_tensor(out=kh_g[:, :, :].rearrange("p b (h d) -> p b h d", h=H),
                                  in0=qkv_g[:, :, D:2 * D].rearrange("p b (h d) -> p b h d", h=H),
                                  in1=wide(rn_g[:, :, H:2 * H], DH), op=ALU.mult).then_inc(s["k_ready"], 1)
                dve.wait_ge(s["tanh_ready"], g + 1)
                own(dve.tensor_scalar(gates[:, seqs, :], gtmp[:, :, :], 0.5, 0.5, ALU.mult, ALU.add))
                dve.wait_ge(s["k_ready"], g + 1)
                dve.wait_ge(s["kb_ps"], g + credit["kb_ps"])
                dve.tensor_tensor(out=kb_g[:, :, :].rearrange("p b (h d) -> p b h d", h=H),
                                  in0=kh_g[:, :, :].rearrange("p b (h d) -> p b h d", h=H),
                                  in1=wide(gates[:, seqs, 0:H], DH), op=ALU.mult).then_inc(s["kb_ready"], 1)
                dve.tensor_copy(rq[:, seqs, :], rn_g[:, :, 0:H])
                dve.tensor_tensor(out=vb[:, :, :].rearrange("p (b h) d -> p b h d", h=H)[:, seqs, :, :],
                                  in0=qkv_g[:, :, 2 * D:3 * D].rearrange("p b (h d) -> p b h d", h=H),
                                  in1=wide(gates[:, seqs, 0:H], DH), op=ALU.mult).then_inc(s["vb_ready"], 1)
                rows_of = as_t[:, :, :, :].rearrange("p (b h) k t -> p b h (k t)", h=H)
                for r in range(2):
                    for h in range(H):
                        dve.wait_ge(s["gram_ps"], g * 2 * H + r * H + h + 1 + credit["gram_ps"])
                        dve.tensor_tensor(out=rows_of[:, bass.ds(g * G + 2 * r, 2), h, :], in0=bank(4 + h, 2),
                                          in1=mid(masks[:, :, :].rearrange("p k t -> p (k t)"), 2),
                                          op=ALU.mult).then_inc(s["gram_kept"], 1)
            assert base[1] == PROJ_STEPS, base[1]
            base[0], base[1] = 0, start + NG * PROJ_STEPS

            def layernorm(y, dst, done):
                for b in range(G):
                    last = dve.bn_stats(out=bn6[:, b, :], in_=y[:, b, :])
                own(last)
                settle(dve, "dve")
                for b in range(G):
                    last = dve.bn_aggr(out=mv[:, b, :], in_=bn6[:, b, :])
                own(last)
                own(dve.tensor_scalar(sm1[:, 0:G], mv[:, :, 1], EPS, None, ALU.add))
                rsqrt(sm2[:, 0:G], sm1[:, 0:G], G)
                for b in range(G):
                    last = dve.tensor_scalar(dst[:, b, :], y[:, b, :], mv[:, b, 0:1], sm2[:, b:b + 1],
                                             ALU.subtract, ALU.mult)
                last.then_inc(s[done], 1)

            def head_sums(xs, squares, to, n):
                settle(dve, "dve")
                own(dve.tensor_reduce(out=sumx[:, 0:n * H], in_=xs.rearrange("p n (h d) -> p (n h) d", h=H),
                                      axis=AX.X, op=ALU.add))
                own(dve.tensor_reduce(out=sumq[:, 0:n * H], in_=squares.rearrange("p n (h d) -> p (n h) d", h=H),
                                      axis=AX.X, op=ALU.add))
                settle(dve, "dve")
                dve.tensor_reduce(out=to(2), in_=xs, axis=AX.X, op=ALU.add, apply_absolute_value=True)
                dve.tensor_reduce(out=to(0), in_=sumx[:, 0:n * H].rearrange("p (n h) -> p n h", h=H),
                                  axis=AX.X, op=ALU.add)

            def head_moments(to, n):
                own(dve.tensor_tensor(out=sm1[:, 0:n * H], in0=sumx[:, 0:n * H], in1=sumx[:, 0:n * H], op=ALU.mult))
                own(dve.scalar_tensor_tensor(out=sm1[:, 0:n * H], in0=sumq[:, 0:n * H], scalar=float(DH),
                                             in1=sm1[:, 0:n * H], op0=ALU.mult, op1=ALU.subtract))
                dve.tensor_reduce(out=to(1), in_=sm1[:, 0:n * H].rearrange("p (n h) -> p n h", h=H),
                                  axis=AX.X, op=ALU.add)
                own(dve.tensor_scalar(sm2[:, 0:n * H], sumq[:, 0:n * H], 1e-30, None, ALU.max))
                rsqrt(nt2[:, 0:n * H], sm2[:, 0:n * H], n * H)
                own(dve.tensor_tensor(out=sm2[:, 0:n * H], in0=sumq[:, 0:n * H], in1=nt2[:, 0:n * H], op=ALU.mult))
                own(dve.tensor_reduce(out=to(3), in_=sm2[:, 0:n * H].rearrange("p (n h) -> p n h", h=H),
                                      axis=AX.X, op=ALU.add))

            def by_head(a):
                return a.rearrange("p b (h d) -> p b h d", h=H)

            def source_sums(k, a, b, squares_ready):
                dve.wait_ge(s["ssq_ready"], squares_ready)
                rows = src[:, a:b, k, :]
                own(dve.tensor_reduce(out=sumx[:, a * H:b * H], in_=rows.rearrange("p n (h d) -> p n h d", h=H),
                                      axis=AX.X, op=ALU.add))
                own(dve.tensor_reduce(out=sumq[:, a * H:b * H],
                                      in_=sq_g[:, a:b, :].rearrange("p n (h d) -> p (n h) d", h=H),
                                      axis=AX.X, op=ALU.add))
                dve.tensor_reduce(out=st_all[:, a:b, 4 * k + 2], in_=rows, axis=AX.X, op=ALU.add,
                                  apply_absolute_value=True)
                dve.tensor_reduce(out=st_all[:, a:b, 4 * k],
                                  in_=sumx[:, a * H:b * H].rearrange("p (n h) -> p n h", h=H),
                                  axis=AX.X, op=ALU.add)

            def source_moments(k):
                head_moments(lambda i: st_all[:, :, 4 * k + i], B)
                own(dve.tensor_tensor(out=st_all[:, :, 4 * k:4 * k + 4], in0=st_all[:, :, 4 * k:4 * k + 4],
                                      in1=mid(stat_scale[:, 0:4], B), op=ALU.mult))
                dve.sem_inc(s["stats_ready"], 1)

            def source_logits(g):
                dve.wait_ge(s["logit_ps"], g + 1)
                own(dve.scalar_tensor_tensor(out=lg, in0=ps[0][:, 0:16].rearrange("p (b k) -> p b k", b=G),
                                             scalar=temp[:, 4:5], in1=bg2_t[:, :, :], op0=ALU.mult, op1=ALU.add))
                own(dve.tensor_reduce(out=red, in_=lg, axis=AX.X, op=ALU.max))
                dve.tensor_tensor(out=lg, in0=lg, in1=wide(red, 4), op=ALU.subtract).then_inc(s["lmax_ready"], 1)

            def source_weights(g):
                seqs = bass.ds(g * G, G)
                dve.wait_ge(s["exp_ready"], g + 1)
                own(dve.tensor_reduce(out=red, in_=pe4, axis=AX.X, op=ALU.add))
                own(dve.reciprocal(red, red))
                own(dve.tensor_tensor(out=pw, in0=pe4, in1=wide(red, 4), op=ALU.mult))
                own(dve.tensor_scalar(pw, pw, FLOOR, None, ALU.max))
                own(dve.tensor_reduce(out=red, in_=pw, axis=AX.X, op=ALU.add))
                own(dve.reciprocal(red, red))
                own(dve.tensor_tensor(out=pw, in0=pw, in1=wide(red, 4), op=ALU.mult))
                own(dve.tensor_tensor(out=w0, in0=gates[:, seqs, H:2 * H], in1=mid(static_g[:, :], G), op=ALU.mult))
                own(dve.tensor_tensor(out=w0, in0=w0, in1=wide(pw[:, :, 0], H), op=ALU.add))

            def mixture(g):
                seqs = bass.ds(g * G, G)
                own(dve.tensor_tensor(out=by_head(o_g), in0=by_head(src[:, seqs, 0, :]), in1=wide(w0, DH),
                                      op=ALU.mult))
                for k in range(1, 4):
                    for b in range(G):
                        last = dve.scalar_tensor_tensor(
                            out=o_g[:, b, :], in0=src[:, bass.ds(g * G + b, 1), k, :].rearrange("p a c -> p (a c)"),
                            scalar=pw[:, b, k:k + 1], in1=o_g[:, b, :], op0=ALU.mult, op1=ALU.add)
                    if k < 3:
                        own(last)
                    else:
                        last.then_inc(s["o_ready"], 1)

            def mixture_stats(g):
                dve.wait_ge(s["osq_ready"], g + 1)
                dve.wait_ge(s["o_ready"], g + 1)
                dve.wait_ge(s["st2_ps"], g + credit["st2_ps"])
                head_sums(o_g, sq_g[:, 0:G, :], lambda k: st2[:, :, k], G)
                head_moments(lambda k: st2[:, :, k], G)
                dve.tensor_tensor(out=st2[:, :, 0:4], in0=st2[:, :, 0:4], in1=mid(stat_scale[:, 0:4], G),
                                  op=ALU.mult).then_inc(s["ostats_ready"], 1)

            def gated(g):
                dve.wait_ge(s["og_tanh"], g + 1)
                own(dve.tensor_scalar(og, og, 0.5, 0.5, ALU.mult, ALU.add))
                own(dve.tensor_tensor(out=sm1[:, 0:G], in0=og, in1=og, op=ALU.mult))
                own(dve.tensor_tensor(out=ogr, in0=sumq[:, 0:G * H].rearrange("p (b h) -> p b h", b=G),
                                      in1=wide(sm1[:, 0:G], H), op=ALU.mult))
                own(dve.tensor_scalar(ogr, ogr, 1.0 / DH, EPS, ALU.mult, ALU.add))
                rsqrt(sm2[:, 0:G * H], ogr.rearrange("p b h -> p (b h)"), G * H)
                own(dve.tensor_tensor(out=ogr, in0=sm2[:, 0:G * H].rearrange("p (b h) -> p b h", b=G),
                                      in1=wide(og, H), op=ALU.mult))
                dve.tensor_tensor(out=by_head(on_g), in0=by_head(o_g), in1=wide(ogr, DH), op=ALU.mult
                                  ).then_inc(s["on_ready"], 1)

            def x1_norm(g):
                dve.wait_ge(s["wo_ps"], g + 1)
                dve.wait_ge(xa_in, 16 * (g + 1))
                own(dve.tensor_tensor(out=y_g, in0=bank(1), in1=xa, op=ALU.add))
                layernorm(y_g, x1, "x1_ready")

            def rotate_keys(g):
                dve.wait_ge(s["k_rot_ps"], g + 1)
                own(dve.tensor_tensor(out=kt, in0=bank(3), in1=mid(tab[:, 3, :], G), op=ALU.mult))
                own(dve.tensor_tensor(out=kr, in0=bank(2), in1=mid(tab[:, 2, :], G), op=ALU.mult))
                dve.tensor_tensor(out=kr, in0=kr, in1=kt, op=ALU.add).then_inc(s["kr_ready"], 1)

            def rotate_queries(g):
                dve.wait_ge(s["qx_ps"], g + 1)
                own(dve.tensor_tensor(out=qt, in0=bank(3), in1=mid(tab[:, 1, :], G), op=ALU.mult))
                own(dve.tensor_tensor(out=qr, in0=bank(2), in1=mid(tab[:, 0, :], G), op=ALU.mult))
                dve.tensor_tensor(out=qr, in0=qr, in1=qt, op=ALU.add).then_inc(s["qr_ready"], 1)

            def decay_scores(g):
                dve.wait_ge(s["sc_ps"], g + 1)
                dve.tensor_tensor(out=sc_t, in0=bank(3), in1=mid(decay_sb[:, :], G), op=ALU.mult
                                  ).then_inc(s["sct_ready"], 1)

            def x2_norm(g):
                dve.wait_ge(s["att_ps"], g + 1)
                dve.wait_ge(s["x1_ready"], g + 1 + credit["x1_ready"])
                own(dve.tensor_tensor(out=y_g, in0=bank(2), in1=x1, op=ALU.add))
                layernorm(y_g, x2, "x2_ready")

            def route_max(g):
                dve.wait_ge(s["route_ps"], g + 1)
                logits = ps[3][:, 0:G * E].rearrange("p (b e) -> p b e", b=G)
                own(dve.tensor_reduce(out=red, in_=logits, axis=AX.X, op=ALU.max))
                dve.tensor_tensor(out=ex, in0=logits, in1=wide(red, E), op=ALU.subtract
                                  ).then_inc(s["rmax_ready"], 1)

            def choose(g):
                dve.wait_ge(s["rexp_ready"], g + 1)
                for k, op in enumerate((ALU.is_ge, ALU.is_gt)):
                    own(dve.tensor_tensor(out=cmp_[:, :, :, k, :], in0=score.unsqueeze(2).broadcast_to([128, G, E, E]),
                                          in1=wide(score, E), op=op))
                for k in range(2):
                    own(dve.tensor_tensor(out=cmp_[:, :, :, k, :], in0=cmp_[:, :, :, k, :],
                                          in1=tie[:, k, :, :].unsqueeze(1).broadcast_to([128, G, E, E]), op=ALU.mult))
                own(dve.tensor_reduce(out=rank, in_=cmp_.rearrange("p b i k j -> p (b i) (k j)"), axis=AX.X,
                                      op=ALU.add))
                own(dve.scalar_tensor_tensor(out=ex, in0=rank, scalar=2.0, in1=score, op0=ALU.is_lt, op1=ALU.mult))
                own(dve.tensor_reduce(out=red, in_=ex, axis=AX.X, op=ALU.add))
                own(dve.reciprocal(red, red))
                dve.tensor_tensor(out=score, in0=ex, in1=wide(red, E), op=ALU.mult).then_inc(s["score_ready"], 1)

            def start_sum(g):
                dve.wait_ge(s["x2_ready"], g + 1 + credit["x2_ready"])
                dve.wait_ge(s["binit_ps"], g + 1)
                dve.wait_ge(s["fin_ready"], g + credit["fin_ready"])
                own(dve.tensor_tensor(out=acc, in0=bank(3), in1=x2, op=ALU.add))
                dve.sem_inc(s["sum_started"], 1)
                dve.wait_ge(s["score_ready"], g + 1)

            def add(g, e):
                dve.wait_ge(s["y_ps"], g * E + e + 1 + credit["y_ps"])
                for b in range(G):
                    last = dve.scalar_tensor_tensor(out=acc[:, b, :], in0=bank(6 + e % 2)[:, b, :],
                                                    scalar=score[:, b, e:e + 1], in1=acc[:, b, :],
                                                    op0=ALU.mult, op1=ALU.add)
                last.then_inc(s["y_added"], 1)
                dve.wait_ge(s["y_added"], g * E + e + 1 + credit["y_added"])

            def finish(g):
                dve.wait_ge(stored, 16 * (g + 1))
                layernorm(acc, fin, "fin_ready")

            source_sums(3, 0, B, 1)
            dve.sem_inc(s["sums_ready"], 1)
            source_moments(3)

            dve.wait_ge(blocks_in, 16)
            for j in range(CH - 1):
                n = CH - 1 - j
                p = prod[:, 0:2 * (j + 1) * n].rearrange("p (a c i) -> p a c i", a=2, c=j + 1)
                own(dve.tensor_tensor(out=p, in0=blk[:, :, j, j + 1:].unsqueeze(2).broadcast_to([128, 2, j + 1, n]),
                                      in1=wide(inv[:, :, 0:j + 1, j], n), op=ALU.mult))
                own(dve.tensor_tensor(out=inv[:, :, 0:j + 1, j + 1:], in0=inv[:, :, 0:j + 1, j + 1:], in1=p,
                                      op=ALU.subtract))
            dve.sem_inc(s["solved"], 1)
            source_sums(0, 0, B, 2)
            dve.sem_inc(s["sums_ready"], 1)
            source_moments(0)

            for n in range(1, NC):
                rows = slice(CH * n, CH * n + CH)
                for g in range(NG):
                    dve.wait_ge(s["a_ps"], (n - 1) * NG + g + 1)
                    pairs = vb[rows, GP * g:GP * g + GP, :]
                    dve.tensor_tensor(out=pairs, in0=pairs,
                                      in1=ps[4 + ((n - 1) * NG + g) % 2][rows, :].rearrange("p (r d) -> p r d", r=GP),
                                      op=ALU.subtract).then_inc(s["r_ready"], 1)
            source_sums(1, 0, B, 3)
            dve.sem_inc(s["sums_ready"], 1)
            source_moments(1)
            rotate_keys(0)
            dve.wait_ge(s["fir_ps"], CHUNKS)
            for g in range(NG):
                dve.wait_ge(s["ot_ps"], g + 1)
                dve.tensor_tensor(out=src[:, g * G:g * G + G, 2, :].rearrange("p b (h d) -> p b h d", h=H),
                                  in0=ps[6 + g % 2][:, :].rearrange("p (b h d) -> p b h d", b=G, h=H),
                                  in1=wide(rq[:, g * G:g * G + G, :], DH), op=ALU.mult
                                  ).then_inc(s["delta_ready"], 1)
                if g:
                    source_sums(2, g * G - G, g * G, 3 + g)
            source_sums(2, B - G, B, 3 + NG)
            source_moments(2)

            dve.wait_ge(pool_step, 15)
            dve.wait_ge(w_late, 16 * LATE_LOADS)
            source_logits(0)
            source_weights(0)
            mixture(0)
            mixture_stats(0)
            gated(0)
            x1_norm(0)
            def step(g, experts_left):
                p, q = g - 1, g - 2
                if experts_left:
                    add(q, 4)
                rotate_queries(p)
                if experts_left:
                    add(q, 5)
                source_logits(g)
                decay_scores(p)
                source_weights(g)
                if experts_left:
                    add(q, 6)
                x2_norm(p)
                if experts_left:
                    add(q, 7)
                mixture(g)
                route_max(p)
                choose(p)
                mixture_stats(g)
                if experts_left:
                    finish(q)
                start_sum(p)
                add(p, 0)
                add(p, 1)
                rotate_keys(g)
                gated(g)
                add(p, 2)
                add(p, 3)
                x1_norm(g)

            step(1, False)
            MIX_STEPS = 101
            start = base[1]
            with dve.Fori(2, NG) as g:
                base[0], base[1] = start + (g - 2) * MIX_STEPS, 0
                step(g, True)
            assert base[1] == MIX_STEPS, base[1]
            base[0], base[1] = 0, start + (NG - 2) * MIX_STEPS
            p, q = NG - 1, NG - 2
            add(q, 4)
            rotate_queries(p)
            add(q, 5)
            decay_scores(p)
            add(q, 6)
            x2_norm(p)
            add(q, 7)
            finish(q)
            route_max(p)
            choose(p)
            start_sum(p)
            for e in range(E):
                add(p, e)
            finish(p)


def xpos_tables():
    import numpy as np

    half = D // 2
    scale_vec = (np.arange(0, D, 2, dtype=np.float32) + np.float32(0.4 * D)) / np.float32(1.4 * D)
    pos = np.arange(L, dtype=np.float32)
    scale = scale_vec[None, :] ** (pos / np.float32(512.0))[:, None]
    freqs = np.float32(1.0) / np.float32(10000.0) ** (np.arange(half, dtype=np.float32) / np.float32(half))
    angle = (pos[:, None] * freqs[None, :]).astype(np.float64)
    sign = np.tile(np.array([-1.0, 1.0]), half)
    out = []
    for sc in (scale.astype(np.float64), 1.0 / scale.astype(np.float64)):
        out += [np.repeat(np.cos(angle) * sc, 2, axis=1), np.repeat(np.sin(angle) * sc, 2, axis=1) * sign]
    return np.ascontiguousarray(np.stack(out).transpose(2, 0, 1).astype(np.float32))


def decay_table():
    import numpy as np

    diff = np.arange(L)[None, :] - np.arange(L)[:, None]
    return np.where(diff >= 0, 0.96875 ** np.maximum(diff, 0), 0.0).astype(np.float32)


def kernel(**inputs):
    import numpy as np
    import concourse.bacc as bacc
    from concourse.bass_utils import run_bass_kernel_spmd

    a = {k: np.asarray(v) for k, v in inputs.items()}
    w = {k[8:]: v for k, v in a.items() if k.startswith("L0_attn_")}

    swap = np.arange(D) ^ 1
    wbundle = np.concatenate(
        [w["Wq"], w["Wk"], w["Wv"], w["Wb"], w["Wres"], w["Wg1"][:D], w["Wog1"][:D], w["Wg2"], w["Wo"],
         a["L0_xattn_Wq"], a["L0_xattn_Wq"][:, swap], a["L0_xattn_Wk"], a["L0_xattn_Wk"][:, swap],
         a["L0_xattn_Wv"], a["L0_ffn_Wg"]], axis=1)
    taps = np.concatenate([w["wq_conv"], w["wk_conv"], w["wv_conv"]], axis=0).T
    rbundle = np.concatenate([np.zeros(H, np.float32), w["bres"], w["bg2"], w["logit_temp"],
                              w["conv_res_logit"], w["bog2"], taps.reshape(-1)])
    col = [w["bg1"][:, None], np.concatenate([w["bog1"], np.zeros(D - D // 2, np.float32)])[:, None],
           np.tile(w["norm_w"], H)[:, None], w["fir_short"].reshape(D, SHORT),
           a["L0_ffn_b1"].reshape(2 * E, 128).T]
    cbundle = np.concatenate(col, axis=1)
    ws = np.zeros((32, D + D // 2), np.float32)
    ws[:16, :D] = w["Wg1"][D:]
    ws[:8, D:] = w["Wog1"][D:]
    taps_long = np.zeros((D, 2 * L - 1), np.float32)
    taps_long[:, L - 1:L - 1 + LONG] = w["fir_long"].reshape(D, LONG)[:, ::-1]
    arrays = {
        "x": a["x"], "ctx_in": a["ctx_1024"], "wbundle": wbundle, "rbundle": rbundle, "cbundle": cbundle, "ws": ws,
        "wog2": w["Wog2"], "taps_long": taps_long, "w1": a["L0_ffn_W1"], "w2": a["L0_ffn_W2"], "b2": a["L0_ffn_b2"],
        "tables": xpos_tables(), "decay": decay_table(),
    }
    arrays = {k: np.ascontiguousarray(v) for k, v in arrays.items()}
    nc = bacc.Bacc("TRN2", target_bir_lowering=False, num_devices=1)
    args = [nc.dram_tensor(k, v.shape, mybir.dt.from_np(v.dtype), kind="ExternalInput").ap()
            for k, v in arrays.items()]
    args += [nc.dram_tensor(k, (NP, NC, CH, CH), F32, kind="Internal").ap() for k in ("blocks", "inverses")]
    out = nc.dram_tensor("result", (B, L, D), F32, kind="ExternalOutput").ap()
    decoder_kernel(nc, *args, out)
    r = run_bass_kernel_spmd(nc, [arrays], core_ids=[0])
    return r.results[0]["result"]
```

```python
from contextlib import ExitStack

import concourse.bass as bass
from concourse import mybir

F32 = mybir.dt.float32
I32 = mybir.dt.int32
ALU = mybir.AluOpType
ACT = mybir.ActivationFunctionType
AX = mybir.AxisListType

B, L, D = 16, 128, 128
H, DH = 4, 32
G = 4
NG = B // G
N = G * L
NP = B * H
GP = G * H
CH = 32
NC = L // CH
E, HID = 8, 256
NQKV = 3 * D
TAPS = 4
LONG, SHORT = 64, 5
PAD = SHORT - 1
EPS = 1e-5
FLOOR = 0.02
RSQRT_GUESS = float(0x5F3759DF)

WB = {}
_at = 0
for _name, _n in (("qkv", NQKV), ("gates", 2 * H), ("g1", D), ("og1", D // 2), ("g2", 4), ("o", D),
                  ("xq", D), ("xqr", D), ("xk", D), ("xkr", D), ("xv", D), ("route", E)):
    WB[_name] = (_at, _at + _n)
    _at += _n
WB_N = _at
RB = {}
_at = 0
for _name, _n in (("gate_bias", 2 * H), ("bg2", 4), ("temp", 1), ("static", H), ("bog2", 1)):
    RB[_name] = (_at, _at + _n)
    _at += _n
RB_N = _at
CB = {}
_at = 0
for _name, _n in (("bg1", 1), ("bog1", 1), ("norm", 1), ("short", SHORT), ("b1", 2 * E)):
    CB[_name] = (_at, _at + _n)
    _at += _n
CB_N = _at


def decoder_kernel(nc, x, ctx_in, wbundle, rbundle, cbundle, ws, wog2, taps_long, w1, w2, b2, tables, decay,
                   blocks_dram, inverse_dram, out):
    stack = ExitStack()
    with stack:
        def sb(name, shape, dt=F32):
            return stack.enter_context(nc.sbuf_tensor(name, shape, dt))

        def sem(name):
            return stack.enter_context(nc.semaphore(name))

        wb = sb("wb", [128, WB_N])
        rb = sb("rb", [128, RB_N])
        cb = sb("cb", [128, CB_N])
        ws_sb = sb("ws_sb", [32, D + D // 2])
        wog2_sb = sb("wog2_sb", [D // 2, 1])
        w1_sb = sb("w1_sb", [128, E, HID])
        w2_sb = sb("w2_sb", [128, E, 2, D])
        b2_sb = sb("b2_sb", [E, D])
        tab = sb("tab", [128, 4, L])
        decay_sb = sb("decay_sb", [128, L])
        ident = sb("ident", [128, 128])
        flip = sb("flip", [128, 128])
        masks = sb("masks", [128, 2, L])
        tie = sb("tie", [128, 2, E, E])
        stat_scale = sb("stat_scale", [128, 16])
        wtap = sb("wtap", [128, TAPS, NQKV])
        diag_short = sb("diag_short", [128, SHORT, 128])
        wo_n = sb("wo_n", [128, D])
        temp = sb("temp", [128, 8])
        bg2_t = sb("bg2_t", [128, G, 4])
        static_g = sb("static_g", [128, H])
        half_bog2 = sb("half_bog2", [128, 1])

        def w_of(name):
            a, b = WB[name]
            return wb[:, a:b]

        def r_of(name):
            a, b = RB[name]
            return rb[:, a:b]

        def c_of(name, i=0):
            a, _ = CB[name]
            return cb[:, a + i:a + i + 1]

        src = sb("src", [128, B, 4, D])
        vb = sb("vb", [128, NP, DH])
        as_t = sb("as_t", [128, NP, 2, L])
        early = sb("early", [128, 3 * NP * CH])
        inv_t = early[:, 0:NP * CH].rearrange("p (r i) -> p r i", r=NP)
        u = early[:, NP * CH:2 * NP * CH].rearrange("p (r i) -> p r i", r=NP)
        fir_c = early[:, NP * CH:NP * CH + 2 * N].rearrange("p (k b t) -> p k b t", k=2, b=4)
        blk = early[:, 2 * NP * CH:3 * NP * CH].rearrange("p (a j i) -> p a j i", a=2, j=CH)
        rq = sb("rq", [128, B, H])
        gates = sb("gates", [128, B, 2 * H])
        inv = sb("inv", [128, 2, CH, CH])
        o_c = inv[:, :, :, :].rearrange("p a j i -> p (a j i)").rearrange("p (g b t) -> p g b t", g=NG, b=G)
        prod_pool = wtap[:, :, :].rearrange("p t n -> p (t n)")[:, 0:2 * 128]
        prod = sb("prod", [128, 2 * 272])
        toep = sb("toep", [128, 2, 16, L])

        qkv_g = early[:, 0:G * NQKV].rearrange("p (b c) -> p b c", b=G)
        kh_g = early[:, G * NQKV:G * NQKV + N].rearrange("p (b c) -> p b c", b=G)
        kh_c = early[:, 4 * N:8 * N].rearrange("p (h b t) -> p h b t", h=H, b=G)
        x_g = early[:, 8 * N:9 * N].rearrange("p (b c) -> p b c", b=G)
        kb_g = early[:, 9 * N:10 * N].rearrange("p (b c) -> p b c", b=G)
        kq_c = early[:, 10 * N:12 * N].rearrange("p (b k t) -> p b k t", b=G, k=2)
        xc_pad = sb("xc_pad", [128, G, PAD + L])
        vc_pad = sb("vc_pad", [128, G, PAD + L])
        v_columns = (xc_pad, vc_pad)
        graw = sb("graw", [128, G, 2 * H])
        gtmp = sb("gtmp", [128, G, 2 * H])
        sq_g = sb("sq_g", [128, G * 4, D])
        ss_g = sb("ss_g", [128, G, 2 * H])
        rn_g = sb("rn_g", [128, G, 2 * H])
        nt1 = sb("nt1", [128, 64])
        nt2 = sb("nt2", [128, 64])
        sumx = sb("sumx", [128, NP])
        sumq = sb("sumq", [128, NP])
        sm1 = sb("sm1", [128, NP])
        sm2 = sb("sm2", [128, NP])
        st_all = sb("st_all", [128, B, 16])

        old = [[toep[:, :, :, :].rearrange("p a b c -> p (a b c)"), 0, 2 * 16 * L],
               [as_t[:, :, :, :].rearrange("p a b c -> p (a b c)"), 0, NP * 2 * L],
               [early[:, :], 0, 3 * NP * CH]]

        def over(n, parts=128):
            for region in old:
                memory, a, size = region
                if a + n <= size:
                    region[1] += n
                    return memory[0:parts, a:a + n]
            raise AssertionError("no room")

        def over3(b, c, parts=128):
            return over(b * c, parts).rearrange("p (b c) -> p b c", b=b)

        xa = over3(G, D)
        xt = over3(G, D)
        xa_c = over3(G, L)
        c_g = over3(G, D)
        c_c = over3(G, L)
        vh = over3(G, D)
        kr = over3(G, L)
        kt = over3(G, L)
        assert [region[1] > 0 for region in old] == [True, False, False]
        old[0][1] = 2 * 16 * L
        st = over3(G, 32)
        st2 = over3(G, 32)
        st_c = over(N, 32)
        st2_c = over(N, 32)
        h1 = over(N)
        h2 = over(N, 64)
        lg = over3(G, 4)
        pe4 = over3(G, 4)
        pw = over3(G, 4)
        red = over(G)
        w0 = over3(G, H)
        og = over(G)
        ogr = over3(G, H)
        o_g = over3(G, D)
        on_g = over3(G, D)
        on_c = over3(G, L)
        y_g = over3(G, D)
        bn6 = over3(G, 6)
        mv = over3(G, 2)
        x1 = over3(G, D)
        x1_c = over3(G, L)
        qr = over3(G, L)
        qt = over3(G, L)
        sc_t = over3(G, L)
        x2 = over3(G, D)
        x2_c = over3(G, L)
        ex = over3(G, E)
        cmp_ = over(G * E * 2 * E).rearrange("p (b i k j) -> p b i k j", b=G, i=E, k=2)
        rank = over3(G, E)
        score = over3(G, E)
        sct = over(N, E)
        hid = over(2 * 2 * N).rearrange("p (s k n) -> p s k n", s=2, k=2)
        acc = over3(G, D)
        fin = over3(G, D)

        ps = [stack.enter_context(nc.psum_tensor(f"bank{i}", [128, 512], F32)) for i in range(8)]

        def bank(i, b=G):
            return ps[i][:, :].rearrange("p (b c) -> p b c", b=b)

        w_in = sem("w_in")
        w_late = sem("w_late")
        x_in = sem("x_in")
        toep_in = [sem("toep_in0"), sem("toep_in1")]
        blocks_out = sem("blocks_out")
        blocks_in = sem("blocks_in")
        inverse_out = [sem("inverse_out0"), sem("inverse_out1")]
        inverse_in = [sem("inverse_in0"), sem("inverse_in1")]
        xa_in = sem("xa_in")
        xt_in = sem("xt_in")
        ctx_loaded = sem("ctx_loaded")
        stored = sem("stored")
        dve_step = sem("dve_step")
        pool_step = sem("pool_step")
        pool_solve = sem("pool_solve")
        act_step = sem("act_step")

        names = ("ident_ready pool_const act_const dve_const "
                 "xt_ps xc_ready proj_ready proj_free silu_ready zsum_ready tanh_ready sq_ready k_ready kb_ready "
                 "vb_ready v_kept vrev_ps vrev_kept q_ps q_c kh_ps kh_cready kb_ps kb_c gram_ps gram_kept "
                 "vt_ps vc_ready short_ps short_ready fir_ps fir_c firt_ps fir_kept solved a_ps r_ready d_ps u_ready "
                 "o_ps oc_ready ot_ps delta_ready ssq_ready sums_ready stats_ready st_ready st2v_ready "
                 "xat_ps xac_ready st_ps stc_ready h1_ps h1_ready logit_ps lmax_ready exp_ready o_ready osq_ready "
                 "ostats_ready st2_ps st2c_ready h2_ps h2_ready z_ps og_tanh on_ready ont_ps onc_ready wo_ps x1_ready "
                 "ct_ps cc_ready vh_ps vh_ready k_rot_ps kr_ready x1t_ps x1c_ready qx_ps qr_ready sc_ps sct_ready "
                 "att_ps x2_ready "
                 "x2t_ps x2c_ready route_ps rmax_ready rexp_ready score_ready scoret_ps scoret_ready binit_ps hid_ps "
                 "hid_ready y_ps sum_started y_added fin_ready").split()
        s = {n: sem(n) for n in names}

        CREDITS = {
            "pe": {"proj_ready": 1, "q_ps": 1, "kh_ps": 1, "kb_ps": 1, "gram_ps": 1,
                   "z_ps": 1, "st_ps": 1, "st2_ps": 1, "y_ps": 2},
            "act": {"kb_c": 2, "proj_free": 2, "onc_ready": 1, "hid_ready": 2},
            "dve": {"vb_ready": 1, "gram_kept": H, "x1_ready": 1, "x2_ready": 1, "ostats_ready": 1, "y_added": 2,
                    "fin_ready": 1, "sum_started": 1},
            "pool": {"v_kept": 1},
        }
        credit = {n: k for of in CREDITS.values() for n, k in of.items()}

        def give_credits(eng, who):
            for n, k in CREDITS[who].items():
                eng.sem_inc(s[n], k)

        settled = {who: sem("settled_" + who) for who in ("act", "dve")}

        def settle(eng, who):
            eng.sem_inc(settled[who], 1)

        block = stack.enter_context(nc.Block())

        EARLY_LOADS, LATE_LOADS = 4, 8
        ROWS_HERE = 11
        CW = 16
        CHUNKS = D // CW
        FIR_BANKS = (0, 3)

        @block.sync
        def _(sp):
            sp.sem_inc(stored, 16)

            def every_partition(source, a, n):
                return bass.AP(tensor=source.tensor, offset=a, ap=[[0, 128], [1, n]])

            sp.dma_start(x_g[:, :, :], x[0:G].rearrange("b t c -> t b c")).then_inc(x_in, 16)
            for dst, source in ((wb[:, :], wbundle),
                                (rb[:, :], every_partition(rbundle, 0, RB_N)),
                                (wtap[:, :, :].rearrange("p t n -> p (t n)"),
                                 every_partition(rbundle, RB_N, TAPS * NQKV)),
                                (cb[:, :], cbundle)):
                sp.dma_start(dst, source).then_inc(w_in, 16)
            for dst, source in ((ws_sb[:, :], ws), (wog2_sb[:, :], wog2),
                                (tab[:, :, :], tables), (decay_sb[:, :], decay), (b2_sb[:, :], b2),
                                (w1_sb[:, :, :], w1.rearrange("e d h -> d e h")),
                                (w2_sb[:, :, 0, :], w2[:, 0:128, :].rearrange("e h d -> h e d")),
                                (w2_sb[:, :, 1, :], w2[:, 128:256, :].rearrange("e h d -> h e d"))):
                sp.dma_start(dst, source).then_inc(w_late, 16)
            with sp.Fori(1, NG) as g:
                sp.wait_ge(s["xt_ps"], g)
                sp.dma_start(x_g[:, :, :], x[bass.ds(g * G, G)].rearrange("b t c -> t b c")).then_inc(x_in, 16)
            for g in range(NG):
                sp.wait_ge(s["gram_kept"], 2 * H * (g + 1) + credit["gram_kept"])
                for n in range(NC):
                    rows = slice(CH * n, CH * n + CH)
                    sp.dma_start(blocks_dram[GP * g:GP * g + GP, n].rearrange("r j i -> j r i"),
                                 as_t[rows, GP * g:GP * g + GP, 0, rows]).then_inc(blocks_out, 16)
            sp.wait_ge(blocks_out, 16 * NG * NC)
            sp.wait_ge(s["v_kept"], NG + credit["v_kept"])
            sp.wait_ge(s["vb_ready"], NG + credit["vb_ready"])
            sp.dma_start(blk[:, :, :, :].rearrange("p a j i -> p (a j i)"),
                         blocks_dram.rearrange("r n j i -> (r n j i)").rearrange("(p m) -> p m", p=128)
                         ).then_inc(blocks_in, 16)
            sp.wait_ge(s["fir_ps"], CHUNKS)
            sp.dma_start(xt, x[0:G].rearrange("b t c -> t b c")).then_inc(xt_in, 16)
            sp.dma_start(xa, x[0:G].rearrange("b t c -> t b c")).then_inc(xa_in, 16)
            sp.dma_start(c_g, ctx_in[0:G].rearrange("b t c -> t b c")).then_inc(ctx_loaded, 16)
            sp.wait_ge(s["solved"], 2)
            for half in range(2):
                sp.dma_start(inverse_dram[half * NP // 2:(half + 1) * NP // 2].rearrange("r n j i -> (r n j i)"
                                                                                       ).rearrange("(p m) -> p m", p=64),
                             inv[half * 64:half * 64 + 64, :, :, :].rearrange("p a j i -> p (a j i)")
                             ).then_inc(inverse_out[half], 16)
            for half in range(2):
                sp.wait_ge(inverse_out[half], 16)
                pairs = slice(half * NP // 2, (half + 1) * NP // 2)
                for n in range(NC):
                    sp.dma_start(inv_t[CH * n:CH * n + CH, pairs, :], inverse_dram[pairs, n].rearrange("r j i -> j r i")
                                 ).then_inc(inverse_in[half], 16)

            def load_xt(g):
                sp.wait_ge(s["xat_ps"], g)
                sp.dma_start(xt, x[bass.ds(g * G, G)].rearrange("b t c -> t b c")).then_inc(xt_in, 16)

            def load_x(g):
                sp.wait_ge(s["x1_ready"], g + credit["x1_ready"])
                sp.dma_start(xa, x[bass.ds(g * G, G)].rearrange("b t c -> t b c")).then_inc(xa_in, 16)

            def load_ctx(g):
                sp.wait_ge(s["ct_ps"], g)
                sp.dma_start(c_g, ctx_in[bass.ds(g * G, G)].rearrange("b t c -> t b c")).then_inc(ctx_loaded, 16)

            def store(g):
                sp.wait_ge(s["fin_ready"], g + 1 + credit["fin_ready"])
                sp.dma_start(out[bass.ds(g * G, G)].rearrange("b t c -> t b c"), fin).then_inc(stored, 16)

            load_ctx(1)
            load_xt(1)
            load_x(1)
            with sp.Fori(2, NG) as g:
                load_xt(g)
                load_ctx(g)
                load_x(g)
                store(g - 2)
            store(NG - 2)
            store(NG - 1)
            sp.wait_ge(stored, 16 * (NG + 1))

        @block.gpsimd
        def _(pool):
            give_credits(pool, "pool")
            pool.memset(ident[:, :], 0.0).then_inc(pool_step, 1)
            pool.memset(masks[:, :, :], 1.0).then_inc(pool_step, 1)
            pool.memset(tie[:, :, :, :], 1.0).then_inc(pool_step, 1)
            pool.memset(xc_pad[:, :, :], 0.0).then_inc(pool_step, 1)
            pool.memset(vc_pad[:, :, :], 0.0).then_inc(pool_step, 1)
            pool.memset(kh_c[:, :, :, :], 0.0).then_inc(pool_step, 1)
            pool.memset(inv[:, :, :, :], 0.0).then_inc(pool_step, 1)
            for k, scale in enumerate((1 / D, 1 / (H * DH * DH), 1 / D, 1 / H)):
                pool.memset(stat_scale[:, :].rearrange("p (a k) -> p a k", k=4)[:, :, k], scale).then_inc(pool_step, 1)
            pool.memset(flip[:, :], 0.0).then_inc(pool_step, 1)
            pool.wait_ge(pool_step, 12)
            pool.affine_select(out=flip[:, :], in_=flip[:, :], compare_op=ALU.not_equal, fill=1.0, base=1 - L,
                               pattern=[[1, 128]], channel_multiplier=1).then_inc(pool_step, 1)
            pool.affine_select(out=ident[:, :], in_=ident[:, :], compare_op=ALU.not_equal, fill=1.0, base=0,
                               pattern=[[-1, 128]], channel_multiplier=1).then_inc(s["ident_ready"], 1)
            pool.affine_select(out=masks[:, 0, :], in_=masks[:, 0, :], compare_op=ALU.is_gt, fill=0.0, base=0,
                               pattern=[[1, L]], channel_multiplier=-1).then_inc(s["pool_const"], 1)
            pool.affine_select(out=masks[:, 1, :], in_=masks[:, 1, :], compare_op=ALU.is_ge, fill=0.0, base=0,
                               pattern=[[1, L]], channel_multiplier=-1).then_inc(s["pool_const"], 1)
            pool.affine_select(out=tie[:, 0, :, :], in_=tie[:, 0, :, :], compare_op=ALU.is_gt, fill=0.0, base=0,
                               pattern=[[1, E], [-1, E]], channel_multiplier=0).then_inc(s["pool_const"], 1)
            pool.affine_select(out=tie[:, 1, :, :], in_=tie[:, 1, :, :], compare_op=ALU.is_gt, fill=0.0, base=0,
                               pattern=[[-1, E], [1, E]], channel_multiplier=0).then_inc(s["pool_const"], 1)
            pool.affine_select(out=inv[:, :, :, :], in_=inv[:, :, :, :], compare_op=ALU.not_equal, fill=1.0, base=0,
                               pattern=[[0, 2], [1, CH], [-1, CH]], channel_multiplier=0).then_inc(s["pool_const"], 1)
            with pool.Fori(0, NG) as g:
                pool.wait_ge(s["silu_ready"], (g + 1) * G)
                pool.tensor_copy(src[:, bass.ds(g * G, G), 3, :], qkv_g[:, :, 2 * D:3 * D]).then_inc(s["v_kept"], 1)
            pool.wait_ge(blocks_in, 16)
            pool.wait_ge(s["pool_const"], 5)
            steps = 0
            for j in range(ROWS_HERE, CH - 1):
                n, m = CH - 1 - j, j + 1 - ROWS_HERE
                p = prod_pool[:, 0:2 * m * n].rearrange("p (a c i) -> p a c i", a=2, c=m)
                column = inv[:, :, ROWS_HERE:j + 1, j]
                rest = inv[:, :, ROWS_HERE:j + 1, j + 1:]
                if steps:
                    pool.wait_ge(pool_solve, steps)
                pool.tensor_tensor(out=p, in0=blk[:, :, j, j + 1:].unsqueeze(2).broadcast_to([128, 2, m, n]),
                                   in1=column.unsqueeze(3).broadcast_to([128, 2, m, n]),
                                   op=ALU.mult).then_inc(pool_solve, 1)
                pool.wait_ge(pool_solve, steps + 1)
                pool.tensor_tensor(out=rest, in0=rest, in1=p, op=ALU.subtract).then_inc(pool_solve, 1)
                steps += 2
            pool.wait_ge(pool_solve, steps)
            pool.sem_inc(s["solved"], 1)
            pool.wait_ge(s["o_ps"], NG)
            pool.memset(st, 0.0).then_inc(pool_step, 1)
            pool.memset(st2, 0.0).then_inc(pool_step, 1)
            pool.wait_ge(pool_step, 15)

            def stats_of(g):
                pool.wait_ge(s["st_ps"], g + credit["st_ps"])
                pool.tensor_copy(st[:, :, 0:16], st_all[:, bass.ds(g * G, G), :]).then_inc(s["st_ready"], 1)
                pool.wait_ge(s["st2_ps"], g + credit["st2_ps"])
                pool.tensor_copy(st2[:, :, 4:8], st_all[:, bass.ds(g * G, G), 12:16]).then_inc(s["st2v_ready"], 1)

            pool.wait_ge(s["stats_ready"], 4)
            stats_of(0)
            pool.wait_ge(s["stats_ready"], 5)
            with pool.Fori(1, NG) as g:
                stats_of(g)

        @block.tensor
        def _(pe):
            give_credits(pe, "pe")

            def transposes(dst, source, rows=128):
                for b in range(G):
                    last = pe.transpose(ps[dst][0:rows, b * L:(b + 1) * L], source[:, b, :], ident[:, :])
                return last

            pe.wait_ge(s["ident_ready"], 1)
            pe.wait_ge(pool_step, 13)
            def x_transposed(g):
                pe.wait_ge(x_in, 16 * (g + 1))
                pe.wait_ge(s["kb_c"], g - 1 + credit["kb_c"])
                transposes(0, x_g).then_inc(s["xt_ps"], 1)

            def project(g, b):
                pe.wait_ge(s["xc_ready"], g + 1)
                pe.wait_ge(s["proj_free"], g * G + b - 1 + credit["proj_free"])
                pr = ps[1 + b % 2]
                for k in range(TAPS):
                    first = PAD - TAPS + 1 + k
                    pe.matmul(pr[:, 0:NQKV], xc_pad[:, b, first:first + L], wtap[:, k, :],
                              start=(k == 0), stop=(k == TAPS - 1))
                pe.matmul(pr[:, NQKV:NQKV + 2 * H], xc_pad[:, b, PAD:PAD + L], w_of("gates"),
                          start=True, stop=True).then_inc(s["proj_ready"], 1)

            def q_transposed(g, x_before):
                pe.wait_ge(s["silu_ready"], (g + 1) * G)
                if x_before:
                    pe.wait_ge(s["xc_ready"], g + 2)
                transposes(0, qkv_g[:, :, 0:D]).then_inc(s["q_ps"], 1)

            def v_reversed(g):
                pe.matmul(bank(3), flip[:, :], qkv_g[:, :, 2 * D:3 * D], start=True, stop=True
                          ).then_inc(s["vrev_ps"], 1)

            def keys_transposed(g):
                pe.wait_ge(s["k_ready"], g + 1)
                pe.wait_ge(s["vrev_kept"], g + 1)
                transposes(3, kh_g).then_inc(s["kh_ps"], 1)
                pe.wait_ge(s["kb_ready"], g + 1)
                pe.wait_ge(s["q_c"], g + 1)
                transposes(0, kb_g).then_inc(s["kb_ps"], 1)

            def products(g, r):
                pe.wait_ge(s["kb_c"], g + 1 + credit["kb_c"])
                pe.wait_ge(s["kh_cready"], g + 1)
                for h in range(H):
                    pe.wait_ge(s["gram_kept"], g * 2 * H + r * H + h + 1 - H + credit["gram_kept"])
                    for b in (2 * r, 2 * r + 1):
                        last = pe.matmul(ps[4 + h][:, (b % 2) * 2 * L:(b % 2 + 1) * 2 * L], kh_c[:, h, b, :],
                                         kq_c[:, b, :, :].rearrange("p k t -> p (k t)"), start=True, stop=True)
                    last.then_inc(s["gram_ps"], 1)

            def project_step(g, more):
                project(g, 0)
                keys_transposed(g - 1)
                project(g, 1)
                project(g, 2)
                products(g - 1, 0)
                project(g, 3)
                products(g - 1, 1)
                if more:
                    x_transposed(g + 1)
                q_transposed(g, more)
                v_reversed(g)

            x_transposed(0)
            pe.wait_ge(s["dve_const"], 1)
            pe.wait_ge(w_in, 16 * EARLY_LOADS)
            for b in range(G):
                project(0, b)
            x_transposed(1)
            q_transposed(0, True)
            v_reversed(0)
            with pe.Fori(1, NG - 1) as g:
                project_step(g, True)
            project_step(NG - 1, False)
            keys_transposed(NG - 1)
            for r in range(2):
                products(NG - 1, r)
            pe.wait_ge(s["v_kept"], NG + credit["v_kept"])
            pe.wait_ge(s["kb_c"], NG + credit["kb_c"])
            pe.wait_ge(s["proj_free"], B + credit["proj_free"])
            pe.wait_ge(s["kh_cready"], NG)
            pe.wait_ge(s["dve_const"], 2)
            for k in range(CHUNKS + 1):
                if k < CHUNKS:
                    pe.wait_ge(toep_in[k % 2], 16 * (k // 2 + 1))
                    if k >= 2:
                        pe.wait_ge(s["fir_c"], k - 1)
                    for c in range(CW):
                        last = pe.matmul(ps[FIR_BANKS[k % 2]][c % 4 * 32:c % 4 * 32 + B, c // 4 * L:(c // 4 + 1) * L],
                                         src[:, :, 2, k * CW + c],
                                         toep[:, k % 2, c, :], start=True, stop=True)
                    last.then_inc(s["fir_ps"], 1)
                if k:
                    pe.wait_ge(s["fir_c"], k)
                    if k >= 3:
                        pe.wait_ge(s["fir_kept"], k - 2)
                    transposes(1 + (k - 1) % 2, fir_c[:, (k - 1) % 2, :, :]).then_inc(s["firt_ps"], 1)
                g = k - 1
                if g == 0:
                    pe.wait_ge(s["gram_kept"], 2 * H * NG + credit["gram_kept"])
                if 0 <= g < NG:
                    if g >= 2:
                        pe.wait_ge(s["vc_ready"], g - 1)
                    transposes(4 + g % 2, src[:, g * G:g * G + G, 3, :]).then_inc(s["vt_ps"], 1)
                if 1 <= g <= NG:
                    pe.wait_ge(s["vc_ready"], g)
                    if g >= 3:
                        pe.wait_ge(s["short_ready"], g - 2)
                    for b in range(G):
                        for i in range(SHORT):
                            last = pe.matmul(bank(6 + (g - 1) % 2)[:, b, :], v_columns[(g - 1) % 2][:, b, i:i + L],
                                             diag_short[:, i, :], start=(i == 0), stop=(i == SHORT - 1))
                    last.then_inc(s["short_ps"], 1)
            def xat(g):
                pe.wait_ge(xt_in, 16 * (g + 1))
                pe.wait_ge(s["onc_ready"], g + credit["onc_ready"])
                transposes(0, xt).then_inc(s["xat_ps"], 1)

            def st_transposed(g):
                pe.wait_ge(s["st_ready"], g + 1)
                pe.wait_ge(s["x1_ready"], g + credit["x1_ready"])
                for b in range(G):
                    last = pe.transpose(ps[1][0:32, b * L:(b + 1) * L], st[:, b, :], ident[:, :])
                last.then_inc(s["st_ps"], 1)

            def source_gate(g):
                pe.wait_ge(s["xac_ready"], g + 1)
                pe.wait_ge(s["stc_ready"], g + 1)
                pe.matmul(ps[1][:, :], w_of("g1"), xa_c.rearrange("p b t -> p (b t)"), start=True, stop=False)
                pe.matmul(ps[1][:, :], ws_sb[:, 0:D], st_c, start=False, stop=True).then_inc(s["h1_ps"], 1)

            def source_logits(g):
                pe.wait_ge(s["h1_ready"], g + 1)
                for b in range(G):
                    last = pe.matmul(ps[0][:, b * 4:b * 4 + 4], h1[:, b * L:(b + 1) * L], w_of("g2"),
                                     start=True, stop=True)
                last.then_inc(s["logit_ps"], 1)
                pe.matmul(ps[1][0:64, :], w_of("og1"), xa_c.rearrange("p b t -> p (b t)"), start=True, stop=False)

            def st2_transposed(g):
                pe.wait_ge(s["ostats_ready"], g + 1 + credit["ostats_ready"])
                pe.wait_ge(s["st2v_ready"], g + 1)
                pe.wait_ge(s["sum_started"], g + credit["sum_started"])
                transposes(0, st2, 32).then_inc(s["st2_ps"], 1)

            def output_gate(g):
                pe.wait_ge(s["st2c_ready"], g + 1)
                pe.matmul(ps[1][0:64, :], ws_sb[:, D:D + 64], st2_c, start=False, stop=True).then_inc(s["h2_ps"], 1)

            def output_z(g):
                pe.wait_ge(s["h2_ready"], g + 1)
                for b in range(G):
                    last = pe.matmul(ps[0][:, b:b + 1], h2[:, b * L:(b + 1) * L], wog2_sb[:, :], start=True, stop=True)
                last.then_inc(s["z_ps"], 1)

            def ont(g):
                pe.wait_ge(s["on_ready"], g + 1)
                transposes(0, on_g).then_inc(s["ont_ps"], 1)

            def wo(g):
                pe.wait_ge(s["onc_ready"], g + 1 + credit["onc_ready"])
                for b in range(G):
                    last = pe.matmul(bank(1)[:, b, :], on_c[:, b, :], wo_n[:, :], start=True, stop=True)
                last.then_inc(s["wo_ps"], 1)

            def ct(g):
                pe.wait_ge(ctx_loaded, 16 * (g + 1))
                pe.wait_ge(s["x2_ready"], g + credit["x2_ready"])
                transposes(2, c_g).then_inc(s["ct_ps"], 1)

            def values(g):
                pe.wait_ge(s["cc_ready"], g + 1)
                for b in range(G):
                    last = pe.matmul(bank(2)[:, b, :], c_c[:, b, :], w_of("xv"), start=True, stop=True)
                last.then_inc(s["vh_ps"], 1)

            def keys(g):
                pe.wait_ge(s["vh_ready"], g + 1)
                pe.matmul(ps[2][:, :], w_of("xk"), c_c.rearrange("p b t -> p (b t)"), start=True, stop=True)
                pe.matmul(ps[3][:, :], w_of("xkr"), c_c.rearrange("p b t -> p (b t)"),
                          start=True, stop=True).then_inc(s["k_rot_ps"], 1)

            def x1t(g):
                pe.wait_ge(s["x1_ready"], g + 1 + credit["x1_ready"])
                pe.wait_ge(s["kr_ready"], g + 1)
                transposes(2, x1).then_inc(s["x1t_ps"], 1)

            def queries(g):
                pe.wait_ge(s["x1c_ready"], g + 1)
                pe.matmul(ps[2][:, :], w_of("xq"), x1_c.rearrange("p b t -> p (b t)"), start=True, stop=True)
                pe.matmul(ps[3][:, :], w_of("xqr"), x1_c.rearrange("p b t -> p (b t)"),
                          start=True, stop=True).then_inc(s["qx_ps"], 1)

            def scores(g):
                pe.wait_ge(s["qr_ready"], g + 1)
                for b in range(G):
                    last = pe.matmul(bank(3)[:, b, :], kr[:, b, :], qr[:, b, :], start=True, stop=True)
                last.then_inc(s["sc_ps"], 1)

            def attend(g):
                pe.wait_ge(s["sct_ready"], g + 1)
                for b in range(G):
                    last = pe.matmul(bank(2)[:, b, :], sc_t[:, b, :], vh[:, b, :], start=True, stop=True)
                last.then_inc(s["att_ps"], 1)

            def x2t(g):
                pe.wait_ge(s["x2_ready"], g + 1 + credit["x2_ready"])
                transposes(3, x2).then_inc(s["x2t_ps"], 1)

            def route(g):
                pe.wait_ge(s["x2c_ready"], g + 1)
                for b in range(G):
                    last = pe.matmul(ps[3][:, b * E:(b + 1) * E], x2_c[:, b, :], w_of("route"), start=True, stop=True)
                last.then_inc(s["route_ps"], 1)

            def scores_transposed(g):
                pe.wait_ge(s["score_ready"], g + 1)
                for b in range(G):
                    last = pe.transpose(ps[0][0:E, b * L:(b + 1) * L], score[:, b, :], ident[:, :])
                last.then_inc(s["scoret_ps"], 1)

            def second_biases(g):
                pe.wait_ge(s["scoret_ready"], g + 1)
                for b in range(G):
                    last = pe.matmul(bank(0)[:, b, :], sct[:, b * L:(b + 1) * L], b2_sb[:, :], start=True, stop=True)
                last.then_inc(s["binit_ps"], 1)

            def hidden(g, e):
                for half in range(2):
                    pe.wait_ge(s["hid_ready"], g * 2 * E + 2 * e + half - 1 + credit["hid_ready"])
                    pe.matmul(ps[4 + half][:, :], w1_sb[:, e, half * 128:half * 128 + 128],
                              x2_c.rearrange("p b t -> p (b t)"), start=True, stop=True).then_inc(s["hid_ps"], 1)

            def result(g, e):
                pe.wait_ge(s["hid_ready"], g * 2 * E + 2 * e + 2 + credit["hid_ready"])
                pe.wait_ge(s["y_added"], g * E + e - 1 + credit["y_added"])
                for b in range(G):
                    for half in range(2):
                        last = pe.matmul(bank(6 + e % 2)[:, b, :], hid[:, e % 2, half, b * L:(b + 1) * L],
                                         w2_sb[:, e, half, :], start=(half == 0), stop=(half == 1))
                last.then_inc(s["y_ps"], 1)

            pe.wait_ge(s["fir_kept"], CHUNKS)
            pe.wait_ge(w_late, 16 * LATE_LOADS)
            ct(0)
            xat(0)
            values(0)
            keys(0)
            pe.wait_ge(s["vc_ready"], NG)
            pe.wait_ge(s["short_ready"], NG)

            def solve_block(n, g):
                at = n * NG + g
                rows = slice(CH * n, CH * n + CH)
                if at >= 2:
                    pe.wait_ge(s["u_ready"], at - 1)
                for r in range(GP):
                    last = pe.matmul(ps[6 + at % 2][rows, r * DH:(r + 1) * DH], inv_t[rows, GP * g + r, :],
                                     vb[rows, GP * g + r, :], start=True, stop=True)
                last.then_inc(s["d_ps"], 1)

            def apply_solved(n, g):
                m = (n - 1) * NG + g
                rows = slice(CH * n, CH * n + CH)
                pe.wait_ge(s["u_ready"], m + 1)
                if m >= 2:
                    pe.wait_ge(s["r_ready"], m - 1)
                for r in range(GP):
                    last = pe.matmul(ps[4 + m % 2][rows, r * DH:(r + 1) * DH],
                                     as_t[0:CH * n, GP * g + r, 0, rows], u[0:CH * n, GP * g + r, :],
                                     start=True, stop=True)
                last.then_inc(s["a_ps"], 1)

            for g in range(NG):
                if g % (NG // 2) == 0:
                    pe.wait_ge(inverse_in[g // (NG // 2)], 16 * NC)
                solve_block(0, g)
            for m in range((NC - 1) * NG + 1):
                if m < (NC - 1) * NG:
                    apply_solved(m // NG + 1, m % NG)
                if m:
                    pe.wait_ge(s["r_ready"], m)
                    solve_block((m - 1) // NG + 1, (m - 1) % NG)
            for g in range(NG + 1):
                if g < NG:
                    pe.wait_ge(s["u_ready"], (NC - 1) * NG + g + 1)
                    if g < 2:
                        pe.wait_ge(s["r_ready"], (NC - 1) * NG)
                    else:
                        pe.wait_ge(s["oc_ready"], g - 1)
                    for r in range(GP):
                        last = pe.matmul(ps[4 + g % 2][r % H * DH:r % H * DH + DH, r // H * L:(r // H + 1) * L],
                                         u[:, GP * g + r, :], as_t[:, GP * g + r, 1, :], start=True, stop=True)
                    last.then_inc(s["o_ps"], 1)
                if g:
                    pe.wait_ge(s["oc_ready"], g)
                    if g < 3:
                        pe.wait_ge(s["u_ready"], NC * NG)
                    else:
                        pe.wait_ge(s["delta_ready"], g - 2)
                    transposes(6 + (g - 1) % 2, o_c[:, g - 1, :, :]).then_inc(s["ot_ps"], 1)

            st_transposed(0)
            source_gate(0)
            source_logits(0)
            pe.wait_ge(s["delta_ready"], NG)
            st2_transposed(0)
            output_gate(0)
            output_z(0)
            ont(0)
            wo(0)
            def step(g, experts_left):
                p, q = g - 1, g - 2
                x1t(p)
                xat(g)
                st_transposed(g)
                queries(p)
                source_gate(g)
                scores(p)
                source_logits(g)
                if experts_left:
                    result(q, 6)
                attend(p)
                if experts_left:
                    hidden(q, 7)
                    result(q, 7)
                x2t(p)
                route(p)
                ct(g)
                hidden(p, 0)
                result(p, 0)
                hidden(p, 1)
                values(g)
                hidden(p, 2)
                result(p, 1)
                pe.wait_ge(s["lmax_ready"], g + 1)
                scores_transposed(p)
                hidden(p, 3)
                second_biases(p)
                keys(g)
                hidden(p, 4)
                st2_transposed(g)
                output_gate(g)
                result(p, 2)
                output_z(g)
                result(p, 3)
                hidden(p, 5)
                ont(g)
                wo(g)
                hidden(p, 6)
                result(p, 4)
                result(p, 5)

            step(1, False)
            with pe.Fori(2, NG) as g:
                step(g, True)
            p, q = NG - 1, NG - 2
            x1t(p)
            queries(p)
            result(q, 6)
            scores(p)
            attend(p)
            hidden(q, 7)
            result(q, 7)
            x2t(p)
            route(p)
            hidden(p, 0)
            hidden(p, 1)
            result(p, 0)
            hidden(p, 2)
            scores_transposed(p)
            second_biases(p)
            result(p, 1)
            hidden(p, 3)
            result(p, 2)
            hidden(p, 4)
            result(p, 3)
            hidden(p, 5)
            result(p, 4)
            hidden(p, 6)
            result(p, 5)
            hidden(p, 7)
            result(p, 6)
            result(p, 7)

        @block.scalar
        def _(act):
            give_credits(act, "act")

            def toeplitz(k):
                source = bass.AP(tensor=taps_long.tensor, offset=k * CW * (2 * L - 1),
                                 ap=[[1, 128], [2 * L - 1, CW], [1, L]])
                act.dma_start(toep[:, k % 2, :, :], source).then_inc(toep_in[k % 2], 16)

            act.wait_ge(pool_step, 13)
            def xc_columns(g):
                act.wait_ge(s["xt_ps"], g + 1)
                act.wait_ge(s["proj_ready"], G * g + credit["proj_ready"])
                act.activation(xc_pad[:, :, PAD:], bank(0), ACT.Copy).then_inc(s["xc_ready"], 1)

            def activate(g, b):
                act.wait_ge(s["vb_ready"], g + credit["vb_ready"])
                act.wait_ge(s["v_kept"], g + credit["v_kept"])
                act.wait_ge(s["q_ps"], g + credit["q_ps"])
                act.wait_ge(s["proj_ready"], g * G + b + 1 + credit["proj_ready"])
                pr = ps[1 + b % 2]
                act.activation(qkv_g[:, b, :], pr[:, 0:NQKV], ACT.Silu).then_inc(s["silu_ready"], 1)
                act.activation(graw[:, b, :], pr[:, NQKV:NQKV + 2 * H], ACT.Copy).then_inc(s["proj_free"], 1)

            def square_qk(g):
                act.wait_ge(s["silu_ready"], (g + 1) * G)
                act.wait_ge(s["k_ready"], g)
                act.activation(sq_g[:, 0:2 * G, :].rearrange("p (b k) c -> p b (k c)", b=G), qkv_g[:, :, 0:2 * D],
                               ACT.Square).then_inc(s["sq_ready"], 1)

            def gate_tanh(g):
                act.wait_ge(s["zsum_ready"], g + 1)
                act.activation(gtmp[:, :, :], graw[:, :, :], ACT.Tanh, scale=0.5).then_inc(s["tanh_ready"], 1)

            def keep_q_v(g):
                act.wait_ge(s["q_ps"], g + 1 + credit["q_ps"])
                act.wait_ge(s["gram_ps"], g * 2 * H + credit["gram_ps"])
                act.activation(kq_c[:, :, 1, :], bank(0), ACT.Copy).then_inc(s["q_c"], 1)
                act.wait_ge(s["vrev_ps"], g + 1)
                settle(act, "act")
                act.activation(src[:, bass.ds(g * G, G), 2, :], bank(3), ACT.Copy).then_inc(s["vrev_kept"], 1)

            def keep_keys(g):
                act.wait_ge(s["kh_ps"], g + 1 + credit["kh_ps"])
                for h in range(H):
                    rows = slice(DH * h, DH * h + DH)
                    last = act.activation(kh_c[rows, h, :, :], ps[3][rows, :].rearrange("p (b t) -> p b t", b=G),
                                          ACT.Copy)
                last.then_inc(s["kh_cready"], 1)
                act.wait_ge(s["kb_ps"], g + 1 + credit["kb_ps"])
                act.activation(kq_c[:, :, 0, :], bank(0), ACT.Copy).then_inc(s["kb_c"], 1)

            def project_step(g, more):
                activate(g, 0)
                keep_keys(g - 1)
                for b in range(1, G):
                    activate(g, b)
                square_qk(g)
                if more:
                    xc_columns(g + 1)
                gate_tanh(g)
                keep_q_v(g)

            xc_columns(0)
            for b in range(G):
                activate(0, b)
            toeplitz(0)
            toeplitz(1)
            act.wait_ge(s["silu_ready"], G)
            act.activation(sq_g[:, 0:2 * G, :].rearrange("p (b k) c -> p b (k c)", b=G), qkv_g[:, :, 0:2 * D],
                           ACT.Square).then_inc(s["sq_ready"], 1)
            xc_columns(1)
            gate_tanh(0)
            keep_q_v(0)
            with act.Fori(1, NG - 1) as g:
                project_step(g, True)
            project_step(NG - 1, False)
            keep_keys(NG - 1)

            def x_columns(g):
                act.wait_ge(s["xat_ps"], g + 1)
                act.wait_ge(s["z_ps"], g + credit["z_ps"])
                act.activation(xa_c, bank(0), ACT.Copy).then_inc(s["xac_ready"], 1)

            def st_columns(g):
                act.wait_ge(s["st_ps"], g + 1 + credit["st_ps"])
                act.activation(st_c, ps[1][0:32, :], ACT.Copy).then_inc(s["stc_ready"], 1)

            def source_gate(g):
                act.wait_ge(s["h1_ps"], g + 1)
                act.activation(h1, ps[1][:, :], ACT.Gelu, bias=c_of("bg1")).then_inc(s["h1_ready"], 1)

            def source_exp(g):
                act.wait_ge(s["lmax_ready"], g + 1)
                act.activation(pe4, lg, ACT.Exp).then_inc(s["exp_ready"], 1)

            def square_mixture(g):
                act.wait_ge(s["o_ready"], g + 1)
                act.activation(sq_g[:, 0:G, :], o_g, ACT.Square).then_inc(s["osq_ready"], 1)

            def st2_columns(g):
                act.wait_ge(s["st2_ps"], g + 1 + credit["st2_ps"])
                act.activation(st2_c, ps[0][0:32, :], ACT.Copy).then_inc(s["st2c_ready"], 1)

            def output_gate(g):
                act.wait_ge(s["h2_ps"], g + 1)
                act.activation(h2, ps[1][0:64, :], ACT.Gelu, bias=cb[0:64, CB["bog1"][0]:CB["bog1"][1]]
                               ).then_inc(s["h2_ready"], 1)

            def output_tanh(g):
                act.wait_ge(s["z_ps"], g + 1 + credit["z_ps"])
                act.activation(og, ps[0][:, 0:G], ACT.Tanh, scale=0.5, bias=half_bog2[:, :]).then_inc(s["og_tanh"], 1)

            def on_columns(g):
                act.wait_ge(s["ont_ps"], g + 1)
                act.activation(on_c, bank(0), ACT.Copy).then_inc(s["onc_ready"], 1)

            def ctx_columns(g):
                act.wait_ge(s["ct_ps"], g + 1)
                act.activation(c_c, bank(2), ACT.Copy).then_inc(s["cc_ready"], 1)

            def keep_values(g):
                act.wait_ge(s["vh_ps"], g + 1)
                act.activation(vh, bank(2), ACT.Copy).then_inc(s["vh_ready"], 1)

            def x1_columns(g):
                act.wait_ge(s["x1t_ps"], g + 1)
                act.activation(x1_c, bank(2), ACT.Copy).then_inc(s["x1c_ready"], 1)

            def x2_columns(g):
                act.wait_ge(s["x2t_ps"], g + 1)
                act.activation(x2_c, bank(3), ACT.Copy).then_inc(s["x2c_ready"], 1)

            def route_exp(g):
                act.wait_ge(s["rmax_ready"], g + 1)
                act.activation(score, ex, ACT.Exp).then_inc(s["rexp_ready"], 1)

            def score_columns(g):
                act.wait_ge(s["scoret_ps"], g + 1)
                act.activation(sct, ps[0][0:E, :], ACT.Copy).then_inc(s["scoret_ready"], 1)

            def hidden(g, e):
                for half in range(2):
                    act.wait_ge(s["hid_ps"], g * 2 * E + 2 * e + half + 1)
                    if half == 0:
                        act.wait_ge(s["y_ps"], g * E + e - 1 + credit["y_ps"])
                    act.activation(hid[:, e % 2, half, :], ps[4 + half][:, :], ACT.Relu,
                                   bias=c_of("b1", 2 * e + half)).then_inc(s["hid_ready"], 1)

            act.wait_ge(s["v_kept"], NG + credit["v_kept"])
            act.wait_ge(s["k_ready"], NG)
            act.activation(sq_g[:, :, :], src[:, :, 3, :], ACT.Square).then_inc(s["ssq_ready"], 1)
            for k in range(CHUNKS + 1):
                if k < CHUNKS:
                    act.wait_ge(s["fir_ps"], k + 1)
                    if k + 2 < CHUNKS:
                        toeplitz(k + 2)
                    if k >= 2:
                        act.wait_ge(s["firt_ps"], k - 1)
                    act.activation(fir_c[:, k % 2, :, :], bank(FIR_BANKS[k % 2]), ACT.Copy).then_inc(s["fir_c"], 1)
                if k:
                    act.wait_ge(s["firt_ps"], k)
                    act.activation(src[:, :, 1, (k - 1) * CW:k * CW].rearrange("p b c -> p c b"),
                                   bank(1 + (k - 1) % 2, CW)[:, :, 0:B], ACT.Copy).then_inc(s["fir_kept"], 1)
                g = k - 1
                if 0 <= g < NG:
                    act.wait_ge(s["vt_ps"], g + 1)
                    if g >= 2:
                        act.wait_ge(s["short_ps"], g - 1)
                    act.activation(v_columns[g % 2][:, :, PAD:], bank(4 + g % 2), ACT.Copy).then_inc(s["vc_ready"], 1)
                if 1 <= g <= NG:
                    act.wait_ge(s["short_ps"], g)
                    act.activation(src[:, g * G - G:g * G, 0, :], bank(6 + (g - 1) % 2), ACT.Copy
                                   ).then_inc(s["short_ready"], 1)
                if g == NG:
                    act.wait_ge(s["short_ready"], NG)
                    act.wait_ge(s["sums_ready"], 1)
                    act.activation(sq_g[:, :, :], src[:, :, 0, :], ACT.Square).then_inc(s["ssq_ready"], 1)
            ctx_columns(0)
            x_columns(0)
            keep_values(0)
            a0 = RB["temp"][0]
            act.activation(temp[:, 0:1], rb[:, a0:a0 + 1], ACT.Abs).then_inc(act_step, 1)
            act.wait_ge(act_step, 1)
            act.activation(temp[:, 1:2], temp[:, 0:1], ACT.Exp, scale=-1.0).then_inc(act_step, 1)
            act.wait_ge(act_step, 2)
            act.activation(temp[:, 2:3], temp[:, 1:2], ACT.Ln, bias=1.0).then_inc(act_step, 1)
            act.activation(static_g[:, :], r_of("static"), ACT.Tanh, scale=0.5).then_inc(act_step, 1)
            act.activation(half_bog2[:, :], r_of("bog2"), ACT.Copy, scale=0.5).then_inc(act_step, 1)
            act.wait_ge(act_step, 5)
            act.sem_inc(s["act_const"], 1)
            act.wait_ge(s["fir_kept"], CHUNKS)
            act.wait_ge(s["sums_ready"], 2)
            act.activation(sq_g[:, :, :], src[:, :, 1, :], ACT.Square).then_inc(s["ssq_ready"], 1)
            for n in range(NC):
                rows = slice(CH * n, CH * n + CH)
                for g in range(NG):
                    at = n * NG + g
                    act.wait_ge(s["d_ps"], at + 1)
                    act.activation(u[rows, GP * g:GP * g + GP, :],
                                   ps[6 + at % 2][rows, :].rearrange("p (r d) -> p r d", r=GP), ACT.Copy
                                   ).then_inc(s["u_ready"], 1)
            act.wait_ge(s["sums_ready"], 3)
            for g in range(NG + 1):
                if g < NG:
                    act.wait_ge(s["o_ps"], g + 1)
                    act.activation(o_c[:, g, :, :], bank(4 + g % 2), ACT.Copy).then_inc(s["oc_ready"], 1)
                if not g:
                    continue
                act.wait_ge(s["delta_ready"], g)
                rows = slice(g * G - G, g * G)
                act.activation(sq_g[:, rows, :], src[:, rows, 2, :], ACT.Square).then_inc(s["ssq_ready"], 1)
            st_columns(0)
            source_gate(0)
            source_exp(0)
            square_mixture(0)
            st2_columns(0)
            output_gate(0)
            output_tanh(0)
            on_columns(0)
            def step(g, experts_left):
                p, q = g - 1, g - 2
                x1_columns(p)
                x_columns(g)
                st_columns(g)
                source_gate(g)
                if experts_left:
                    hidden(q, 7)
                source_exp(g)
                x2_columns(p)
                route_exp(p)
                hidden(p, 0)
                square_mixture(g)
                ctx_columns(g)
                hidden(p, 1)
                hidden(p, 2)
                keep_values(g)
                score_columns(p)
                hidden(p, 3)
                st2_columns(g)
                output_gate(g)
                output_tanh(g)
                hidden(p, 4)
                hidden(p, 5)
                on_columns(g)
                hidden(p, 6)

            step(1, False)
            with act.Fori(2, NG) as g:
                step(g, True)
            p, q = NG - 1, NG - 2
            x1_columns(p)
            hidden(q, 7)
            x2_columns(p)
            route_exp(p)
            hidden(p, 0)
            hidden(p, 1)
            hidden(p, 2)
            score_columns(p)
            hidden(p, 3)
            hidden(p, 4)
            hidden(p, 5)
            hidden(p, 6)
            hidden(p, 7)

        @block.vector
        def _(dve):
            give_credits(dve, "dve")
            base = [0, 0]

            def own(ins):
                base[1] += 1
                ins.then_inc(dve_step, 1)
                dve.wait_ge(dve_step, base[0] + base[1])

            def rsqrt(y, a, n):
                t = nt1[:, 0:n]
                own(dve.tensor_scalar(y.bitcast(I32), a.bitcast(I32), -0.5, RSQRT_GUESS, ALU.mult, ALU.add))
                for i in range(3):
                    own(dve.tensor_tensor(out=t, in0=y, in1=y, op=ALU.mult))
                    own(dve.scalar_tensor_tensor(out=t, in0=t, scalar=-0.5, in1=a, op0=ALU.mult, op1=ALU.mult))
                    own(dve.scalar_tensor_tensor(out=y, in0=t, scalar=1.5, in1=y, op0=ALU.add, op1=ALU.mult))

            def wide(a, m):
                return a.unsqueeze(len(a.shape)).broadcast_to(list(a.shape) + [m])

            def mid(a, m):
                return a.unsqueeze(1).broadcast_to([a.shape[0], m, a.shape[1]])

            dve.wait_ge(w_in, 16 * EARLY_LOADS)
            dve.wait_ge(s["ident_ready"], 1)
            dve.tensor_tensor(out=wtap[:, :, :], in0=mid(w_of("qkv"), TAPS),
                              in1=wtap[:, :, :], op=ALU.mult).then_inc(s["dve_const"], 1)
            for t in range(SHORT):
                dve.tensor_scalar(diag_short[:, t, :], ident[:, :], c_of("short", t), None, ALU.mult)
            dve.tensor_scalar(wo_n[:, :], w_of("o"), c_of("norm"), None, ALU.mult
                              ).then_inc(s["dve_const"], 1)
            dve.wait_ge(s["pool_const"], 5)

            def gate_sums(g):
                dve.wait_ge(s["proj_free"], G * (g + 1) + credit["proj_free"])
                dve.tensor_tensor(out=gtmp[:, :, :], in0=graw[:, :, :], in1=mid(r_of("gate_bias"), G),
                                  op=ALU.add).then_inc(s["zsum_ready"], 1)

            def norms(g):
                seqs = bass.ds(g * G, G)
                dve.wait_ge(s["sq_ready"], g + 1)
                own(dve.tensor_reduce(out=ss_g[:, :, :].rearrange("p b h -> p (b h)"),
                                      in_=sq_g[:, 0:2 * G, :].rearrange("p k (h d) -> p (k h) d", h=H),
                                      axis=AX.X, op=ALU.add))
                own(dve.tensor_scalar(ss_g[:, :, :], ss_g[:, :, :], 1e-6, None, ALU.add))
                rsqrt(rn_g[:, :, :].rearrange("p b h -> p (b h)"), ss_g[:, :, :].rearrange("p b h -> p (b h)"),
                      G * 2 * H)
                dve.wait_ge(s["kh_ps"], g + credit["kh_ps"])
                dve.tensor_tensor(out=kh_g[:, :, :].rearrange("p b (h d) -> p b h d", h=H),
                                  in0=qkv_g[:, :, D:2 * D].rearrange("p b (h d) -> p b h d", h=H),
                                  in1=wide(rn_g[:, :, H:2 * H], DH), op=ALU.mult).then_inc(s["k_ready"], 1)
                dve.wait_ge(s["tanh_ready"], g + 1)
                own(dve.tensor_scalar(gates[:, seqs, :], gtmp[:, :, :], 0.5, 0.5, ALU.mult, ALU.add))
                dve.wait_ge(s["k_ready"], g + 1)
                dve.wait_ge(s["kb_ps"], g + credit["kb_ps"])
                dve.tensor_tensor(out=kb_g[:, :, :].rearrange("p b (h d) -> p b h d", h=H),
                                  in0=kh_g[:, :, :].rearrange("p b (h d) -> p b h d", h=H),
                                  in1=wide(gates[:, seqs, 0:H], DH), op=ALU.mult).then_inc(s["kb_ready"], 1)
                dve.tensor_copy(rq[:, seqs, :], rn_g[:, :, 0:H])
                dve.tensor_tensor(out=vb[:, :, :].rearrange("p (b h) d -> p b h d", h=H)[:, seqs, :, :],
                                  in0=qkv_g[:, :, 2 * D:3 * D].rearrange("p b (h d) -> p b h d", h=H),
                                  in1=wide(gates[:, seqs, 0:H], DH), op=ALU.mult).then_inc(s["vb_ready"], 1)

            def mask_products(g, r):
                rows_of = as_t[:, :, :, :].rearrange("p (b h) k t -> p b h (k t)", h=H)
                for h in range(H):
                    dve.wait_ge(s["gram_ps"], g * 2 * H + r * H + h + 1 + credit["gram_ps"])
                    dve.tensor_tensor(out=rows_of[:, bass.ds(g * G + 2 * r, 2), h, :], in0=bank(4 + h, 2),
                                      in1=mid(masks[:, :, :].rearrange("p k t -> p (k t)"), 2),
                                      op=ALU.mult).then_inc(s["gram_kept"], 1)

            gate_sums(0)
            norms(0)
            PROJ_STEPS = 13
            start = base[1]
            with dve.Fori(1, NG) as g:
                base[0], base[1] = start + (g - 1) * PROJ_STEPS, 0
                mask_products(g - 1, 0)
                gate_sums(g)
                norms(g)
                mask_products(g - 1, 1)
            assert base[1] == PROJ_STEPS, base[1]
            base[0], base[1] = 0, start + (NG - 1) * PROJ_STEPS
            for r in range(2):
                mask_products(NG - 1, r)

            def layernorm(y, dst, done):
                for b in range(G):
                    last = dve.bn_stats(out=bn6[:, b, :], in_=y[:, b, :])
                own(last)
                settle(dve, "dve")
                for b in range(G):
                    last = dve.bn_aggr(out=mv[:, b, :], in_=bn6[:, b, :])
                own(last)
                own(dve.tensor_scalar(sm1[:, 0:G], mv[:, :, 1], EPS, None, ALU.add))
                rsqrt(sm2[:, 0:G], sm1[:, 0:G], G)
                for b in range(G):
                    last = dve.tensor_scalar(dst[:, b, :], y[:, b, :], mv[:, b, 0:1], sm2[:, b:b + 1],
                                             ALU.subtract, ALU.mult)
                last.then_inc(s[done], 1)

            def head_sums(xs, squares, to, n):
                settle(dve, "dve")
                own(dve.tensor_reduce(out=sumx[:, 0:n * H], in_=xs.rearrange("p n (h d) -> p (n h) d", h=H),
                                      axis=AX.X, op=ALU.add))
                own(dve.tensor_reduce(out=sumq[:, 0:n * H], in_=squares.rearrange("p n (h d) -> p (n h) d", h=H),
                                      axis=AX.X, op=ALU.add))
                settle(dve, "dve")
                dve.tensor_reduce(out=to(2), in_=xs, axis=AX.X, op=ALU.add, apply_absolute_value=True)
                dve.tensor_reduce(out=to(0), in_=sumx[:, 0:n * H].rearrange("p (n h) -> p n h", h=H),
                                  axis=AX.X, op=ALU.add)

            def head_moments(to, n, first=0):
                mine = slice(first * H, (first + n) * H)
                own(dve.tensor_tensor(out=sm1[:, mine], in0=sumx[:, mine], in1=sumx[:, mine], op=ALU.mult))
                own(dve.scalar_tensor_tensor(out=sm1[:, mine], in0=sumq[:, mine], scalar=float(DH),
                                             in1=sm1[:, mine], op0=ALU.mult, op1=ALU.subtract))
                dve.tensor_reduce(out=to(1), in_=sm1[:, mine].rearrange("p (n h) -> p n h", h=H),
                                  axis=AX.X, op=ALU.add)
                own(dve.tensor_scalar(sm2[:, mine], sumq[:, mine], 1e-30, None, ALU.max))
                rsqrt(nt2[:, mine], sm2[:, mine], n * H)
                own(dve.tensor_tensor(out=sm2[:, mine], in0=sumq[:, mine], in1=nt2[:, mine], op=ALU.mult))
                own(dve.tensor_reduce(out=to(3), in_=sm2[:, mine].rearrange("p (n h) -> p n h", h=H),
                                      axis=AX.X, op=ALU.add))

            def by_head(a):
                return a.rearrange("p b (h d) -> p b h d", h=H)

            def source_sums(k, a, b, squares_ready):
                dve.wait_ge(s["ssq_ready"], squares_ready)
                rows = src[:, a:b, k, :]
                own(dve.tensor_reduce(out=sumx[:, a * H:b * H], in_=rows.rearrange("p n (h d) -> p n h d", h=H),
                                      axis=AX.X, op=ALU.add))
                own(dve.tensor_reduce(out=sumq[:, a * H:b * H],
                                      in_=sq_g[:, a:b, :].rearrange("p n (h d) -> p (n h) d", h=H),
                                      axis=AX.X, op=ALU.add))
                dve.tensor_reduce(out=st_all[:, a:b, 4 * k + 2], in_=rows, axis=AX.X, op=ALU.add,
                                  apply_absolute_value=True)
                dve.tensor_reduce(out=st_all[:, a:b, 4 * k],
                                  in_=sumx[:, a * H:b * H].rearrange("p (n h) -> p n h", h=H),
                                  axis=AX.X, op=ALU.add)

            def source_moments(k, a, b):
                head_moments(lambda i: st_all[:, a:b, 4 * k + i], b - a, a)
                own(dve.tensor_tensor(out=st_all[:, a:b, 4 * k:4 * k + 4], in0=st_all[:, a:b, 4 * k:4 * k + 4],
                                      in1=mid(stat_scale[:, 0:4], b - a), op=ALU.mult))
                dve.sem_inc(s["stats_ready"], 1)

            def source_logits(g):
                dve.wait_ge(s["logit_ps"], g + 1)
                own(dve.scalar_tensor_tensor(out=lg, in0=ps[0][:, 0:16].rearrange("p (b k) -> p b k", b=G),
                                             scalar=temp[:, 4:5], in1=bg2_t[:, :, :], op0=ALU.mult, op1=ALU.add))
                own(dve.tensor_reduce(out=red, in_=lg, axis=AX.X, op=ALU.max))
                dve.tensor_tensor(out=lg, in0=lg, in1=wide(red, 4), op=ALU.subtract).then_inc(s["lmax_ready"], 1)

            def source_weights(g):
                seqs = bass.ds(g * G, G)
                dve.wait_ge(s["exp_ready"], g + 1)
                own(dve.tensor_reduce(out=red, in_=pe4, axis=AX.X, op=ALU.add))
                own(dve.reciprocal(red, red))
                own(dve.tensor_tensor(out=pw, in0=pe4, in1=wide(red, 4), op=ALU.mult))
                own(dve.tensor_scalar(pw, pw, FLOOR, None, ALU.max))
                own(dve.tensor_reduce(out=red, in_=pw, axis=AX.X, op=ALU.add))
                own(dve.reciprocal(red, red))
                own(dve.tensor_tensor(out=pw, in0=pw, in1=wide(red, 4), op=ALU.mult))
                own(dve.tensor_tensor(out=w0, in0=gates[:, seqs, H:2 * H], in1=mid(static_g[:, :], G), op=ALU.mult))
                own(dve.tensor_tensor(out=w0, in0=w0, in1=wide(pw[:, :, 0], H), op=ALU.add))

            def mixture(g):
                seqs = bass.ds(g * G, G)
                own(dve.tensor_tensor(out=by_head(o_g), in0=by_head(src[:, seqs, 0, :]), in1=wide(w0, DH),
                                      op=ALU.mult))
                for k in range(1, 4):
                    for b in range(G):
                        last = dve.scalar_tensor_tensor(
                            out=o_g[:, b, :], in0=src[:, bass.ds(g * G + b, 1), k, :].rearrange("p a c -> p (a c)"),
                            scalar=pw[:, b, k:k + 1], in1=o_g[:, b, :], op0=ALU.mult, op1=ALU.add)
                    if k < 3:
                        own(last)
                    else:
                        last.then_inc(s["o_ready"], 1)

            def mixture_stats(g):
                dve.wait_ge(s["osq_ready"], g + 1)
                dve.wait_ge(s["o_ready"], g + 1)
                dve.wait_ge(s["st2_ps"], g + credit["st2_ps"])
                head_sums(o_g, sq_g[:, 0:G, :], lambda k: st2[:, :, k], G)
                head_moments(lambda k: st2[:, :, k], G)
                dve.tensor_tensor(out=st2[:, :, 0:4], in0=st2[:, :, 0:4], in1=mid(stat_scale[:, 0:4], G),
                                  op=ALU.mult).then_inc(s["ostats_ready"], 1)

            def gated(g):
                dve.wait_ge(s["og_tanh"], g + 1)
                own(dve.tensor_scalar(og, og, 0.5, 0.5, ALU.mult, ALU.add))
                own(dve.tensor_tensor(out=sm1[:, 0:G], in0=og, in1=og, op=ALU.mult))
                own(dve.tensor_tensor(out=ogr, in0=sumq[:, 0:G * H].rearrange("p (b h) -> p b h", b=G),
                                      in1=wide(sm1[:, 0:G], H), op=ALU.mult))
                own(dve.tensor_scalar(ogr, ogr, 1.0 / DH, EPS, ALU.mult, ALU.add))
                rsqrt(sm2[:, 0:G * H], ogr.rearrange("p b h -> p (b h)"), G * H)
                own(dve.tensor_tensor(out=ogr, in0=sm2[:, 0:G * H].rearrange("p (b h) -> p b h", b=G),
                                      in1=wide(og, H), op=ALU.mult))
                dve.tensor_tensor(out=by_head(on_g), in0=by_head(o_g), in1=wide(ogr, DH), op=ALU.mult
                                  ).then_inc(s["on_ready"], 1)

            def x1_norm(g):
                dve.wait_ge(s["wo_ps"], g + 1)
                dve.wait_ge(xa_in, 16 * (g + 1))
                own(dve.tensor_tensor(out=y_g, in0=bank(1), in1=xa, op=ALU.add))
                layernorm(y_g, x1, "x1_ready")

            def rotate_keys(g):
                dve.wait_ge(s["k_rot_ps"], g + 1)
                own(dve.tensor_tensor(out=kt, in0=bank(3), in1=mid(tab[:, 3, :], G), op=ALU.mult))
                own(dve.tensor_tensor(out=kr, in0=bank(2), in1=mid(tab[:, 2, :], G), op=ALU.mult))
                dve.tensor_tensor(out=kr, in0=kr, in1=kt, op=ALU.add).then_inc(s["kr_ready"], 1)

            def rotate_queries(g):
                dve.wait_ge(s["qx_ps"], g + 1)
                own(dve.tensor_tensor(out=qt, in0=bank(3), in1=mid(tab[:, 1, :], G), op=ALU.mult))
                own(dve.tensor_tensor(out=qr, in0=bank(2), in1=mid(tab[:, 0, :], G), op=ALU.mult))
                dve.tensor_tensor(out=qr, in0=qr, in1=qt, op=ALU.add).then_inc(s["qr_ready"], 1)

            def decay_scores(g):
                dve.wait_ge(s["sc_ps"], g + 1)
                dve.tensor_tensor(out=sc_t, in0=bank(3), in1=mid(decay_sb[:, :], G), op=ALU.mult
                                  ).then_inc(s["sct_ready"], 1)

            def x2_norm(g):
                dve.wait_ge(s["att_ps"], g + 1)
                dve.wait_ge(s["x1_ready"], g + 1 + credit["x1_ready"])
                own(dve.tensor_tensor(out=y_g, in0=bank(2), in1=x1, op=ALU.add))
                layernorm(y_g, x2, "x2_ready")

            def route_max(g):
                dve.wait_ge(s["route_ps"], g + 1)
                logits = ps[3][:, 0:G * E].rearrange("p (b e) -> p b e", b=G)
                own(dve.tensor_reduce(out=red, in_=logits, axis=AX.X, op=ALU.max))
                dve.tensor_tensor(out=ex, in0=logits, in1=wide(red, E), op=ALU.subtract
                                  ).then_inc(s["rmax_ready"], 1)

            def choose(g):
                dve.wait_ge(s["rexp_ready"], g + 1)
                for k, op in enumerate((ALU.is_ge, ALU.is_gt)):
                    own(dve.tensor_tensor(out=cmp_[:, :, :, k, :], in0=score.unsqueeze(2).broadcast_to([128, G, E, E]),
                                          in1=wide(score, E), op=op))
                for k in range(2):
                    own(dve.tensor_tensor(out=cmp_[:, :, :, k, :], in0=cmp_[:, :, :, k, :],
                                          in1=tie[:, k, :, :].unsqueeze(1).broadcast_to([128, G, E, E]), op=ALU.mult))
                own(dve.tensor_reduce(out=rank, in_=cmp_.rearrange("p b i k j -> p (b i) (k j)"), axis=AX.X,
                                      op=ALU.add))
                own(dve.scalar_tensor_tensor(out=ex, in0=rank, scalar=2.0, in1=score, op0=ALU.is_lt, op1=ALU.mult))
                own(dve.tensor_reduce(out=red, in_=ex, axis=AX.X, op=ALU.add))
                own(dve.reciprocal(red, red))
                dve.tensor_tensor(out=score, in0=ex, in1=wide(red, E), op=ALU.mult).then_inc(s["score_ready"], 1)

            def start_sum(g):
                dve.wait_ge(s["x2_ready"], g + 1 + credit["x2_ready"])
                dve.wait_ge(s["binit_ps"], g + 1)
                dve.wait_ge(s["fin_ready"], g + credit["fin_ready"])
                own(dve.tensor_tensor(out=acc, in0=bank(0), in1=x2, op=ALU.add))
                dve.sem_inc(s["sum_started"], 1)
                dve.wait_ge(s["score_ready"], g + 1)

            def add(g, e):
                dve.wait_ge(s["y_ps"], g * E + e + 1 + credit["y_ps"])
                for b in range(G):
                    last = dve.scalar_tensor_tensor(out=acc[:, b, :], in0=bank(6 + e % 2)[:, b, :],
                                                    scalar=score[:, b, e:e + 1], in1=acc[:, b, :],
                                                    op0=ALU.mult, op1=ALU.add)
                last.then_inc(s["y_added"], 1)
                dve.wait_ge(s["y_added"], g * E + e + 1 + credit["y_added"])

            def finish(g):
                dve.wait_ge(stored, 16 * (g + 1))
                layernorm(acc, fin, "fin_ready")

            source_sums(3, 0, B, 1)
            dve.sem_inc(s["sums_ready"], 1)
            source_moments(3, 0, B)

            dve.wait_ge(blocks_in, 16)
            for j in range(CH - 1):
                n, m = CH - 1 - j, min(j + 1, ROWS_HERE)
                p = prod[:, 0:2 * m * n].rearrange("p (a c i) -> p a c i", a=2, c=m)
                own(dve.tensor_tensor(out=p, in0=blk[:, :, j, j + 1:].unsqueeze(2).broadcast_to([128, 2, m, n]),
                                      in1=wide(inv[:, :, 0:m, j], n), op=ALU.mult))
                own(dve.tensor_tensor(out=inv[:, :, 0:m, j + 1:], in0=inv[:, :, 0:m, j + 1:], in1=p,
                                      op=ALU.subtract))
            dve.sem_inc(s["solved"], 1)
            source_sums(0, 0, B, 2)
            dve.sem_inc(s["sums_ready"], 1)
            source_moments(0, 0, B)
            rotate_keys(0)
            source_sums(1, 0, B // 2, 3)

            for n in range(1, NC):
                rows = slice(CH * n, CH * n + CH)
                for g in range(NG):
                    dve.wait_ge(s["a_ps"], (n - 1) * NG + g + 1)
                    pairs = vb[rows, GP * g:GP * g + GP, :]
                    dve.tensor_tensor(out=pairs, in0=pairs,
                                      in1=ps[4 + ((n - 1) * NG + g) % 2][rows, :].rearrange("p (r d) -> p r d", r=GP),
                                      op=ALU.subtract).then_inc(s["r_ready"], 1)
                    if g == 1 and n > 1:
                        source_sums(1, B // 2 + (n - 2) * G, B // 2 + (n - 1) * G, 3)
            dve.sem_inc(s["sums_ready"], 1)
            source_moments(1, 0, B)
            dve.wait_ge(s["act_const"], 1)
            own(dve.tensor_scalar(static_g[:, :], static_g[:, :], 0.5, 0.5, ALU.mult, ALU.add))
            a0 = RB["temp"][0]
            own(dve.scalar_tensor_tensor(out=temp[:, 3:4], in0=rb[:, a0:a0 + 1], scalar=0.0, in1=temp[:, 2:3],
                                         op0=ALU.max, op1=ALU.add))
            own(dve.reciprocal(temp[:, 4:5], temp[:, 3:4]))
            own(dve.tensor_scalar(bg2_t[:, :, :], mid(r_of("bg2"), G), temp[:, 4:5], None, ALU.mult))
            dve.wait_ge(s["fir_ps"], CHUNKS)
            for g in range(NG):
                dve.wait_ge(s["ot_ps"], g + 1)
                dve.tensor_tensor(out=src[:, g * G:g * G + G, 2, :].rearrange("p b (h d) -> p b h d", h=H),
                                  in0=ps[6 + g % 2][:, :].rearrange("p (b h d) -> p b h d", b=G, h=H),
                                  in1=wide(rq[:, g * G:g * G + G, :], DH), op=ALU.mult
                                  ).then_inc(s["delta_ready"], 1)
            source_sums(2, 0, G, 4)
            source_moments(2, 0, G)
            for g in range(1, NG):
                source_sums(2, g * G, g * G + G, 4 + g)

            dve.wait_ge(pool_step, 15)
            dve.wait_ge(w_late, 16 * LATE_LOADS)
            source_logits(0)
            source_weights(0)
            mixture(0)
            mixture_stats(0)
            source_moments(2, G, B)
            gated(0)
            x1_norm(0)
            def step(g, experts_left):
                p, q = g - 1, g - 2
                if experts_left:
                    add(q, 5)
                rotate_queries(p)
                decay_scores(p)
                source_logits(g)
                if experts_left:
                    add(q, 6)
                x2_norm(p)
                if experts_left:
                    add(q, 7)
                source_weights(g)
                route_max(p)
                mixture(g)
                choose(p)
                if experts_left:
                    finish(q)
                mixture_stats(g)
                start_sum(p)
                add(p, 0)
                add(p, 1)
                rotate_keys(g)
                add(p, 2)
                gated(g)
                add(p, 3)
                x1_norm(g)
                add(p, 4)

            step(1, False)
            MIX_STEPS = 101
            start = base[1]
            with dve.Fori(2, NG) as g:
                base[0], base[1] = start + (g - 2) * MIX_STEPS, 0
                step(g, True)
            assert base[1] == MIX_STEPS, base[1]
            base[0], base[1] = 0, start + (NG - 2) * MIX_STEPS
            p, q = NG - 1, NG - 2
            add(q, 5)
            rotate_queries(p)
            decay_scores(p)
            add(q, 6)
            x2_norm(p)
            add(q, 7)
            route_max(p)
            choose(p)
            finish(q)
            start_sum(p)
            add(p, 0)
            add(p, 1)
            add(p, 2)
            add(p, 3)
            add(p, 4)
            add(p, 5)
            add(p, 6)
            add(p, 7)
            finish(p)


def xpos_tables():
    import numpy as np

    half = D // 2
    scale_vec = (np.arange(0, D, 2, dtype=np.float32) + np.float32(0.4 * D)) / np.float32(1.4 * D)
    pos = np.arange(L, dtype=np.float32)
    scale = scale_vec[None, :] ** (pos / np.float32(512.0))[:, None]
    freqs = np.float32(1.0) / np.float32(10000.0) ** (np.arange(half, dtype=np.float32) / np.float32(half))
    angle = (pos[:, None] * freqs[None, :]).astype(np.float64)
    sign = np.tile(np.array([-1.0, 1.0]), half)
    out = []
    for sc in (scale.astype(np.float64), 1.0 / scale.astype(np.float64)):
        out += [np.repeat(np.cos(angle) * sc, 2, axis=1), np.repeat(np.sin(angle) * sc, 2, axis=1) * sign]
    return np.ascontiguousarray(np.stack(out).transpose(2, 0, 1).astype(np.float32))


def decay_table():
    import numpy as np

    diff = np.arange(L)[None, :] - np.arange(L)[:, None]
    return np.where(diff >= 0, 0.96875 ** np.maximum(diff, 0), 0.0).astype(np.float32)


def kernel(**inputs):
    import numpy as np
    import concourse.bacc as bacc
    from concourse.bass_utils import run_bass_kernel_spmd

    a = {k: np.asarray(v) for k, v in inputs.items()}
    w = {k[8:]: v for k, v in a.items() if k.startswith("L0_attn_")}

    swap = np.arange(D) ^ 1
    wbundle = np.concatenate(
        [w["Wq"], w["Wk"], w["Wv"], w["Wb"], w["Wres"], w["Wg1"][:D], w["Wog1"][:D], w["Wg2"], w["Wo"],
         a["L0_xattn_Wq"], a["L0_xattn_Wq"][:, swap], a["L0_xattn_Wk"], a["L0_xattn_Wk"][:, swap],
         a["L0_xattn_Wv"], a["L0_ffn_Wg"]], axis=1)
    taps = np.concatenate([w["wq_conv"], w["wk_conv"], w["wv_conv"]], axis=0).T
    rbundle = np.concatenate([np.zeros(H, np.float32), w["bres"], w["bg2"], w["logit_temp"],
                              w["conv_res_logit"], w["bog2"], taps.reshape(-1)])
    col = [w["bg1"][:, None], np.concatenate([w["bog1"], np.zeros(D - D // 2, np.float32)])[:, None],
           np.tile(w["norm_w"], H)[:, None], w["fir_short"].reshape(D, SHORT),
           a["L0_ffn_b1"].reshape(2 * E, 128).T]
    cbundle = np.concatenate(col, axis=1)
    ws = np.zeros((32, D + D // 2), np.float32)
    ws[:16, :D] = w["Wg1"][D:]
    ws[:8, D:] = w["Wog1"][D:]
    taps_long = np.zeros((D, 2 * L - 1), np.float32)
    taps_long[:, L - 1:L - 1 + LONG] = w["fir_long"].reshape(D, LONG)[:, ::-1]
    arrays = {
        "x": a["x"], "ctx_in": a["ctx_1024"], "wbundle": wbundle, "rbundle": rbundle, "cbundle": cbundle, "ws": ws,
        "wog2": w["Wog2"], "taps_long": taps_long, "w1": a["L0_ffn_W1"], "w2": a["L0_ffn_W2"], "b2": a["L0_ffn_b2"],
        "tables": xpos_tables(), "decay": decay_table(),
    }
    arrays = {k: np.ascontiguousarray(v) for k, v in arrays.items()}
    nc = bacc.Bacc("TRN2", target_bir_lowering=False, num_devices=1)
    args = [nc.dram_tensor(k, v.shape, mybir.dt.from_np(v.dtype), kind="ExternalInput").ap()
            for k, v in arrays.items()]
    args += [nc.dram_tensor(k, (NP, NC, CH, CH), F32, kind="Internal").ap() for k in ("blocks", "inverses")]
    out = nc.dram_tensor("result", (B, L, D), F32, kind="ExternalOutput").ap()
    decoder_kernel(nc, *args, out)
    r = run_bass_kernel_spmd(nc, [arrays], core_ids=[0])
    return r.results[0]["result"]
```
